# Optimizing a Trainium2 kernel written in Bass

```python
import numpy as np
import jax
import jax.numpy as jnp

def _softmax(x, axis=-1):
    return jax.nn.softmax(x, axis=axis)

def _gelu(x):
    return jax.nn.gelu(x, approximate=True)

def _silu(x):
    return jax.nn.silu(x)

def _sigmoid(x):
    return jax.nn.sigmoid(x)

def _layernorm(x, axis=-1, eps=1e-05):
    m = jnp.mean(x, axis=axis, keepdims=True)
    v = jnp.var(x, axis=axis, keepdims=True)
    return (x - m) / jnp.sqrt(v + eps)

def _scatter_add(tgt, idx, src, axis=0):
    return tgt.at[idx].add(src)

def _segment_sum(src, seg, n):
    return jax.ops.segment_sum(src, seg, n)
kernel_name = 'mk_conv_attn_hybrid_d2_conv_nchw512_r4_e19f9f'

def setup_inputs(seed: int=0):
    np.random.seed(seed)
    _w = jnp.asarray

    def _rec_inputs():
        import jax
        import jax.numpy as jnp
        _gk = jax.random.key(seed)
        x = 7.22e-05 + 1 * jax.random.normal(jax.random.fold_in(_gk, 1), (16, 128, 16, 16), jnp.float32)
        return x
    x = _rec_inputs()

    def _L0_conv_setup():
        import jax, jax.numpy as jnp
        import numpy as np
        DN = ('NCHW', 'OIHW', 'NCHW')

        def conv3x3(x, w):
            return jax.lax.conv_general_dilated(x, w, (1, 1), [(1, 1), (1, 1)], dimension_numbers=DN)
        key = jax.random.key(seed)
        ks = jax.random.split(key, 5)
        N, C, H, W = (16, 128, 16, 16)
        fan = C * 3 * 3
        s = 1.0 / np.sqrt(fan)
        x = jax.random.normal(ks[0], (N, C, H, W), dtype=jnp.float32)
        Wq = jax.random.normal(ks[1], (C, C, 3, 3), dtype=jnp.float32) * s
        Wk = jax.random.normal(ks[2], (C, C, 3, 3), dtype=jnp.float32) * s
        Wv = jax.random.normal(ks[3], (C, C, 3, 3), dtype=jnp.float32) * s
        Wc = jax.random.normal(ks[4], (C, C, 3, 3), dtype=jnp.float32) * s
        gamma = jnp.ones((C,), dtype=jnp.float32)
        beta = jnp.zeros((C,), dtype=jnp.float32)
        return {'x': x, 'Wq': Wq, 'Wk': Wk, 'Wv': Wv, 'Wc': Wc, 'gamma': gamma, 'beta': beta}
    _L0_conv_all = _L0_conv_setup()
    _L0_conv_in = {k: v for k, v in _L0_conv_all.items() if k in ('Wq', 'Wk', 'Wv', 'Wc', 'gamma', 'beta')}
    del _L0_conv_all

    def _L1_attn_setup():
        import jax, jax.numpy as jnp
        import numpy as np
        S, R, DH = (8, 2, 16)
        key = jax.random.key(seed)
        ks = jax.random.split(key, 7)
        b, n, dim = (2, 512, 128)

        def w(k, i, o):
            return jax.random.normal(k, (i, o), dtype=jnp.float32) / np.sqrt(i)
        return {'x': jax.random.normal(ks[0], (b, n, dim), dtype=jnp.float32), 'wq_s': w(ks[1], dim, S * DH), 'wk_s': w(ks[2], dim, S * DH), 'wv_r': w(ks[3], dim, R * DH), 'wq_r': w(ks[4], dim, S * DH), 'wk_ret': w(ks[5], DH, DH), 'w_out': w(ks[6], S * DH, dim)}
    _L1_attn_all = _L1_attn_setup()
    _L1_attn_in = {k: v for k, v in _L1_attn_all.items() if k in ('wq_s', 'wk_s', 'wv_r', 'wq_r', 'wk_ret', 'w_out')}
    del _L1_attn_all

    def _L1_ffn_setup():
        import jax, jax.numpy as jnp
        import numpy as np
        D_MODEL = 128
        D_FF = 512
        NUM_EXPERTS = 8
        TOP_K = 2
        key = jax.random.key(seed)
        k_x, k_g, k_w1, k_w2 = jax.random.split(key, 4)
        x = jax.random.normal(k_x, (8, 1024, D_MODEL), dtype=jnp.float32)
        Wg = jax.random.normal(k_g, (D_MODEL, NUM_EXPERTS), dtype=jnp.float32) * (1.0 / np.sqrt(D_MODEL))
        W1 = jax.random.normal(k_w1, (NUM_EXPERTS, D_MODEL, D_FF), dtype=jnp.float32) * (1.0 / np.sqrt(D_MODEL))
        W2 = jax.random.normal(k_w2, (NUM_EXPERTS, D_FF, D_MODEL), dtype=jnp.float32) * (1.0 / np.sqrt(D_FF))
        return {'x': x, 'Wg': Wg, 'W1': W1, 'W2': W2}
    _L1_ffn_all = _L1_ffn_setup()
    _L1_ffn_in = {k: v for k, v in _L1_ffn_all.items() if k in ('Wg', 'W1', 'W2')}
    del _L1_ffn_all
    return {'x': x, 'L0_conv_Wq': _L0_conv_in['Wq'], 'L0_conv_Wk': _L0_conv_in['Wk'], 'L0_conv_Wv': _L0_conv_in['Wv'], 'L0_conv_Wc': _L0_conv_in['Wc'], 'L0_conv_gamma': _L0_conv_in['gamma'], 'L0_conv_beta': _L0_conv_in['beta'], 'L1_attn_wq_s': _L1_attn_in['wq_s'], 'L1_attn_wk_s': _L1_attn_in['wk_s'], 'L1_attn_wv_r': _L1_attn_in['wv_r'], 'L1_attn_wq_r': _L1_attn_in['wq_r'], 'L1_attn_wk_ret': _L1_attn_in['wk_ret'], 'L1_attn_w_out': _L1_attn_in['w_out'], 'L1_ffn_Wg': _L1_ffn_in['Wg'], 'L1_ffn_W1': _L1_ffn_in['W1'], 'L1_ffn_W2': _L1_ffn_in['W2']}

def reference(x, L0_conv_Wq, L0_conv_Wk, L0_conv_Wv, L0_conv_Wc, L0_conv_gamma, L0_conv_beta, L1_attn_wq_s, L1_attn_wk_s, L1_attn_wv_r, L1_attn_wq_r, L1_attn_wk_ret, L1_attn_w_out, L1_ffn_Wg, L1_ffn_W1, L1_ffn_W2):
    import jax
    import jax.numpy as jnp

    def _L0_conv_ref(x, Wq, Wk, Wv, Wc, gamma, beta):
        import jax, jax.numpy as jnp
        import numpy as np
        DN = ('NCHW', 'OIHW', 'NCHW')

        def conv3x3(x, w):
            return jax.lax.conv_general_dilated(x, w, (1, 1), [(1, 1), (1, 1)], dimension_numbers=DN)
        C = x.shape[1]
        q = conv3x3(x, Wq)
        k = conv3x3(x, Wk)
        v = conv3x3(x, Wv)
        att = jnp.einsum('nchw,mchw->nmhw', q, k) / jnp.sqrt(jnp.float32(C))
        att = jax.nn.softmax(att, axis=1)
        virt = jnp.einsum('nmhw,mchw->nchw', att, v)
        mu = jnp.mean(virt, axis=(1, 2, 3), keepdims=True)
        var = jnp.var(virt, axis=(1, 2, 3), keepdims=True)
        virt = (virt - mu) * jax.lax.rsqrt(var + 1e-05)
        virt = virt * gamma[None, :, None, None] + beta[None, :, None, None]
        virt = jax.nn.relu(virt)
        virt = conv3x3(virt, Wc)
        return x + virt

    def _L1_attn_ref(x, wq_s, wk_s, wv_r, wq_r, wk_ret, w_out):
        import jax, jax.numpy as jnp
        import numpy as np
        S, R, DH = (8, 2, 16)
        b, n, dim = x.shape
        scale = DH ** (-0.5)
        sq = (x @ wq_s).reshape(b, n, S, DH).transpose(0, 2, 1, 3) * scale
        sk = (x @ wk_s).reshape(b, n, S, DH).transpose(0, 2, 1, 3)
        rv = (x @ wv_r).reshape(b, n, R, DH).transpose(0, 2, 1, 3)
        search_sim = jnp.einsum('bsid,bsjd->bsij', sq, sk)
        search_attn = jax.nn.softmax(search_sim, axis=-1)
        retrieved = jnp.einsum('bsij,brjd->bsird', search_attn, rv)
        rq = (x @ wq_r).reshape(b, n, S, DH).transpose(0, 2, 1, 3) * scale
        rk = retrieved @ wk_ret
        retrieval_sim = jnp.einsum('bsid,bsird->bsir', rq, rk)
        retrieval_attn = jax.nn.softmax(retrieval_sim, axis=-1)
        out = jnp.einsum('bsir,bsird->bsid', retrieval_attn, retrieved)
        out = out.transpose(0, 2, 1, 3).reshape(b, n, S * DH)
        return out @ w_out

    def _L1_ffn_ref(x, Wg, W1, W2):
        import jax, jax.numpy as jnp
        import numpy as np
        D_MODEL = 128
        D_FF = 512
        NUM_EXPERTS = 8
        TOP_K = 2
        B, S, D = x.shape
        E = Wg.shape[-1]
        router_logits = jnp.einsum('bsd,de->bse', x, Wg)
        top_logits, top_idx = jax.lax.top_k(router_logits, TOP_K)
        top_w = jax.nn.softmax(top_logits, axis=-1)
        combine = jnp.sum(jax.nn.one_hot(top_idx, E, dtype=x.dtype) * top_w[..., None], axis=-2)
        xt = x.reshape(B * S, D)
        cw = combine.reshape(B * S, E)
        out = jnp.zeros_like(xt)
        for e in range(E):
            h = jax.nn.silu(xt @ W1[e]) @ W2[e]
            out = out + cw[:, e:e + 1] * h
        return out.reshape(B, S, D)

    def _gn(v, G=32, eps=1e-05):
        B_, C_, H_, W_ = v.shape
        g = v.reshape(B_, G, C_ // G, H_, W_)
        m = jnp.mean(g, axis=(2, 3, 4), keepdims=True)
        s = jnp.var(g, axis=(2, 3, 4), keepdims=True)
        return ((g - m) / jnp.sqrt(s + eps)).reshape(v.shape)

    def _ln_c(v, eps=1e-06):
        m = jnp.mean(v, axis=1, keepdims=True)
        s = jnp.var(v, axis=1, keepdims=True)
        return (v - m) / jnp.sqrt(s + eps)

    def _ln_t(v, eps=1e-05):
        m = jnp.mean(v, axis=-1, keepdims=True)
        s = jnp.var(v, axis=-1, keepdims=True)
        return (v - m) / jnp.sqrt(s + eps)

    def _to_tokens(v):
        B_, C_, H_, W_ = v.shape
        return v.reshape(B_, C_, H_ * W_).transpose(0, 2, 1)

    def _from_tokens(t, like):
        B_, C_, H_, W_ = like.shape
        return t.transpose(0, 2, 1).reshape(B_, C_, H_, W_)
    x = _L0_conv_ref(x, L0_conv_Wq, L0_conv_Wk, L0_conv_Wv, L0_conv_Wc, L0_conv_gamma, L0_conv_beta)
    t = _to_tokens(x)
    t = t + _L1_attn_ref(_ln_t(t), L1_attn_wq_s, L1_attn_wk_s, L1_attn_wv_r, L1_attn_wq_r, L1_attn_wk_ret, L1_attn_w_out)
    t = t + _L1_ffn_ref(_ln_t(t), L1_ffn_Wg, L1_ffn_W1, L1_ffn_W2)
    x = _from_tokens(t, x)
    return x

_drawn_inputs = setup_inputs


def setup_inputs(seed=0):
    import zlib

    import numpy as np

    out = dict(_drawn_inputs(seed))
    spreads = {'L0_conv_gamma': (1.0, 0.2), 'L0_conv_beta': (0.0, 0.1)}
    factors = {}
    for name, (base, spread) in spreads.items():
        noise = np.random.default_rng([zlib.crc32(name.encode()), seed]).standard_normal(out[name].shape)
        drawn = base * np.exp(spread * noise) if base else spread * noise
        out[name] = jnp.asarray(drawn.astype(out[name].dtype))
    for name, factor in factors.items():
        out[name] = (out[name] * factor).astype(out[name].dtype)
    return out
```

```python
from contextlib import ExitStack

import concourse.bass as bass
from concourse import mybir

F32 = mybir.dt.float32
F32R = mybir.dt.float32r
I32 = mybir.dt.int32
U32 = mybir.dt.uint32
ALU = mybir.AluOpType
ACT = mybir.ActivationFunctionType
AX = mybir.AxisListType

P = 128
NI, HW = 16, 16
PIX = HW * HW
TOK = NI * PIX
PAD = HW + 2
CH = 512
NCH = TOK // CH
G = CH // P
TAPS = [(dy, dx) for dy in range(3) for dx in range(3)]
NEG = -1.0e30
EPS = 1e-5


def f32(ap):
    return ap.bitcast(F32)


def need(eng, semaphore, count):
    if not isinstance(count, int) or count > 0:
        eng.wait_ge(semaphore, count)


def split_product(pe, out, w_h, w_l, x_h, x_l, start, stop):
    pe.matmul(out, w_h, x_h, start=start, stop=False)
    pe.matmul(out, w_h, x_l, start=False, stop=False)
    return pe.matmul(out, w_l, x_h, start=False, stop=stop)


def conv_attention(nc, sb, sem, bank, pad_h, pad_l, resid, virt, ident, wc_h, wc_l, x_chwn, x_cnhw,
                   w_qkv, w_c):
    scale = float(P) ** -0.5
    with ExitStack() as ctx:
        x_raw = sb("x_raw", [P, HW, HW * NI], where=ctx)
        w_raw = sb("w_raw", [P, 4, 9, P], where=ctx)
        w_h = sb("w_h", [P, 3, 9, P], F32R, ctx)
        w_l = sb("w_l", [P, 3, 9, P], F32R, ctx)
        qkv = sb("qkv", [P, 3, CH], where=ctx)
        mask = sb("mask", [P, P], where=ctx)
        scores = sb("scores", [P, G, P], where=ctx)
        expd = sb("expd", [P, G, P], where=ctx)
        probs = sb("probs", [P, G, P], where=ctx)
        probs_t = sb("probs_t", [P, G, P], where=ctx)
        v_tok = sb("v_tok", [P, G, P], where=ctx)
        row_max = sb("row_max", [P, G], where=ctx)
        row_sum = sb("row_sum", [P, G], where=ctx)
        row_inv = sb("row_inv", [P, G], where=ctx)

        x_loaded = [sem(f"x_loaded{i}") for i in range(4)]
        w_loaded = [sem(f"w_loaded{i}") for i in range(4)]
        late_loaded = sem("late_loaded")
        border_zeroed = sem("border_zeroed")
        ident_zeroed = sem("ident_zeroed")
        ident_ready = sem("ident_ready")
        mask_steps = sem("mask_steps")
        x_high = sem("x_high")
        x_ready = sem("x_ready")
        w_high = sem("w_high")
        w_ready = sem("w_ready")
        conv_done = [sem(f"conv_{n}_done") for n in "qkv"]
        conv_copied = [sem(f"conv_{n}_copied") for n in "qkv"]
        a_scores = sem("a_scores")
        v_turned = sem("v_turned")
        v_tok_ready = sem("v_tok_ready")
        masked = sem("masked")
        maxed = sem("maxed")
        shifted = sem("shifted")
        a_exp = sem("a_exp")
        summed = sem("summed")
        inverted = sem("inverted")
        probs_ready = sem("probs_ready")
        probs_turned = sem("probs_turned")
        probs_t_ready = sem("probs_t_ready")
        a_out = sem("a_out")
        virt_ready = sem("virt_ready")

        ps_conv, ps_s, ps_vt, ps_pt, ps_o = bank[0:3], bank[3], bank[4], bank[5], bank[6]
        grid_h = pad_h[:, :].rearrange("p (h c) -> p h c", h=PAD)
        grid_l = pad_l[:, :].rearrange("p (h c) -> p h c", h=PAD)
        block = ctx.enter_context(nc.Block())

        @block.sync
        def _(sp):
            sp.dma_start(w_raw[:, 0], w_qkv[:, 0]).then_inc(w_loaded[0], 16)
            for i in range(4):
                sp.dma_start(x_raw[:, 4 * i:4 * i + 4], x_chwn[:, 4 * i:4 * i + 4]).then_inc(x_loaded[i], 16)
                if i == 0:
                    sp.dma_start(w_raw[:, 1], w_qkv[:, 1]).then_inc(w_loaded[1], 16)
                if i == 1:
                    sp.dma_start(w_raw[:, 2], w_qkv[:, 2]).then_inc(w_loaded[2], 16)
            sp.dma_start(w_raw[:, 3], w_c).then_inc(w_loaded[3], 16)
            sp.dma_start(resid[:, :], x_cnhw).then_inc(late_loaded, 16)
            sp.wait_ge(late_loaded, 16)

        @block.gpsimd
        def _(pool):
            for grid in (grid_h, grid_l):
                pool.memset(f32(grid[:, 0:PAD:PAD - 1, :]), 0.0).then_inc(border_zeroed, 1)
                columns = grid[:, 1:PAD - 1, :].rearrange("p h (c n) -> p h c n", n=NI)
                pool.memset(f32(columns[:, :, 0:PAD:PAD - 1, :]), 0.0).then_inc(border_zeroed, 1)
            pool.memset(ident[:, :], 0.0).then_inc(ident_zeroed, 1)
            pool.memset(mask[:, :], 0.0).then_inc(mask_steps, 1)
            pool.wait_ge(ident_zeroed, 1)
            pool.affine_select(out=ident[:, :], in_=ident[:, :], compare_op=ALU.not_equal, fill=1.0, base=0,
                               pattern=[[-1, P]], channel_multiplier=1).then_inc(ident_ready, 1)
            blocks = mask[:, :].rearrange("p (b n) -> p b n", n=NI)
            pool.wait_ge(mask_steps, 1)
            pool.affine_select(out=blocks, in_=blocks, compare_op=ALU.is_ge, fill=NEG, base=0,
                               pattern=[[-NI, P // NI], [0, NI]], channel_multiplier=1).then_inc(mask_steps, 1)
            pool.wait_ge(mask_steps, 2)
            pool.affine_select(out=blocks, in_=blocks, compare_op=ALU.is_ge, fill=NEG, base=NI - 1,
                               pattern=[[NI, P // NI], [0, NI]], channel_multiplier=-1).then_inc(mask_steps, 1)

        def rows(grid, i):
            return grid[:, 2 * i + 1:2 * i + 3, NI:NI + HW * NI]

        @block.scalar
        def _(act):
            def weight_high(n):
                act.wait_ge(w_loaded[n], 16)
                dst = w_h[:, n] if n < 3 else wc_h[:, :, :]
                nc.scalar.activation(dst, w_raw[:, n], ACT.Copy).then_inc(w_high, 1)

            def x_half(i):
                act.wait_ge(x_loaded[i // 2], 16)
                nc.scalar.activation(rows(grid_h, i), x_raw[:, 2 * i:2 * i + 2], ACT.Copy).then_inc(x_high, 1)

            weight_high(0)
            x_half(0)
            x_half(1)
            weight_high(1)
            x_half(2)
            weight_high(2)
            for i in range(3, NCH):
                x_half(i)
            weight_high(3)

            def copies(c, j):
                act.wait_ge(conv_done[j], c + 1)
                need(act, a_scores, c)
                need(act, v_turned, c)
                nc.scalar.activation(qkv[:, j, :], ps_conv[j][:, :], ACT.Copy).then_inc(conv_copied[j], 1)

            def exponent(c):
                act.wait_ge(shifted, c + 1)
                need(act, probs_ready, c)
                nc.scalar.activation(expd[:, :, :], scores[:, :, :], ACT.Exp, scale=scale).then_inc(a_exp, 1)

            def turn_probs(c):
                act.wait_ge(probs_turned, c + 1)
                need(act, a_out, c)
                nc.scalar.activation(probs_t[:, :, :], ps_pt[:, :].rearrange("p (g n) -> p g n", g=G),
                                     ACT.Copy).then_inc(probs_t_ready, 1)

            for j in range(3):
                copies(0, j)
            def step(c):
                exponent(c)
                copies(c + 1, 0)
                copies(c + 1, 1)
                turn_probs(c)
                copies(c + 1, 2)

            step(0)
            with act.Fori(1, NCH - 1) as c:
                step(c)
            exponent(NCH - 1)
            turn_probs(NCH - 1)

        @block.vector
        def _(dve):
            def weight_low(n):
                dve.wait_ge(w_high, n + 1)
                high, low = (w_h[:, n], w_l[:, n]) if n < 3 else (wc_h[:, :, :], wc_l[:, :, :])
                nc.vector.tensor_tensor(low, w_raw[:, n], f32(high), ALU.subtract).then_inc(w_ready, 1)

            def x_low(i, count=1):
                dve.wait_ge(x_high, i + 1)
                nc.vector.tensor_tensor(rows(grid_l, i), x_raw[:, 2 * i:2 * i + 2], f32(rows(grid_h, i)),
                                        ALU.subtract).then_inc(x_ready, count)

            weight_low(0)
            x_low(0)
            x_low(1)
            weight_low(1)
            x_low(2)
            weight_low(2)
            for i in range(3, NCH - 1):
                x_low(i)
            x_low(NCH - 1, 2)
            weight_low(3)
            dve.wait_ge(mask_steps, 3)

            def turn_v(c):
                dve.wait_ge(v_turned, c + 1)
                need(dve, a_out, c)
                nc.vector.tensor_copy(v_tok[:, :, :], ps_vt[:, :].rearrange("p (g n) -> p g n", g=G)
                                      ).then_inc(v_tok_ready, 1)

            def softmax(c):
                dve.wait_ge(a_scores, c + 1)
                need(dve, a_exp, c)
                nc.vector.tensor_tensor(scores[:, :, :], ps_s[:, :].rearrange("p (g n) -> p g n", g=G),
                                        mask[:, :].unsqueeze(1).broadcast_to([P, G, P]), ALU.add
                                        ).then_inc(masked, 1)
                dve.wait_ge(masked, c + 1)
                nc.vector.tensor_reduce(row_max[:, :], scores[:, :, :], AX.X, ALU.max).then_inc(maxed, 1)
                dve.wait_ge(maxed, c + 1)
                nc.vector.tensor_tensor(scores[:, :, :], scores[:, :, :],
                                        row_max[:, :].unsqueeze(2).broadcast_to([P, G, P]), ALU.subtract
                                        ).then_inc(shifted, 1)
                turn_v(c)
                dve.wait_ge(a_exp, c + 1)
                nc.vector.tensor_reduce(row_sum[:, :], expd[:, :, :], AX.X, ALU.add).then_inc(summed, 1)
                dve.wait_ge(summed, c + 1)
                nc.vector.reciprocal(row_inv[:, :], row_sum[:, :]).then_inc(inverted, 1)
                dve.wait_ge(inverted, c + 1)
                need(dve, probs_turned, c)
                nc.vector.tensor_tensor(probs[:, :, :], expd[:, :, :],
                                        row_inv[:, :].unsqueeze(2).broadcast_to([P, G, P]), ALU.mult
                                        ).then_inc(probs_ready, 1)

            def store_virt(c):
                dve.wait_ge(a_out, c + 1)
                dst = virt[:, :, bass.ds(2 * c, 2), :]
                nc.vector.tensor_copy(dst, ps_o[:, :].rearrange("p (h w n) -> p n h w", h=2, w=HW)
                                      ).then_inc(virt_ready, 1)

            softmax(0)
            store_virt(0)
            with dve.Fori(1, NCH) as c:
                softmax(c)
                store_virt(c)

        @block.tensor
        def _(pe):
            def convolve(c, j):
                pe.wait_ge(x_ready, c + 2)
                need(pe, conv_copied[j], c)
                for t, (dy, dx) in enumerate(TAPS):
                    span = slice(dx * NI, (dx + HW) * NI)
                    last = split_product(pe, ps_conv[j][:, :], w_h[:, j, t, :], w_l[:, j, t, :],
                                         grid_h[:, bass.ds(2 * c + dy, 2), span],
                                         grid_l[:, bass.ds(2 * c + dy, 2), span], t == 0, t == 8)
                last.then_inc(conv_done[j], 1)

            def score(c):
                for j in range(3):
                    pe.wait_ge(conv_copied[j], c + 1)
                need(pe, masked, c)
                for g in range(G):
                    part = slice(g * P, (g + 1) * P)
                    last = pe.matmul(ps_s[:, part], qkv[:, 0, part], qkv[:, 1, part], start=True, stop=True)
                last.then_inc(a_scores, 1)
                need(pe, v_tok_ready, c)
                for g in range(G):
                    part = slice(g * P, (g + 1) * P)
                    last = pe.transpose(ps_vt[:, part], qkv[:, 2, part], ident[:, :])
                last.then_inc(v_turned, 1)

            def turn(c):
                pe.wait_ge(probs_ready, c + 1)
                need(pe, probs_t_ready, c)
                for g in range(G):
                    last = pe.transpose(ps_pt[:, g * P:(g + 1) * P], probs[:, g, :], ident[:, :])
                last.then_inc(probs_turned, 1)

            def attend(c):
                pe.wait_ge(probs_t_ready, c + 1)
                pe.wait_ge(v_tok_ready, c + 1)
                need(pe, virt_ready, c)
                for g in range(G):
                    last = pe.matmul(ps_o[:, g * P:(g + 1) * P], v_tok[:, g, :], probs_t[:, g, :],
                                     start=True, stop=True)
                last.then_inc(a_out, 1)

            pe.wait_ge(border_zeroed, 4)
            pe.wait_ge(ident_ready, 1)
            for j in range(3):
                pe.wait_ge(w_ready, j + 1)
                convolve(0, j)

            def step(c):
                score(c)
                convolve(c + 1, 0)
                turn(c)
                convolve(c + 1, 1)
                attend(c)
                convolve(c + 1, 2)

            step(0)
            with pe.Fori(1, NCH - 1) as c:
                step(c)
            score(NCH - 1)
            turn(NCH - 1)
            attend(NCH - 1)


def image_norm(nc, sb, sem, bank, pad_h, pad_l, virt, gamma, beta, ones, norm_a, norm_b):
    with ExitStack() as ctx:
        stats = sb("stats", [P, NI, 6], where=ctx)
        chan = sb("chan", [P, NI, 2], where=ctx)
        off = sb("off", [P, NI], where=ctx)
        spread = sb("spread", [P, NI], where=ctx)
        mu = sb("mu", [P, NI], where=ctx)
        var = sb("var", [P, NI], where=ctx)
        power = sb("power", [P, NI], where=ctx)
        gb = sb("gb", [P, 2], where=ctx)

        gb_loaded = sem("gb_loaded")
        b_consts = sem("b_consts")
        border2_zeroed = sem("border2_zeroed")
        stats_done = sem("stats_done")
        chan_done = sem("chan_done")
        mean_summed = sem("mean_summed")
        b_steps = sem("b_steps")
        var_summed = sem("var_summed")
        rstd_done = sem("rstd_done")
        block = ctx.enter_context(nc.Block())

        @block.sync
        def _(sp):
            sp.dma_start(gb[:, 0:1], gamma).then_inc(gb_loaded, 16)
            sp.dma_start(gb[:, 1:2], beta).then_inc(gb_loaded, 16)

        @block.gpsimd
        def _(pool):
            pool.memset(power[:, :], -0.5).then_inc(b_consts, 1)
            pool.memset(ones[:, :], 1.0 / P).then_inc(b_consts, 1)
            for pad in (pad_h, pad_l):
                grid = pad[:, :].rearrange("p (n h w) -> p n h w", n=NI, h=PAD)
                pool.memset(f32(grid[:, :, 0:PAD:PAD - 1, :]), 0.0).then_inc(border2_zeroed, 1)
                pool.memset(f32(grid[:, :, 1:PAD - 1, 0:PAD:PAD - 1]), 0.0).then_inc(border2_zeroed, 1)
            pool.wait_ge(b_consts, 2)
            pool.wait_ge(b_steps, 4)
            pool.tensor_tensor(norm_a[:, :], var[:, :], power[:, :], ALU.pow).then_inc(rstd_done, 1)

        @block.vector
        def _(dve):
            for n in range(NI):
                nc.vector.bn_stats(stats[:, n, :], virt[:, n].rearrange("p h w -> p (h w)")).then_inc(stats_done, 1)
            dve.wait_ge(stats_done, NI)
            for n in range(NI):
                nc.vector.bn_aggr(chan[:, n, :], stats[:, n, :]).then_inc(chan_done, 1)
            dve.wait_ge(mean_summed, 1)
            nc.vector.tensor_copy(mu[:, :], bank[0][:, 0:NI]).then_inc(b_steps, 1)
            dve.wait_ge(b_steps, 1)
            nc.vector.tensor_tensor(off[:, :], chan[:, :, 0], mu[:, :], ALU.subtract).then_inc(b_steps, 1)
            dve.wait_ge(b_steps, 2)
            nc.vector.tensor_tensor(spread[:, :], off[:, :], off[:, :], ALU.mult).then_inc(b_steps, 1)
            dve.wait_ge(b_steps, 3)
            nc.vector.tensor_tensor(off[:, :], spread[:, :], chan[:, :, 1], ALU.add).then_inc(var_summed, 1)
            dve.wait_ge(var_summed, 2)
            nc.vector.tensor_scalar(var[:, :], bank[1][:, 0:NI], EPS, None, ALU.add).then_inc(b_steps, 1)
            dve.wait_ge(rstd_done, 1)
            dve.wait_ge(gb_loaded, 32)
            nc.vector.tensor_scalar(norm_a[:, :], norm_a[:, :], gb[:, 0:1], None, ALU.mult).then_inc(b_steps, 1)
            dve.wait_ge(b_steps, 5)
            nc.vector.tensor_tensor(off[:, :], mu[:, :], norm_a[:, :], ALU.mult).then_inc(b_steps, 1)
            dve.wait_ge(b_steps, 6)
            nc.vector.tensor_scalar(norm_b[:, :], off[:, :], -1.0, gb[:, 1:2], ALU.mult, ALU.add).then_inc(b_steps, 1)

        @block.tensor
        def _(pe):
            pe.wait_ge(b_consts, 2)
            pe.wait_ge(chan_done, NI)
            pe.matmul(bank[0][:, 0:NI], ones[:, :], chan[:, :, 0], start=True, stop=True).then_inc(mean_summed, 1)
            pe.wait_ge(var_summed, 1)
            pe.matmul(bank[1][:, 0:NI], ones[:, :], off[:, :], start=True, stop=True).then_inc(var_summed, 1)


def token_attention(nc, sb, sem, bank, pad_h, pad_l, resid, virt, z2_h, z2_l, logits, ident, wc_h, wc_l, norm_a,
                    norm_b, d_wqs, d_wks, d_wvr, d_wqrT, d_wkretT, d_wout, d_wg):
    S, D = 8, 16
    NP = S // 2
    NR = 160
    RV = 34
    RVW = 96
    with ExitStack() as ctx:
        t_chunk = sb("t_chunk", [P, CH], where=ctx)
        z_tok = sb("z_tok", [P, G, P], where=ctx)
        zt = sb("zt", [P, CH], where=ctx)
        zt_h = sb("zt_h", [P, CH], F32R, ctx)
        zt_l = sb("zt_l", [P, CH], F32R, ctx)
        wq = sb("wq", [P, P], where=ctx)
        wk = sb("wk", [P, P], where=ctx)
        wq_h = sb("wq_h", [P, P], F32R, ctx)
        wq_l = sb("wq_l", [P, P], F32R, ctx)
        wk_h = sb("wk_h", [P, P], F32R, ctx)
        wk_l = sb("wk_l", [P, P], F32R, ctx)
        wvr = sb("wvr", [P, 2 * D], where=ctx)
        wqr_t = sb("wqr_t", [P, P], where=ctx)
        ret_blocks = sb("ret_blocks", [P, P], where=ctx)
        w_tok = sb("w_tok", [P, NR], where=ctx)
        wout = sb("wout", [P, P], where=ctx)
        wg = sb("wg", [P, S], where=ctx)
        q_h = sb("q_h", [P, CH], F32R, ctx)
        q_l = sb("q_l", [P, CH], F32R, ctx)
        k_h = sb("k_h", [P, CH], F32R, ctx)
        k_l = sb("k_l", [P, CH], F32R, ctx)
        q_stack = sb("q_stack", [P, NP, CH], F32R, ctx)
        k_stack = sb("k_stack", [P, S, CH], F32R, ctx)
        one_rows = sb("one_rows", [P, 2, CH], where=ctx)
        rvx = sb("rvx", [P, G, RVW], where=ctx)
        r_query = virt[:, :].rearrange("p n h w -> p (n h w)").rearrange("p (g j f) -> p g j f", j=G, f=P)
        s_max = sb("s_max", [P, 2, S], where=ctx)
        m_split = sb("m_split", [P, 2, S, 2], F32R, ctx)
        m_rows = sb("m_rows", [2 * S, PIX], F32R, ctx)
        expd = sb("s_expd", [P, 2, 2, PIX], where=ctx)
        ret = sb("ret", [P, 2, S, 2, RV], where=ctx)
        prod = sb("prod", [P, 2, S, D], where=ctx)
        sim = sb("sim", [P, 2, S], where=ctx)
        r_inv = sb("r_inv", [P, 2, S], where=ctx)
        r_gate = sb("r_gate", [P, 2, S], where=ctx)
        o_tok = sb("o_tok", [P, G, P], where=ctx)
        o_t = sb("o_t", [P, CH], where=ctx)
        ln_stats = sb("ln_stats", [P, G, 6], where=ctx)
        ln_mv = sb("ln_mv", [P, G, 2], where=ctx)
        ln_var = sb("ln_var", [P, G], where=ctx)
        ln_rstd = sb("ln_rstd", [P, G], where=ctx)
        power = sb("ln_power", [P, G], where=ctx)

        y_done = sem("y_done")
        y_high = sem("y_high")
        y_ready = sem("y_ready")
        a_loaded = sem("a_loaded")
        blocks_zeroed = sem("blocks_zeroed")
        blocks_loaded = sem("blocks_loaded")
        c_consts = sem("c_consts")
        ones_steps = sem("ones_steps")
        stack_init = sem("stack_init")
        wa_high = sem("wa_high")
        wa_ready = sem("wa_ready")
        folded = sem("folded")
        w_tok_ready = sem("w_tok_ready")
        conv_done = sem("convc_done")
        t_ready = sem("t_ready")
        t_kept = sem("t_kept")
        t_turned = sem("t_turned")
        ln_steps = sem("ln_steps")
        ln_power = sem("ln_power_done")
        z_ready = sem("z_ready")
        z_turned = sem("z_turned")
        zt_steps = sem("zt_steps")
        zt_ready = sem("zt_ready")
        q_done = sem("q_done")
        k_done = sem("k_done")
        q_high = sem("q_high")
        k_high = sem("k_high")
        q_ready = sem("q_ready")
        k_ready = sem("k_ready")
        tok_done = sem("tok_done")
        tok_copied = sem("tok_copied")
        stacked = [sem("stacked0"), sem("stacked1")]
        s_done = sem("s_done")
        max_done = sem("max_done")
        m_steps = sem("m_steps")
        m_turned = sem("m_turned")
        m_ready = sem("m_ready")
        m_moved = sem("m_moved")
        st_done = sem("st_done")
        exp_done = sem("exp_done")
        pv_done = sem("pv_done")
        ret_copied = sem("ret_copied")
        ret_steps = sem("ret_steps")
        gate_exp = sem("gate_exp")
        o_turned = sem("o_turned")
        o_t_ready = sem("o_t_ready")
        out_done = sem("out_done")
        t2_ready = sem("t2_ready")
        t2_kept = sem("t2_kept")
        t2_turned = sem("t2_turned")
        z2_turned = sem("z2_turned")
        z2_steps = sem("z2_steps")
        z2_ready = sem("z2_ready")
        routed = sem("routed")
        logits_kept = sem("logits_kept")
        t2_chunk, z2_tok, z2_f = sb("t2_chunk", [P, CH], where=ctx), sb("z2_tok", [P, G, P], where=ctx), \
            sb("z2_f", [P, CH], where=ctx)

        img_h = pad_h[:, :].rearrange("p (n h w) -> p n h w", n=NI, h=PAD)
        img_l = pad_l[:, :].rearrange("p (n h w) -> p n h w", n=NI, h=PAD)
        ps_conv, ps_s, ps_st, ps_pv, ps_x = bank[0], bank[1:3], bank[3:5], bank[5:7], bank[7]
        WLOADS = 6
        STACK = 16 * (3 * NP + 3 * S)
        RS, LS = 10, 3
        block = ctx.enter_context(nc.Block())

        def chunk(tensor, g):
            return tensor[:, bass.ds(g * CH, CH)]

        @block.sync
        def _(sp):
            for dst, src in ((wq, d_wqs), (wk, d_wks), (wvr, d_wvr), (wqr_t, d_wqrT), (wout, d_wout), (wg, d_wg)):
                sp.dma_start(dst[:, :], src).then_inc(a_loaded, 16)
            sp.wait_ge(blocks_zeroed, 1)
            for s in range(S):
                at = slice(s * D, (s + 1) * D)
                sp.dma_start(ret_blocks[at, at], d_wkretT).then_inc(blocks_loaded, 16)

            def stack(g, b):
                tok = slice(b * PIX, (b + 1) * PIX)
                if b == 0:
                    sp.wait_ge(q_ready, g + 1)
                else:
                    need(sp, st_done, 2 * S * g)
                for p in range(NP):
                    for slot, part in enumerate((q_h, q_l, q_h)):
                        sp.dma_start(f32(q_stack[32 * slot:32 * slot + 32, p, tok]), f32(part[32 * p:32 * p + 32, tok])
                                     ).then_inc(stacked[b], 16)
                if b == 0:
                    sp.wait_ge(k_ready, g + 1)
                for s in range(S):
                    for slot, part in enumerate((k_h, k_h, k_l)):
                        row = 32 * slot + D * (s % 2)
                        sp.dma_start(f32(k_stack[row:row + D, s, tok]), f32(part[D * s:D * s + D, tok])
                                     ).then_inc(stacked[b], 16)

            def move_max(g, b):
                sp.wait_ge(m_ready, 2 * g + b + 1)
                for p in range(NP):
                    sp.dma_start(f32(q_stack[96:100, p, b * PIX:(b + 1) * PIX]), f32(m_rows[4 * p:4 * p + 4, :])
                                 ).then_inc(m_moved, 16)

            def body(g, last=False):
                move_max(g, 0)
                move_max(g, 1)
                if not last:
                    stack(g + 1, 0)
                    stack(g + 1, 1)

            sp.wait_ge(stack_init, NP + 1)
            stack(0, 0)
            stack(0, 1)
            body(0)
            with sp.Fori(1, NCH - 1) as g:
                body(g)
            body(NCH - 1, last=True)

        @block.gpsimd
        def _(pool):
            pool.memset(ret_blocks[:, :], 0.0).then_inc(blocks_zeroed, 1)
            pool.memset(power[:, :], -0.5).then_inc(c_consts, 1)
            pool.memset(rvx[:, :, 2 * D:RVW], 1.0).then_inc(c_consts, 1)
            pool.memset(f32(k_stack[:, :, :]), 0.0).then_inc(stack_init, 1)
            pool.wait_ge(blocks_zeroed, 1)
            pool.wait_ge(c_consts, 2)
            pool.wait_ge(stack_init, 1)
            pool.memset(one_rows[96:100], 1.0).then_inc(ones_steps, 1)
            pool.wait_ge(ones_steps, 1)
            pool.affine_select(out=one_rows[96:100], in_=one_rows[96:100], compare_op=ALU.is_ge, fill=0.0, base=0,
                               pattern=[[-2, 2], [0, CH]], channel_multiplier=1).then_inc(ones_steps, 1)
            pool.wait_ge(ones_steps, 2)
            pool.affine_select(out=one_rows[96:100], in_=one_rows[96:100], compare_op=ALU.is_ge, fill=0.0, base=1,
                               pattern=[[2, 2], [0, CH]], channel_multiplier=-1).then_inc(ones_steps, 1)
            pool.wait_ge(ones_steps, 3)
            for p in range(NP):
                pool.tensor_copy(k_stack[96:100, 2 * p:2 * p + 2, :], one_rows[96:100]).then_inc(stack_init, 1)
                pool.wait_ge(stack_init, p + 2)

            def rstd(n):
                pool.wait_ge(ln_steps, LS * n + 3)
                pool.tensor_tensor(ln_rstd[:, :], ln_var[:, :], power[:, :], ALU.pow).then_inc(ln_power, 1)

            rstd(0)
            rstd(1)
            with pool.Fori(2, 2 * NCH) as n:
                rstd(n)

        @block.scalar
        def _(act):
            def normalise(n):
                nc.scalar.activation(virt[:, n], virt[:, n], ACT.Relu, scale=norm_a[:, n:n + 1],
                                     bias=norm_b[:, n:n + 1]).then_inc(y_done, 1)

            def high(n):
                act.wait_ge(y_done, n + 1)
                nc.scalar.activation(img_h[:, n, 1:1 + HW, 1:1 + HW], virt[:, n], ACT.Copy).then_inc(y_high, 1)

            for n in range(NI):
                normalise(n)
                if n % 2:
                    high(n - 1)
                    high(n)
            act.wait_ge(a_loaded, 16 * WLOADS)
            nc.scalar.activation(wq_h[:, :], wq[:, :], ACT.Copy, scale=float(D) ** -0.5).then_inc(wa_high, 1)
            nc.scalar.activation(wk_h[:, :], wk[:, :], ACT.Copy).then_inc(wa_high, 1)

            def keep_t(g):
                act.wait_ge(t_ready, g + 1)
                nc.scalar.activation(chunk(resid, g), t_chunk[:, :], ACT.Copy).then_inc(t_kept, 1)

            def split_zt(g):
                act.wait_ge(z_turned, g + 1)
                nc.scalar.activation(zt[:, :], ps_conv[:, :], ACT.Copy).then_inc(zt_steps, 1)
                act.wait_ge(zt_steps, 2 * g + 1)
                nc.scalar.activation(zt_h[:, :], zt[:, :], ACT.Copy).then_inc(zt_steps, 1)

            def split_qk(g):
                if not (isinstance(g, int) and g == 0):
                    for b in range(2):
                        act.wait_ge(stacked[b], STACK * g)
                act.wait_ge(q_done, g + 1)
                nc.scalar.activation(q_h[:, :], ps_x[:, :], ACT.Copy).then_inc(q_high, 1)
                act.wait_ge(k_done, g + 1)
                nc.scalar.activation(k_h[:, :], ps_conv[:, :], ACT.Copy).then_inc(k_high, 1)

            def keep_tok(g, half):
                act.wait_ge(tok_done, 2 * g + half + 1)
                need(act, pv_done, 2 * S * g)
                src = (ps_x, ps_conv)[half][:, 0:2 * NR].rearrange("p (j f) -> p j f", j=2)
                two = slice(2 * half, 2 * half + 2)
                nc.scalar.activation(r_query[:, g, two, :], src[:, :, 0:P], ACT.Copy).then_inc(tok_copied, 1)
                nc.scalar.activation(rvx[:, two, 0:2 * D], src[:, :, P:NR], ACT.Copy).then_inc(tok_copied, 1)

            def exponent(g, b, s):
                act.wait_ge(st_done, 2 * S * g + S * b + s + 1)
                need(act, pv_done, 2 * S * g + S * b + s - 1)
                nc.scalar.activation(expd[:, s % 2].rearrange("p a i -> p (a i)"), ps_st[s % 2][:, :], ACT.Exp
                                     ).then_inc(exp_done, 1)

            def keep_ret(g, b, half):
                act.wait_ge(pv_done, 2 * S * g + S * b + 4 * half + 4)
                need(act, ret_steps, RS * (2 * g + b - 1))
                nc.scalar.activation(ret[:, b, 4 * half:4 * half + 4].rearrange("p s i f -> p (s i f)"),
                                     ps_pv[half][:, 0:8 * RV], ACT.Copy).then_inc(ret_copied, 1)

            def gate(g, b):
                act.wait_ge(ret_steps, RS * (2 * g + b) + 4)
                nc.scalar.activation(r_gate[:, :, :], sim[:, :, :], ACT.Exp, scale=-1.0).then_inc(gate_exp, 1)

            def keep_o(g):
                act.wait_ge(o_turned, g + 1)
                nc.scalar.activation(o_t[:, :], ps_x[:, :], ACT.Copy).then_inc(o_t_ready, 1)

            def keep_t2(g):
                act.wait_ge(t2_ready, g + 1)
                nc.scalar.activation(chunk(resid, g), t2_chunk[:, :], ACT.Copy).then_inc(t2_kept, 1)

            def split_z2(g):
                act.wait_ge(z2_turned, g + 1)
                nc.scalar.activation(z2_f[:, :], ps_x[:, :], ACT.Copy).then_inc(z2_steps, 1)
                act.wait_ge(z2_steps, 2 * g + 1)
                nc.scalar.activation(chunk(z2_h, g), z2_f[:, :], ACT.Copy).then_inc(z2_steps, 1)

            def body(g, first=False, last=False):
                if not first:
                    gate(g - 1, 1)
                if not last:
                    keep_t(g + 1)
                for s in range(S):
                    exponent(g, 0, s)
                    if not first:
                        if s == 0:
                            keep_o(g - 1)
                        if s == 2:
                            keep_t2(g - 1)
                        if s == 5:
                            split_z2(g - 1)
                keep_ret(g, 0, 0)
                keep_ret(g, 0, 1)
                for s in range(S):
                    exponent(g, 1, s)
                    if s == 1:
                        gate(g, 0)
                    if not last and s == 2:
                        split_zt(g + 1)
                    if not last and s == 4:
                        split_qk(g + 1)
                    if s == 5:
                        keep_ret(g, 1, 0)
                keep_ret(g, 1, 1)
                if not last:
                    keep_tok(g + 1, 0)
                    keep_tok(g + 1, 1)

            act.wait_ge(y_ready, NI)
            keep_t(0)
            split_zt(0)
            split_qk(0)
            keep_tok(0, 0)
            keep_tok(0, 1)
            body(0, first=True)
            with act.Fori(1, NCH - 1) as g:
                body(g)
            body(NCH - 1, last=True)
            gate(NCH - 1, 1)
            keep_o(NCH - 1)
            keep_t2(NCH - 1)
            split_z2(NCH - 1)

        @block.vector
        def _(dve):
            def low(n):
                dve.wait_ge(y_high, n + 1)
                inside = img_l[:, n, 1:1 + HW, 1:1 + HW]
                nc.vector.tensor_tensor(inside, virt[:, n], f32(img_h[:, n, 1:1 + HW, 1:1 + HW]), ALU.subtract
                                        ).then_inc(y_ready, 1)

            for n in range(NI):
                low(n)
            dve.wait_ge(wa_high, 1)
            nc.vector.scalar_tensor_tensor(wq_l[:, :], wq[:, :], float(D) ** -0.5, f32(wq_h[:, :]), ALU.mult,
                                           ALU.subtract).then_inc(wa_ready, 1)
            dve.wait_ge(wa_high, 2)
            nc.vector.tensor_tensor(wk_l[:, :], wk[:, :], f32(wk_h[:, :]), ALU.subtract).then_inc(wa_ready, 1)
            nc.vector.tensor_tensor(w_tok[:, P:P + D], wvr[:, 0:D], wvr[:, D:2 * D], ALU.subtract
                                    ).then_inc(w_tok_ready, 1)
            nc.vector.tensor_copy(w_tok[:, P + D:NR], wvr[:, D:2 * D]).then_inc(w_tok_ready, 1)
            dve.wait_ge(folded, 1)
            nc.vector.tensor_scalar(w_tok[:, 0:P], ps_x[:, 0:P], float(D) ** -0.5, None, ALU.mult
                                    ).then_inc(w_tok_ready, 1)
            dve.wait_ge(c_consts, 2)

            def add_conv(g):
                dve.wait_ge(conv_done, g + 1)
                need(dve, t_kept, g)
                need(dve, t_turned, g)
                nc.vector.tensor_tensor(t_chunk[:, :], ps_conv[:, :], chunk(resid, g), ALU.add).then_inc(t_ready, 1)

            def layer_norm(n, turned, count, dst):
                dve.wait_ge(turned, count)
                for j in range(G):
                    last = nc.vector.bn_stats(ln_stats[:, j, :], ps_x[:, j * P:(j + 1) * P])
                last.then_inc(ln_steps, 1)
                dve.wait_ge(ln_steps, LS * n + 1)
                nc.vector.memset(ln_var[:, :], 0.0)
                for j in range(G):
                    last = nc.vector.bn_aggr(ln_mv[:, j, :], ln_stats[:, j, :])
                last.then_inc(ln_steps, 1)
                dve.wait_ge(ln_steps, LS * n + 2)
                nc.vector.tensor_scalar(ln_var[:, :], ln_mv[:, :, 1], EPS, None, ALU.add).then_inc(ln_steps, 1)
                dve.wait_ge(ln_power, n + 1)
                for j in range(G):
                    last = nc.vector.tensor_scalar(dst[:, j, :], ps_x[:, j * P:(j + 1) * P], ln_mv[:, j, 0:1],
                                                   ln_rstd[:, j:j + 1], ALU.subtract, ALU.mult)
                last.then_inc(z_ready, 1)

            def low_zt(g):
                dve.wait_ge(zt_steps, 2 * g + 2)
                nc.vector.tensor_tensor(zt_l[:, :], zt[:, :], f32(zt_h[:, :]), ALU.subtract).then_inc(zt_ready, 1)

            def low_qk(g):
                dve.wait_ge(q_high, g + 1)
                nc.vector.tensor_tensor(q_l[:, :], ps_x[:, :], f32(q_h[:, :]), ALU.subtract).then_inc(q_ready, 1)
                dve.wait_ge(k_high, g + 1)
                nc.vector.tensor_tensor(k_l[:, :], ps_conv[:, :], f32(k_h[:, :]), ALU.subtract).then_inc(k_ready, 1)

            def row_max(g, b, s):
                dve.wait_ge(s_done, 2 * S * g + S * b + s + 1)
                nc.vector.tensor_reduce(s_max[:, :, s], ps_s[s % 2][:, :].rearrange("p (a j) -> p a j", a=2), AX.X,
                                        ALU.max).then_inc(max_done, 1)

            def split_max(g, b):
                dve.wait_ge(max_done, 2 * S * g + S * b + S)
                nc.vector.tensor_scalar(m_split[:, :, :, 0], s_max[:, :, :], -1.0, None, ALU.mult).then_inc(m_steps, 1)
                dve.wait_ge(m_steps, 2 * (2 * g + b) + 1)
                nc.vector.scalar_tensor_tensor(m_split[:, :, :, 1], s_max[:, :, :], -1.0, f32(m_split[:, :, :, 0]),
                                               ALU.mult, ALU.subtract).then_inc(m_steps, 1)
                dve.wait_ge(m_turned, 2 * g + b + 1)
                need(dve, m_moved, 16 * NP * (2 * g + b))
                nc.vector.tensor_copy(m_rows[:, :], ps_x[0:2 * S, 0:PIX]).then_inc(m_ready, 1)

            def retrieve(g, b):
                r = ret[:, b].rearrange("p s i f -> p i s f")
                diff, value1, total = r[:, :, :, 0:D], r[:, :, :, D:2 * D], r[:, :, :, 2 * D]
                query = r_query[:, g, 2 * b:2 * b + 2, :].rearrange("p i (s d) -> p i s d", s=S)
                base = RS * (2 * g + b)
                wide = [P, 2, S, D]
                need(dve, ret_steps, base)
                dve.wait_ge(ret_copied, 2 * (2 * g + b) + 2)
                nc.vector.reciprocal(r_inv[:, :, :], total).then_inc(ret_steps, 1)
                nc.vector.tensor_tensor(prod[:, :, :, :], diff, query, ALU.mult).then_inc(ret_steps, 1)
                dve.wait_ge(ret_steps, base + 2)
                nc.vector.tensor_reduce(sim[:, :, :], prod[:, :, :, :], AX.X, ALU.add).then_inc(ret_steps, 1)
                dve.wait_ge(ret_steps, base + 3)
                nc.vector.tensor_tensor(sim[:, :, :], sim[:, :, :], r_inv[:, :, :], ALU.mult).then_inc(ret_steps, 1)
                dve.wait_ge(gate_exp, 2 * g + b + 1)
                nc.vector.tensor_scalar(r_gate[:, :, :], r_gate[:, :, :], 1.0, None, ALU.add).then_inc(ret_steps, 1)
                dve.wait_ge(ret_steps, base + 5)
                nc.vector.reciprocal(r_gate[:, :, :], r_gate[:, :, :]).then_inc(ret_steps, 1)
                dve.wait_ge(ret_steps, base + 6)
                nc.vector.tensor_tensor(prod[:, :, :, :], diff, r_gate[:, :, :].unsqueeze(3).broadcast_to(wide),
                                        ALU.mult).then_inc(ret_steps, 1)
                dve.wait_ge(ret_steps, base + 7)
                nc.vector.tensor_tensor(prod[:, :, :, :], prod[:, :, :, :], value1, ALU.add).then_inc(ret_steps, 1)
                dve.wait_ge(ret_steps, base + 8)
                need(dve, o_turned, g)
                nc.vector.tensor_tensor(o_tok[:, 2 * b:2 * b + 2, :].rearrange("p i (s d) -> p i s d", s=S),
                                        prod[:, :, :, :], r_inv[:, :, :].unsqueeze(3).broadcast_to(wide),
                                        ALU.mult).then_inc(ret_steps, 2)

            def add_attention(g):
                dve.wait_ge(out_done, g + 1)
                nc.vector.tensor_tensor(t2_chunk[:, :], ps_x[:, :], chunk(resid, g), ALU.add).then_inc(t2_ready, 1)

            def low_z2(g):
                dve.wait_ge(z2_steps, 2 * g + 2)
                nc.vector.tensor_tensor(chunk(z2_l, g), z2_f[:, :], f32(chunk(z2_h, g)), ALU.subtract
                                        ).then_inc(z2_ready, 1)

            def keep_logits(g):
                dve.wait_ge(routed, g + 1)
                nc.vector.tensor_copy(logits[:, bass.ds(g * G, G), :],
                                      ps_x[:, 0:G * S].rearrange("p (j e) -> p j e", j=G)).then_inc(logits_kept, 1)

            def body(g, first=False, last=False):
                for s in range(S):
                    row_max(g, 0, s)
                    if s == 3 and not first:
                        retrieve(g - 1, 1)
                split_max(g, 0)
                for s in range(S):
                    row_max(g, 1, s)
                    if s == 0 and not last:
                        add_conv(g + 1)
                    if not first:
                        if s == 1:
                            add_attention(g - 1)
                        if s == 3:
                            layer_norm(2 * g, t2_turned, g, z2_tok)
                        if s == 6:
                            low_z2(g - 1)
                        if s == 7:
                            keep_logits(g - 1)
                split_max(g, 1)
                if not last:
                    layer_norm(1 if first else 2 * g + 1, t_turned, g + 2, z_tok)
                retrieve(g, 0)
                if not last:
                    low_zt(g + 1)
                    low_qk(g + 1)

            add_conv(0)
            layer_norm(0, t_turned, 1, z_tok)
            low_zt(0)
            low_qk(0)
            body(0, first=True)
            with dve.Fori(1, NCH - 1) as g:
                body(g)
            body(NCH - 1, last=True)
            retrieve(NCH - 1, 1)
            add_attention(NCH - 1)
            layer_norm(2 * NCH - 1, t2_turned, NCH, z2_tok)
            low_z2(NCH - 1)
            keep_logits(NCH - 1)

        @block.tensor
        def _(pe):
            def conv_taps(g, taps):
                if taps[0] == 0:
                    pe.wait_ge(y_ready, 2 * g + 2)
                    need(pe, tok_copied, 4 * g)
                for t in taps:
                    dy, dx = TAPS[t]
                    part = (slice(None), bass.ds(2 * g, 2), slice(dy, dy + HW), slice(dx, dx + HW))
                    last = split_product(pe, ps_conv[:, :], wc_h[:, t, :], wc_l[:, t, :], img_h[part], img_l[part],
                                         t == 0, t == 8)
                if taps[-1] == 8:
                    last.then_inc(conv_done, 1)

            def turn(dst, src, signal):
                for j in range(G):
                    last = pe.transpose(dst[:, j * P:(j + 1) * P], src[:, j * P:(j + 1) * P], ident[:, :])
                last.then_inc(signal, 1)

            def flat(t):
                return t[:, :, :].rearrange("p j f -> p (j f)")

            def head_turn(g):
                pe.wait_ge(t_ready, g + 1)
                turn(ps_x, t_chunk, t_turned)

            def head_turn_back(g, norm):
                pe.wait_ge(z_ready, norm)
                turn(ps_conv, flat(z_tok), z_turned)

            def head_project(g):
                pe.wait_ge(zt_ready, g + 1)
                split_product(pe, ps_x[:, :], wq_h[:, :], wq_l[:, :], zt_h[:, :], zt_l[:, :], True, True
                              ).then_inc(q_done, 1)
                split_product(pe, ps_conv[:, :], wk_h[:, :], wk_l[:, :], zt_h[:, :], zt_l[:, :], True, True
                              ).then_inc(k_done, 1)

            def head_tokens(g):
                for half, (ps, free) in enumerate(((ps_x, q_ready), (ps_conv, k_ready))):
                    pe.wait_ge(free, g + 1)
                    for j in range(2):
                        at = (2 * half + j) * P
                        last = pe.matmul(ps[:, j * NR:(j + 1) * NR], zt[:, at:at + P], w_tok[:, :], start=True,
                                         stop=True)
                    last.then_inc(tok_done, 1)

            def scores(g, b, s):
                if s == 0:
                    pe.wait_ge(stacked[b], STACK * (g + 1))
                need(pe, max_done, 2 * S * g + S * b + s - 1)
                at = b * PIX
                for i in range(2):
                    last = pe.matmul(ps_s[s % 2][:, i * PIX:(i + 1) * PIX],
                                     q_stack[0:96, s // 2, at + i * P:at + (i + 1) * P],
                                     k_stack[0:96, s, at:at + PIX], start=True, stop=True)
                last.then_inc(s_done, 1)

            def turn_max(g, b, free, count):
                pe.wait_ge(m_steps, 2 * (2 * g + b) + 2)
                need(pe, free, count)
                for i in range(2):
                    src = f32(m_split[:, i].rearrange("p s t -> p (s t)"))
                    last = pe.transpose(ps_x[0:2 * S, i * P:(i + 1) * P], src, ident[:, :])
                last.then_inc(m_turned, 1)

            def shifted_scores(g, b, s):
                if s == 0:
                    pe.wait_ge(m_moved, 16 * NP * (2 * g + b + 1))
                need(pe, exp_done, 2 * S * g + S * b + s - 1)
                at = b * PIX
                for i in range(2):
                    last = pe.matmul(ps_st[s % 2][:, i * PIX:(i + 1) * PIX],
                                     k_stack[0:100, s, at + i * P:at + (i + 1) * P],
                                     q_stack[0:100, s // 2, at:at + PIX], start=True, stop=True)
                last.then_inc(st_done, 1)

            def retrieve(g, b, s):
                pe.wait_ge(exp_done, 2 * S * g + S * b + s + 1)
                if s % 4 == 0:
                    need(pe, ret_copied, 2 * (2 * g + b - 1) + s // 4 + 1)
                if s == 0 and b == 0:
                    pe.wait_ge(tok_copied, 4 * g + 4)
                for i in range(2):
                    at = ((s % 4) * 2 + i) * RV
                    for a in range(2):
                        last = pe.matmul(ps_pv[s // 4][:, at:at + RVW], expd[:, s % 2, a, i * P:(i + 1) * P],
                                         rvx[:, 2 * b + a, :], start=(a == 0), stop=(a == 1))
                last.then_inc(pv_done, 1)

            def tail_turn(g):
                pe.wait_ge(ret_steps, RS * (2 * g + 2))
                pe.wait_ge(m_ready, 2 * g + 3 if not (isinstance(g, int) and g == NCH - 1) else 2 * NCH)
                turn(ps_x, flat(o_tok), o_turned)

            def tail_out(g):
                pe.wait_ge(o_t_ready, g + 1)
                pe.matmul(ps_x[:, :], wout[:, :], o_t[:, :], start=True, stop=True).then_inc(out_done, 1)

            def tail_turn2(g):
                pe.wait_ge(t2_ready, g + 1)
                turn(ps_x, t2_chunk, t2_turned)

            def tail_turn_back(g, norm):
                pe.wait_ge(z_ready, norm)
                turn(ps_x, flat(z2_tok), z2_turned)

            def tail_route(g):
                pe.wait_ge(z2_steps, 2 * g + 1)
                for j in range(G):
                    last = pe.matmul(ps_x[:, j * S:(j + 1) * S], z2_f[:, j * P:(j + 1) * P], wg[:, :], start=True,
                                     stop=True)
                last.then_inc(routed, 1)

            def body(g, first=False, last=False):
                for s in range(S):
                    scores(g, 0, s)
                    if not last:
                        conv_taps(g + 1, range(s, s + 1) if s < 7 else range(7, 9))
                turn_max(g, 0, tok_copied, 4 * g + 2)
                for s in range(S):
                    shifted_scores(g, 0, s)
                    scores(g, 1, s)
                    if s:
                        retrieve(g, 0, s - 1)
                    if not first:
                        if s == 0:
                            tail_turn(g - 1)
                        if s == 1:
                            tail_out(g - 1)
                        if s == 2:
                            tail_turn2(g - 1)
                        if s == 5:
                            tail_turn_back(g - 1, 2 * g + 1)
                        if s == 6:
                            tail_route(g - 1)
                retrieve(g, 0, S - 1)
                turn_max(g, 1, *((m_ready, 1) if first else (logits_kept, g)))
                if not last:
                    pe.wait_ge(m_ready, 2 * g + 2)
                    head_turn(g + 1)
                for s in range(S):
                    shifted_scores(g, 1, s)
                    if s:
                        retrieve(g, 1, s - 1)
                    if not last and s == 2:
                        head_turn_back(g + 1, 2 if first else 2 * g + 2)
                    if not last and s == 4:
                        head_project(g + 1)
                retrieve(g, 1, S - 1)
                if not last:
                    head_tokens(g + 1)

            pe.wait_ge(a_loaded, 16 * WLOADS)
            pe.wait_ge(blocks_loaded, 16 * S)
            pe.matmul(ps_x[:, 0:P], wqr_t[:, :], ret_blocks[:, :], start=True, stop=True).then_inc(folded, 1)
            conv_taps(0, range(9))
            pe.wait_ge(w_tok_ready, 3)
            pe.wait_ge(wa_ready, 2)
            head_turn(0)
            head_turn_back(0, 1)
            head_project(0)
            head_tokens(0)
            body(0, first=True)
            with pe.Fori(1, NCH - 1) as g:
                body(g)
            body(NCH - 1, last=True)
            tail_turn(NCH - 1)
            tail_out(NCH - 1)
            tail_turn2(NCH - 1)
            tail_turn_back(NCH - 1, 2 * NCH)
            tail_route(NCH - 1)


def experts(nc, sb, sem, bank, resid, z2_h, z2_l, logits, ident, f_w1, f_w2, out):
    E, FB = 8, 4
    NK = E * FB
    NT = NCH * G
    HR, YR = 4, 2
    with ExitStack() as ctx:
        w1 = sb("w1", [P, E, CH], where=ctx)
        w1_h = sb("w1_h", [P, E, CH], F32R, ctx)
        w1_l = sb("w1_l", [P, E, CH], F32R, ctx)
        w2 = sb("w2", [P, E, FB, P], where=ctx)
        rank_i = sb("rank_i", [P, E], I32, ctx)
        rank = sb("rank", [P, E], where=ctx)
        hot = sb("hot", [P, 2, NT, E], where=ctx)
        best = sb("best", [P, 2, NT], where=ctx)
        first = sb("first", [P, NT], where=ctx)
        other = sb("other", [P, NT, E], where=ctx)
        gap = sb("gap", [P, NT], where=ctx)
        share = sb("share", [P, 2, NT], where=ctx)
        weight = sb("weight", [P, NT, E], where=ctx)
        weight_chunk = sb("weight_chunk", [P, G, E], where=ctx)
        weight_t = sb("weight_t", [P, CH], F32R, ctx)
        sel_f = sb("sel_f", [P, E, P], where=ctx)
        sel = sb("sel", [P, E, P], F32R, ctx)
        hid = sb("hid", [P, 2, CH], where=ctx)
        scaled = sb("scaled", [P, 2, CH], where=ctx)
        out_sb = sb("out_sb", [P, 2, CH], where=ctx)

        w1_loaded = [sem(f"w1_loaded{e}") for e in range(E)]
        w2_loaded = [sem(f"w2_loaded{e}") for e in range(E)]
        w1_high = sem("w1_high")
        w1_ready = sem("w1_ready")
        rank_made = sem("rank_made")
        rows_zeroed = sem("rows_zeroed")
        sel_steps = sem("sel_steps")
        choice = sem("choice")
        share_exp = sem("share_exp")
        weights_ready = sem("weights_ready")
        wt_staged = sem("wt_staged")
        wt_turned = sem("wt_turned")
        wt_high = sem("wt_high")
        wt_ready = sem("wt_ready")
        spread = sem("spread_done")
        hidden = sem("hidden_done")
        silu_done = sem("silu_done")
        scaled_done = sem("scaled_done")
        down_done = sem("down_done")
        out_ready = sem("out_ready")
        stored = [sem("stored0"), sem("stored1")]
        ps_h, ps_w, ps_y, ps_t = bank[0:HR], bank[HR:HR + YR], bank[6], bank[7]
        block = ctx.enter_context(nc.Block())

        @block.sync
        def _(sp):
            for e in range(E):
                sp.dma_start(w1[:, e], f_w1[:, e]).then_inc(w1_loaded[e], 16)
                sp.dma_start(w2[:, e], f_w2[:, e]).then_inc(w2_loaded[e], 16)
            for g in range(NCH):
                sp.wait_ge(out_ready, g + 1)
                sp.dma_start(out[:, g * CH:(g + 1) * CH], out_sb[:, g % 2, :]).then_inc(stored[g % 2], 16)
            for half in stored:
                sp.wait_ge(half, 16 * NCH // 2)

        @block.gpsimd
        def _(pool):
            pool.iota(rank_i[:, :], [[-1, E]], base=E, channel_multiplier=0).then_inc(rank_made, 1)
            pool.memset(f32(weight_t[:, :]), 0.0).then_inc(rows_zeroed, 1)
            pool.memset(sel_f[:, :, :], 0.0).then_inc(sel_steps, 1)
            for n, base in enumerate((0, -32)):
                pool.wait_ge(sel_steps, n + 1)
                pool.affine_select(out=sel_f[:, :, :], in_=sel_f[:, :, :], compare_op=ALU.not_equal, fill=1.0,
                                   base=base, pattern=[[-1, E], [0, P]], channel_multiplier=1).then_inc(sel_steps, 1)
            pool.wait_ge(sel_steps, 3)
            pool.tensor_copy(sel[:, :, :], sel_f[:, :, :]).then_inc(sel_steps, 1)

        @block.scalar
        def _(act):
            for e in range(E):
                act.wait_ge(w1_loaded[e], 16)
                nc.scalar.activation(w1_h[:, e], w1[:, e], ACT.Copy).then_inc(w1_high, 1)
            act.wait_ge(choice, 12)
            nc.scalar.activation(share[:, 1, :], gap[:, :], ACT.Exp).then_inc(share_exp, 1)

            def stage_weights(g):
                need(act, wt_turned, g)
                nc.scalar.activation(weight_chunk[:, :, :], weight[:, bass.ds(g * G, G), :], ACT.Copy
                                     ).then_inc(wt_staged, 1)

            def high_weights(g):
                act.wait_ge(wt_turned, g + 1)
                need(act, spread, E * g)
                nc.scalar.activation(weight_t[0:E, :], ps_t[0:E, :], ACT.Copy).then_inc(wt_high, 1)

            def silu(g, k):
                act.wait_ge(hidden, NK * g + k + 1)
                need(act, scaled_done, NK * g + k - 1)
                nc.scalar.activation(hid[:, k % 2], ps_h[k % HR][:, :], ACT.Silu).then_inc(silu_done, 1)

            def body(g, last=False):
                for k in range(NK):
                    silu(g, k)
                    if k == NK // 4 and not last:
                        stage_weights(g + 1)
                    if k == NK - 5 and not last:
                        high_weights(g + 1)

            act.wait_ge(rows_zeroed, 1)
            act.wait_ge(weights_ready, 1)
            stage_weights(0)
            high_weights(0)
            body(0)
            with act.Fori(1, NCH - 1) as g:
                body(g)
            body(NCH - 1, last=True)

        @block.vector
        def _(dve):
            wide = [P, NT, E]

            def step(ins, count):
                ins.then_inc(choice, 1)
                dve.wait_ge(choice, count)

            dve.wait_ge(rank_made, 1)
            step(nc.vector.tensor_copy(rank[:, :], rank_i[:, :]), 1)
            count = 1
            for n, src in ((0, logits), (1, other)):
                top, mark = best[:, n, :], hot[:, n]
                step(nc.vector.tensor_reduce(top, src[:, :, :], AX.X, ALU.max), count + 1)
                step(nc.vector.tensor_tensor(mark, src[:, :, :], top.unsqueeze(2).broadcast_to(wide), ALU.is_equal),
                     count + 2)
                step(nc.vector.tensor_tensor(mark, mark, rank[:, :].unsqueeze(1).broadcast_to(wide), ALU.mult),
                     count + 3)
                step(nc.vector.tensor_reduce(first[:, :], mark, AX.X, ALU.max), count + 4)
                step(nc.vector.tensor_tensor(mark, mark, first[:, :].unsqueeze(2).broadcast_to(wide), ALU.is_equal),
                     count + 5)
                count += 5
                if n == 0:
                    nc.vector.scalar_tensor_tensor(other[:, :, :], mark, NEG, logits[:, :, :], ALU.mult, ALU.add
                                                   ).then_inc(rank_made, 1)
                    dve.wait_ge(rank_made, 2)
            nc.vector.tensor_tensor(gap[:, :], best[:, 1, :], best[:, 0, :], ALU.subtract).then_inc(choice, 1)

            def low_w1(e):
                dve.wait_ge(w1_high, e + 1)
                nc.vector.tensor_tensor(w1_l[:, e], w1[:, e], f32(w1_h[:, e]), ALU.subtract).then_inc(w1_ready, 1)

            for e in range(E):
                low_w1(e)
            dve.wait_ge(share_exp, 1)
            step(nc.vector.tensor_scalar(first[:, :], share[:, 1, :], 1.0, None, ALU.add), 13)
            step(nc.vector.reciprocal(share[:, 0, :], first[:, :]), 14)
            step(nc.vector.tensor_tensor(share[:, 1, :], share[:, 1, :], share[:, 0, :], ALU.mult), 15)
            for n in range(2):
                step(nc.vector.tensor_tensor(hot[:, n], hot[:, n], share[:, n, :].unsqueeze(2).broadcast_to(wide),
                                             ALU.mult), 16 + n)
            nc.vector.tensor_tensor(weight[:, :, :], hot[:, 0], hot[:, 1], ALU.add).then_inc(weights_ready, 1)

            def low_weights(g):
                dve.wait_ge(wt_high, g + 1)
                nc.vector.tensor_tensor(weight_t[32:32 + E, :], ps_t[0:E, :], f32(weight_t[0:E, :]), ALU.subtract
                                        ).then_inc(wt_ready, 1)

            def scale(g, k):
                dve.wait_ge(silu_done, NK * g + k + 1)
                if k % FB == 0:
                    dve.wait_ge(spread, E * g + k // FB + 1)
                need(dve, down_done, NK * g + k - 1)
                nc.vector.tensor_tensor(scaled[:, k % 2], hid[:, k % 2], ps_w[k // FB % YR][:, :], ALU.mult
                                        ).then_inc(scaled_done, 1)

            def finish(g, slot, turn):
                dve.wait_ge(down_done, NK * g + NK)
                need(dve, stored[slot], 16 * turn)
                nc.vector.tensor_tensor(out_sb[:, slot], ps_y[:, :], resid[:, bass.ds(g * CH, CH)], ALU.add
                                        ).then_inc(out_ready, 1)

            def body(g, slot, turn, last=False):
                for k in range(NK):
                    scale(g, k)
                    if k == NK - 4 and not last:
                        low_weights(g + 1)
                finish(g, slot, turn)

            low_weights(0)
            body(0, 0, 0)
            body(1, 1, 0)
            with dve.Fori(1, NCH // 2 - 1) as pair:
                body(2 * pair, 0, pair)
                body(2 * pair + 1, 1, pair)
            body(NCH - 2, 0, NCH // 2 - 1)
            body(NCH - 1, 1, NCH // 2 - 1, last=True)

        @block.tensor
        def _(pe):
            def turn_weights(g):
                pe.wait_ge(wt_staged, g + 1)
                need(pe, wt_ready, g)
                for j in range(G):
                    last = pe.transpose(ps_t[0:E, j * P:(j + 1) * P], weight_chunk[:, j, :], ident[:, :])
                last.then_inc(wt_turned, 1)

            def spread_weight(g, e):
                if e == 0:
                    pe.wait_ge(wt_ready, g + 1)
                need(pe, scaled_done, NK * g + FB * (e - 1))
                pe.matmul(ps_w[e % YR][:, :], sel[:, e, :], weight_t[:, :], start=True, stop=True
                          ).then_inc(spread, 1)

            def up(g, k):
                e, f = k // FB, k % FB
                if isinstance(g, int) and g == 0 and f == 0:
                    pe.wait_ge(w1_ready, e + 1)
                need(pe, silu_done, NK * g + k - HR + 1)
                at = (slice(None), bass.ds(g * CH, CH))
                w = slice(f * P, (f + 1) * P)
                split_product(pe, ps_h[k % HR][:, :], w1_h[:, e, w], w1_l[:, e, w], z2_h[at], z2_l[at], True, True
                              ).then_inc(hidden, 1)

            def down(g, k):
                e, f = k // FB, k % FB
                if isinstance(g, int) and g == 0 and f == 0:
                    pe.wait_ge(w2_loaded[e], 16)
                if k == 0:
                    need(pe, out_ready, g)
                pe.wait_ge(scaled_done, NK * g + k + 1)
                pe.matmul(ps_y[:, :], w2[:, e, f, :], scaled[:, k % 2], start=(k == 0), stop=(k == NK - 1)
                          ).then_inc(down_done, 1)

            LEAD = 3

            def body(g, last=False):
                for k in range(NK):
                    if k + LEAD < NK:
                        if (k + LEAD) % FB == 0:
                            spread_weight(g, (k + LEAD) // FB)
                        up(g, k + LEAD)
                    elif not last:
                        if k + LEAD == NK:
                            spread_weight(g + 1, 0)
                        up(g + 1, k + LEAD - NK)
                    down(g, k)
                    if k == NK // 2 and not last:
                        turn_weights(g + 1)

            for k in range(LEAD):
                up(0, k)
            pe.wait_ge(sel_steps, 4)
            pe.wait_ge(weights_ready, 1)
            turn_weights(0)
            spread_weight(0, 0)
            body(0)
            with pe.Fori(1, NCH - 1) as g:
                body(g)
            body(NCH - 1, last=True)


def mixed_kernel(nc, x_chwn, x_cnhw, w_qkv, w_c, gamma, beta, wqs, wks, wvr, wqrT, wkretT, wout, wg, f_w1, f_w2, out):
    with ExitStack() as ctx:
        def sb(name, shape, dt=F32, where=ctx):
            return where.enter_context(nc.sbuf_tensor(name, shape, dt))

        def sem(name):
            return ctx.enter_context(nc.semaphore(name))

        bank = [ctx.enter_context(nc.psum_tensor(f"bank{i}", [P, CH], F32)) for i in range(8)]
        resid = sb("resid", [P, TOK])
        wc_h = sb("wc_h", [P, 9, P], F32R)
        wc_l = sb("wc_l", [P, 9, P], F32R)
        ident = sb("ident", [P, P])
        ones = sb("ones", [P, P])
        norm_a = sb("norm_a", [P, NI])
        norm_b = sb("norm_b", [P, NI])
        pad_h = sb("pad_h", [P, PAD * PAD * NI], F32R)
        pad_l = sb("pad_l", [P, PAD * PAD * NI], F32R)
        virt = sb("virt", [P, NI, HW, HW])

        conv_attention(nc, sb, sem, bank, pad_h, pad_l, resid, virt, ident, wc_h, wc_l, x_chwn, x_cnhw,
                       w_qkv, w_c)
        image_norm(nc, sb, sem, bank, pad_h, pad_l, virt, gamma, beta, ones, norm_a, norm_b)
        z2_h = sb("z2_h", [P, TOK], F32R)
        z2_l = sb("z2_l", [P, TOK], F32R)
        logits = sb("logits", [P, NCH * G, 8])
        token_attention(nc, sb, sem, bank, pad_h, pad_l, resid, virt, z2_h, z2_l, logits, ident, wc_h, wc_l, norm_a,
                        norm_b, wqs, wks, wvr, wqrT, wkretT, wout, wg)
        experts(nc, sb, sem, bank, resid, z2_h, z2_l, logits, ident, f_w1, f_w2, out)


_INS = ["x_chwn", "x_cnhw", "w_qkv", "w_c", "gamma", "beta", "wqs", "wks", "wvr", "wqrT", "wkretT", "wout", "wg",
        "w1", "w2"]


def kernel(x, L0_conv_Wq, L0_conv_Wk, L0_conv_Wv, L0_conv_Wc, L0_conv_gamma, L0_conv_beta, L1_attn_wq_s,
           L1_attn_wk_s, L1_attn_wv_r, L1_attn_wq_r, L1_attn_wk_ret, L1_attn_w_out, L1_ffn_Wg, L1_ffn_W1, L1_ffn_W2):
    import numpy as np
    import concourse.bacc as bacc
    from concourse.bass_utils import run_bass_kernel_spmd

    def taps(w):
        return np.asarray(w).transpose(1, 2, 3, 0).reshape(P, 9, P)

    x, w1, w2 = np.asarray(x), np.asarray(L1_ffn_W1), np.asarray(L1_ffn_W2)
    laid = [
        x.transpose(1, 2, 3, 0).reshape(P, HW, HW * NI), x.transpose(1, 0, 2, 3).reshape(P, TOK),
        np.stack([taps(w) for w in (L0_conv_Wq, L0_conv_Wk, L0_conv_Wv)], axis=1), taps(L0_conv_Wc),
        np.asarray(L0_conv_gamma).reshape(P, 1), np.asarray(L0_conv_beta).reshape(P, 1),
        np.asarray(L1_attn_wq_s), np.asarray(L1_attn_wk_s), np.asarray(L1_attn_wv_r),
        np.asarray(L1_attn_wq_r).T, np.asarray(L1_attn_wk_ret).T, np.asarray(L1_attn_w_out),
        np.asarray(L1_ffn_Wg), w1.transpose(1, 0, 2), w2.reshape(8, G, P, P).transpose(2, 0, 1, 3),
    ]
    nc = bacc.Bacc("TRN2", target_bir_lowering=False, num_devices=1)
    arrays, args = {}, []
    for name, a in zip(_INS, laid):
        arrays[f"in_{name}"] = np.ascontiguousarray(a)
        args.append(nc.dram_tensor(f"in_{name}", a.shape, mybir.dt.from_np(a.dtype), kind="ExternalInput").ap())
    args.append(nc.dram_tensor("out", (P, TOK), F32, kind="ExternalOutput").ap())
    mixed_kernel(nc, *args)
    r = run_bass_kernel_spmd(nc, [arrays], core_ids=[0])
    return np.ascontiguousarray(r.results[0]["out"].reshape(P, NI, HW, HW).transpose(1, 0, 2, 3))
```

```python
from contextlib import ExitStack

import concourse.bass as bass
from concourse import mybir

F32 = mybir.dt.float32
F32R = mybir.dt.float32r
I32 = mybir.dt.int32
U32 = mybir.dt.uint32
ALU = mybir.AluOpType
ACT = mybir.ActivationFunctionType
AX = mybir.AxisListType

P = 128
NI, HW = 16, 16
PIX = HW * HW
TOK = NI * PIX
PAD = HW + 2
CH = 512
NCH = TOK // CH
G = CH // P
TAPS = [(dy, dx) for dy in range(3) for dx in range(3)]
NEG = -1.0e30
EPS = 1e-5


def f32(ap):
    return ap.bitcast(F32)


def need(eng, semaphore, count):
    if not isinstance(count, int) or count > 0:
        eng.wait_ge(semaphore, count)


def split_product(pe, out, w_h, w_l, x_h, x_l, start, stop):
    pe.matmul(out, w_h, x_h, start=start, stop=False)
    pe.matmul(out, w_h, x_l, start=False, stop=False)
    return pe.matmul(out, w_l, x_h, start=False, stop=stop)


def conv_attention(nc, sb, sem, bank, pad_h, pad_l, resid, virt, ident, wc_h, wc_l, x_chwn, x_cnhw,
                   w_qkv, w_c):
    scale = float(P) ** -0.5
    with ExitStack() as ctx:
        x_raw = sb("x_raw", [P, HW, HW * NI], where=ctx)
        w_raw = sb("w_raw", [P, 4, 9, P], where=ctx)
        w_h = sb("w_h", [P, 3, 9, P], F32R, ctx)
        w_l = sb("w_l", [P, 3, 9, P], F32R, ctx)
        qkv = sb("qkv", [P, 3, CH], where=ctx)
        mask = sb("mask", [P, P], where=ctx)
        scores = sb("scores", [P, G, P], where=ctx)
        expd = sb("expd", [P, G, P], where=ctx)
        probs = sb("probs", [P, G, P], where=ctx)
        probs_t = sb("probs_t", [P, G, P], where=ctx)
        v_tok = sb("v_tok", [P, G, P], where=ctx)
        row_max = sb("row_max", [P, G], where=ctx)
        row_sum = sb("row_sum", [P, G], where=ctx)
        row_inv = sb("row_inv", [P, G], where=ctx)

        x_loaded = [sem(f"x_loaded{i}") for i in range(4)]
        w_loaded = [sem(f"w_loaded{i}") for i in range(4)]
        late_loaded = sem("late_loaded")
        border_zeroed = sem("border_zeroed")
        ident_zeroed = sem("ident_zeroed")
        ident_ready = sem("ident_ready")
        mask_steps = sem("mask_steps")
        x_high = sem("x_high")
        x_ready = sem("x_ready")
        w_high = sem("w_high")
        w_ready = sem("w_ready")
        conv_done = [sem(f"conv_{n}_done") for n in "qkv"]
        conv_copied = [sem(f"conv_{n}_copied") for n in "qkv"]
        a_scores = sem("a_scores")
        v_turned = sem("v_turned")
        v_tok_ready = sem("v_tok_ready")
        masked = sem("masked")
        maxed = sem("maxed")
        shifted = sem("shifted")
        a_exp = sem("a_exp")
        summed = sem("summed")
        inverted = sem("inverted")
        probs_ready = sem("probs_ready")
        probs_turned = sem("probs_turned")
        probs_t_ready = sem("probs_t_ready")
        a_out = sem("a_out")
        virt_ready = sem("virt_ready")

        ps_conv, ps_s, ps_vt, ps_pt, ps_o = bank[0:3], bank[3], bank[4], bank[5], bank[6]
        grid_h = pad_h[:, :].rearrange("p (h c) -> p h c", h=PAD)
        grid_l = pad_l[:, :].rearrange("p (h c) -> p h c", h=PAD)
        block = ctx.enter_context(nc.Block())

        @block.sync
        def _(sp):
            sp.dma_start(w_raw[:, 0], w_qkv[:, 0]).then_inc(w_loaded[0], 16)
            for i in range(4):
                sp.dma_start(x_raw[:, 4 * i:4 * i + 4], x_chwn[:, 4 * i:4 * i + 4]).then_inc(x_loaded[i], 16)
                if i == 0:
                    sp.dma_start(w_raw[:, 1], w_qkv[:, 1]).then_inc(w_loaded[1], 16)
                if i == 1:
                    sp.dma_start(w_raw[:, 2], w_qkv[:, 2]).then_inc(w_loaded[2], 16)
            sp.dma_start(w_raw[:, 3], w_c).then_inc(w_loaded[3], 16)
            sp.dma_start(resid[:, :], x_cnhw).then_inc(late_loaded, 16)
            sp.wait_ge(late_loaded, 16)

        @block.gpsimd
        def _(pool):
            for grid in (grid_h, grid_l):
                pool.memset(f32(grid[:, 0:PAD:PAD - 1, :]), 0.0).then_inc(border_zeroed, 1)
                columns = grid[:, 1:PAD - 1, :].rearrange("p h (c n) -> p h c n", n=NI)
                pool.memset(f32(columns[:, :, 0:PAD:PAD - 1, :]), 0.0).then_inc(border_zeroed, 1)
            pool.memset(ident[:, :], 0.0).then_inc(ident_zeroed, 1)
            pool.memset(mask[:, :], 0.0).then_inc(mask_steps, 1)
            pool.wait_ge(ident_zeroed, 1)
            pool.affine_select(out=ident[:, :], in_=ident[:, :], compare_op=ALU.not_equal, fill=1.0, base=0,
                               pattern=[[-1, P]], channel_multiplier=1).then_inc(ident_ready, 1)
            blocks = mask[:, :].rearrange("p (b n) -> p b n", n=NI)
            pool.wait_ge(mask_steps, 1)
            pool.affine_select(out=blocks, in_=blocks, compare_op=ALU.is_ge, fill=NEG, base=0,
                               pattern=[[-NI, P // NI], [0, NI]], channel_multiplier=1).then_inc(mask_steps, 1)
            pool.wait_ge(mask_steps, 2)
            pool.affine_select(out=blocks, in_=blocks, compare_op=ALU.is_ge, fill=NEG, base=NI - 1,
                               pattern=[[NI, P // NI], [0, NI]], channel_multiplier=-1).then_inc(mask_steps, 1)

        def rows(grid, i):
            return grid[:, 2 * i + 1:2 * i + 3, NI:NI + HW * NI]

        @block.scalar
        def _(act):
            def weight_high(n):
                act.wait_ge(w_loaded[n], 16)
                dst = w_h[:, n] if n < 3 else wc_h[:, :, :]
                nc.scalar.activation(dst, w_raw[:, n], ACT.Copy).then_inc(w_high, 1)

            def x_half(i):
                act.wait_ge(x_loaded[i // 2], 16)
                nc.scalar.activation(rows(grid_h, i), x_raw[:, 2 * i:2 * i + 2], ACT.Copy).then_inc(x_high, 1)

            weight_high(0)
            x_half(0)
            x_half(1)
            weight_high(1)
            x_half(2)
            weight_high(2)
            for i in range(3, NCH):
                x_half(i)
            weight_high(3)

            def copies(c, j):
                act.wait_ge(conv_done[j], c + 1)
                need(act, a_scores, c)
                need(act, v_turned, c)
                nc.scalar.activation(qkv[:, j, :], ps_conv[j][:, :], ACT.Copy).then_inc(conv_copied[j], 1)

            def exponent(c):
                act.wait_ge(shifted, c + 1)
                need(act, probs_ready, c)
                nc.scalar.activation(expd[:, :, :], scores[:, :, :], ACT.Exp, scale=scale).then_inc(a_exp, 1)

            def turn_probs(c):
                act.wait_ge(probs_turned, c + 1)
                need(act, a_out, c)
                nc.scalar.activation(probs_t[:, :, :], ps_pt[:, :].rearrange("p (g n) -> p g n", g=G),
                                     ACT.Copy).then_inc(probs_t_ready, 1)

            for j in range(3):
                copies(0, j)
            def step(c):
                exponent(c)
                copies(c + 1, 0)
                copies(c + 1, 1)
                turn_probs(c)
                copies(c + 1, 2)

            step(0)
            with act.Fori(1, NCH - 1) as c:
                step(c)
            exponent(NCH - 1)
            turn_probs(NCH - 1)

        @block.vector
        def _(dve):
            def weight_low(n):
                dve.wait_ge(w_high, n + 1)
                high, low = (w_h[:, n], w_l[:, n]) if n < 3 else (wc_h[:, :, :], wc_l[:, :, :])
                nc.vector.tensor_tensor(low, w_raw[:, n], f32(high), ALU.subtract).then_inc(w_ready, 1)

            def x_low(i, count=1):
                dve.wait_ge(x_high, i + 1)
                nc.vector.tensor_tensor(rows(grid_l, i), x_raw[:, 2 * i:2 * i + 2], f32(rows(grid_h, i)),
                                        ALU.subtract).then_inc(x_ready, count)

            weight_low(0)
            x_low(0)
            x_low(1)
            weight_low(1)
            x_low(2)
            weight_low(2)
            for i in range(3, NCH - 1):
                x_low(i)
            x_low(NCH - 1, 2)
            weight_low(3)
            dve.wait_ge(mask_steps, 3)

            def turn_v(c):
                dve.wait_ge(v_turned, c + 1)
                need(dve, a_out, c)
                nc.vector.tensor_copy(v_tok[:, :, :], ps_vt[:, :].rearrange("p (g n) -> p g n", g=G)
                                      ).then_inc(v_tok_ready, 1)

            def softmax(c):
                dve.wait_ge(a_scores, c + 1)
                need(dve, a_exp, c)
                nc.vector.tensor_tensor(scores[:, :, :], ps_s[:, :].rearrange("p (g n) -> p g n", g=G),
                                        mask[:, :].unsqueeze(1).broadcast_to([P, G, P]), ALU.add
                                        ).then_inc(masked, 1)
                dve.wait_ge(masked, c + 1)
                nc.vector.tensor_reduce(row_max[:, :], scores[:, :, :], AX.X, ALU.max).then_inc(maxed, 1)
                dve.wait_ge(maxed, c + 1)
                nc.vector.tensor_tensor(scores[:, :, :], scores[:, :, :],
                                        row_max[:, :].unsqueeze(2).broadcast_to([P, G, P]), ALU.subtract
                                        ).then_inc(shifted, 1)
                turn_v(c)
                dve.wait_ge(a_exp, c + 1)
                nc.vector.tensor_reduce(row_sum[:, :], expd[:, :, :], AX.X, ALU.add).then_inc(summed, 1)
                dve.wait_ge(summed, c + 1)
                nc.vector.reciprocal(row_inv[:, :], row_sum[:, :]).then_inc(inverted, 1)
                dve.wait_ge(inverted, c + 1)
                need(dve, probs_turned, c)
                nc.vector.tensor_tensor(probs[:, :, :], expd[:, :, :],
                                        row_inv[:, :].unsqueeze(2).broadcast_to([P, G, P]), ALU.mult
                                        ).then_inc(probs_ready, 1)

            def store_virt(c):
                dve.wait_ge(a_out, c + 1)
                dst = virt[:, :, bass.ds(2 * c, 2), :]
                nc.vector.tensor_copy(dst, ps_o[:, :].rearrange("p (h w n) -> p n h w", h=2, w=HW)
                                      ).then_inc(virt_ready, 1)

            softmax(0)
            store_virt(0)
            with dve.Fori(1, NCH) as c:
                softmax(c)
                store_virt(c)

        @block.tensor
        def _(pe):
            def convolve(c, j):
                pe.wait_ge(x_ready, c + 2)
                need(pe, conv_copied[j], c)
                for t, (dy, dx) in enumerate(TAPS):
                    span = slice(dx * NI, (dx + HW) * NI)
                    last = split_product(pe, ps_conv[j][:, :], w_h[:, j, t, :], w_l[:, j, t, :],
                                         grid_h[:, bass.ds(2 * c + dy, 2), span],
                                         grid_l[:, bass.ds(2 * c + dy, 2), span], t == 0, t == 8)
                last.then_inc(conv_done[j], 1)

            def score(c):
                for j in range(3):
                    pe.wait_ge(conv_copied[j], c + 1)
                need(pe, masked, c)
                for g in range(G):
                    part = slice(g * P, (g + 1) * P)
                    last = pe.matmul(ps_s[:, part], qkv[:, 0, part], qkv[:, 1, part], start=True, stop=True)
                last.then_inc(a_scores, 1)
                need(pe, v_tok_ready, c)
                for g in range(G):
                    part = slice(g * P, (g + 1) * P)
                    last = pe.transpose(ps_vt[:, part], qkv[:, 2, part], ident[:, :])
                last.then_inc(v_turned, 1)

            def turn(c):
                pe.wait_ge(probs_ready, c + 1)
                need(pe, probs_t_ready, c)
                for g in range(G):
                    last = pe.transpose(ps_pt[:, g * P:(g + 1) * P], probs[:, g, :], ident[:, :])
                last.then_inc(probs_turned, 1)

            def attend(c):
                pe.wait_ge(probs_t_ready, c + 1)
                pe.wait_ge(v_tok_ready, c + 1)
                need(pe, virt_ready, c)
                for g in range(G):
                    last = pe.matmul(ps_o[:, g * P:(g + 1) * P], v_tok[:, g, :], probs_t[:, g, :],
                                     start=True, stop=True)
                last.then_inc(a_out, 1)

            pe.wait_ge(border_zeroed, 4)
            pe.wait_ge(ident_ready, 1)
            for j in range(3):
                pe.wait_ge(w_ready, j + 1)
                convolve(0, j)

            def step(c):
                score(c)
                convolve(c + 1, 0)
                turn(c)
                convolve(c + 1, 1)
                attend(c)
                convolve(c + 1, 2)

            step(0)
            with pe.Fori(1, NCH - 1) as c:
                step(c)
            score(NCH - 1)
            turn(NCH - 1)
            attend(NCH - 1)


def image_norm(nc, sb, sem, bank, pad_h, pad_l, virt, gamma, beta, ones, norm_a, norm_b):
    with ExitStack() as ctx:
        stats = sb("stats", [P, NI, 6], where=ctx)
        chan = sb("chan", [P, NI, 2], where=ctx)
        off = sb("off", [P, NI], where=ctx)
        spread = sb("spread", [P, NI], where=ctx)
        mu = sb("mu", [P, NI], where=ctx)
        var = sb("var", [P, NI], where=ctx)
        power = sb("power", [P, NI], where=ctx)
        gb = sb("gb", [P, 2], where=ctx)

        gb_loaded = sem("gb_loaded")
        b_consts = sem("b_consts")
        border2_zeroed = sem("border2_zeroed")
        stats_done = sem("stats_done")
        chan_done = sem("chan_done")
        mean_summed = sem("mean_summed")
        b_steps = sem("b_steps")
        var_summed = sem("var_summed")
        rstd_done = sem("rstd_done")
        block = ctx.enter_context(nc.Block())

        @block.sync
        def _(sp):
            sp.dma_start(gb[:, 0:1], gamma).then_inc(gb_loaded, 16)
            sp.dma_start(gb[:, 1:2], beta).then_inc(gb_loaded, 16)

        @block.gpsimd
        def _(pool):
            pool.memset(power[:, :], -0.5).then_inc(b_consts, 1)
            pool.memset(ones[:, :], 1.0 / P).then_inc(b_consts, 1)
            for pad in (pad_h, pad_l):
                grid = pad[:, :].rearrange("p (n h w) -> p n h w", n=NI, h=PAD)
                pool.memset(f32(grid[:, :, 0:PAD:PAD - 1, :]), 0.0).then_inc(border2_zeroed, 1)
                pool.memset(f32(grid[:, :, 1:PAD - 1, 0:PAD:PAD - 1]), 0.0).then_inc(border2_zeroed, 1)
            pool.wait_ge(b_consts, 2)
            pool.wait_ge(b_steps, 4)
            pool.tensor_tensor(norm_a[:, :], var[:, :], power[:, :], ALU.pow).then_inc(rstd_done, 1)

        @block.vector
        def _(dve):
            for n in range(NI):
                nc.vector.bn_stats(stats[:, n, :], virt[:, n].rearrange("p h w -> p (h w)")).then_inc(stats_done, 1)
            dve.wait_ge(stats_done, NI)
            for n in range(NI):
                nc.vector.bn_aggr(chan[:, n, :], stats[:, n, :]).then_inc(chan_done, 1)
            dve.wait_ge(mean_summed, 1)
            nc.vector.tensor_copy(mu[:, :], bank[0][:, 0:NI]).then_inc(b_steps, 1)
            dve.wait_ge(b_steps, 1)
            nc.vector.tensor_tensor(off[:, :], chan[:, :, 0], mu[:, :], ALU.subtract).then_inc(b_steps, 1)
            dve.wait_ge(b_steps, 2)
            nc.vector.tensor_tensor(spread[:, :], off[:, :], off[:, :], ALU.mult).then_inc(b_steps, 1)
            dve.wait_ge(b_steps, 3)
            nc.vector.tensor_tensor(off[:, :], spread[:, :], chan[:, :, 1], ALU.add).then_inc(var_summed, 1)
            dve.wait_ge(var_summed, 2)
            nc.vector.tensor_scalar(var[:, :], bank[1][:, 0:NI], EPS, None, ALU.add).then_inc(b_steps, 1)
            dve.wait_ge(rstd_done, 1)
            dve.wait_ge(gb_loaded, 32)
            nc.vector.tensor_scalar(norm_a[:, :], norm_a[:, :], gb[:, 0:1], None, ALU.mult).then_inc(b_steps, 1)
            dve.wait_ge(b_steps, 5)
            nc.vector.tensor_tensor(off[:, :], mu[:, :], norm_a[:, :], ALU.mult).then_inc(b_steps, 1)
            dve.wait_ge(b_steps, 6)
            nc.vector.tensor_scalar(norm_b[:, :], off[:, :], -1.0, gb[:, 1:2], ALU.mult, ALU.add).then_inc(b_steps, 1)

        @block.tensor
        def _(pe):
            pe.wait_ge(b_consts, 2)
            pe.wait_ge(chan_done, NI)
            pe.matmul(bank[0][:, 0:NI], ones[:, :], chan[:, :, 0], start=True, stop=True).then_inc(mean_summed, 1)
            pe.wait_ge(var_summed, 1)
            pe.matmul(bank[1][:, 0:NI], ones[:, :], off[:, :], start=True, stop=True).then_inc(var_summed, 1)


def token_attention(nc, sb, sem, bank, pad_h, pad_l, resid, virt, z2_h, z2_l, logits, ident, wc_h, wc_l, norm_a,
                    norm_b, d_wqs, d_wks, d_wvr, d_wqrT, d_wkretT, d_wout, d_wg):
    S, D = 8, 16
    NP = S // 2
    NR = 160
    RV = 34
    RVW = 96
    with ExitStack() as ctx:
        t_chunk = sb("t_chunk", [P, CH], where=ctx)
        z_tok = sb("z_tok", [P, G, P], where=ctx)
        zt = sb("zt", [P, CH], where=ctx)
        zt_h = sb("zt_h", [P, CH], F32R, ctx)
        zt_l = sb("zt_l", [P, CH], F32R, ctx)
        wq = sb("wq", [P, P], where=ctx)
        wk = sb("wk", [P, P], where=ctx)
        wq_h = sb("wq_h", [P, P], F32R, ctx)
        wq_l = sb("wq_l", [P, P], F32R, ctx)
        wk_h = sb("wk_h", [P, P], F32R, ctx)
        wk_l = sb("wk_l", [P, P], F32R, ctx)
        wvr = sb("wvr", [P, 2 * D], where=ctx)
        wqr_t = sb("wqr_t", [P, P], where=ctx)
        ret_blocks = sb("ret_blocks", [P, P], where=ctx)
        w_tok = sb("w_tok", [P, NR], where=ctx)
        wout = sb("wout", [P, P], where=ctx)
        wg = sb("wg", [P, S], where=ctx)
        q_h = sb("q_h", [P, CH], F32R, ctx)
        q_l = sb("q_l", [P, CH], F32R, ctx)
        k_h = sb("k_h", [P, CH], F32R, ctx)
        k_l = sb("k_l", [P, CH], F32R, ctx)
        q_stack = sb("q_stack", [P, 2, NP, CH], F32R, ctx)
        k_stack = sb("k_stack", [P, 2, S, CH], F32R, ctx)
        one_rows = sb("one_rows", [P, 2], where=ctx)
        rvx = sb("rvx", [P, 2, G, RVW], where=ctx)
        r_query = virt[:, :].rearrange("p n h w -> p (n h w)").rearrange("p (g j f) -> p g j f", j=G, f=P)
        s_max = sb("s_max", [P, 2, S], where=ctx)
        s_neg = sb("s_neg", [P, 2, S], where=ctx)
        m_split = sb("m_split", [P, 2, NP, 32], F32R, ctx)
        expd = sb("s_expd", [P, 2, 2, PIX], where=ctx)
        ret = sb("ret", [P, 2, S, 2, RV], where=ctx)
        prod = sb("prod", [P, 2, S, D], where=ctx)
        sim = sb("sim", [P, 2, S], where=ctx)
        r_inv = sb("r_inv", [P, 2, S], where=ctx)
        r_gate = sb("r_gate", [P, 2, S], where=ctx)
        o_tok = sb("o_tok", [P, G, P], where=ctx)
        z2_tok = sb("z2_tok", [P, G, P], where=ctx)
        o_t = z2_tok[:, :, :].rearrange("p j f -> p (j f)")
        t2_chunk = sb("t2_chunk", [P, CH], where=ctx)
        z2_f = t2_chunk
        ln_stats = sb("ln_stats", [P, G, 6], where=ctx)
        ln_mv = sb("ln_mv", [P, G, 2], where=ctx)
        ln_var = sb("ln_var", [P, G], where=ctx)
        ln_rstd = sb("ln_rstd", [P, G], where=ctx)
        power = sb("ln_power", [P, G], where=ctx)

        y_done = sem("y_done")
        y_high = sem("y_high")
        y_ready = sem("y_ready")
        a_loaded = sem("a_loaded")
        blocks_zeroed = sem("blocks_zeroed")
        blocks_loaded = sem("blocks_loaded")
        c_consts = sem("c_consts")
        ones_steps = sem("ones_steps")
        stack_init = sem("stack_init")
        wa_high = sem("wa_high")
        wa_ready = sem("wa_ready")
        folded = sem("folded")
        w_tok_ready = sem("w_tok_ready")
        conv_done = sem("convc_done")
        t_ready = sem("t_ready")
        t_kept = sem("t_kept")
        t_turned = sem("t_turned")
        ln_steps = sem("ln_steps")
        ln_power = sem("ln_power_done")
        z_ready = sem("z_ready")
        z_turned = sem("z_turned")
        zt_steps = sem("zt_steps")
        zt_ready = sem("zt_ready")
        q_done = sem("q_done")
        k_done = sem("k_done")
        q_high = sem("q_high")
        k_high = sem("k_high")
        q_ready = sem("q_ready")
        k_ready = sem("k_ready")
        tok_done = sem("tok_done")
        tok_copied = sem("tok_copied")
        stacked = sem("stacked")
        s_done = sem("s_done")
        max_done = sem("max_done")
        m_steps = sem("m_steps")
        m_turned = sem("m_turned")
        m_even = sem("m_even")
        m_odd = sem("m_odd")
        st_done = sem("st_done")
        exp_done = sem("exp_done")
        pv_done = sem("pv_done")
        ret_copied = sem("ret_copied")
        ret_steps = sem("ret_steps")
        gate_exp = sem("gate_exp")
        o_turned = sem("o_turned")
        o_t_ready = sem("o_t_ready")
        out_done = sem("out_done")
        t2_ready = sem("t2_ready")
        t2_kept = sem("t2_kept")
        t2_turned = sem("t2_turned")
        z2_turned = sem("z2_turned")
        z2_steps = sem("z2_steps")
        z2_ready = sem("z2_ready")
        routed = sem("routed")
        logits_kept = sem("logits_kept")

        img_h = pad_h[:, :].rearrange("p (n h w) -> p n h w", n=NI, h=PAD)
        img_l = pad_l[:, :].rearrange("p (n h w) -> p n h w", n=NI, h=PAD)
        ps_conv, ps_s, ps_st, ps_pv, ps_x = bank[0], bank[1:3], bank[3:5], bank[5:7], bank[7]
        WLOADS = 6
        STACK = 16 * (3 * NP + 3 * S)
        RS, LS = 10, 3
        block = ctx.enter_context(nc.Block())

        def tail_norm(g):
            return 2 * g + 3 if not isinstance(g, int) or g < NCH - 2 else NCH + g

        def chunk(tensor, g):
            return tensor[:, bass.ds(g * CH, CH)]

        @block.sync
        def _(sp):
            for dst, src in ((wq, d_wqs), (wk, d_wks), (wvr, d_wvr), (wqr_t, d_wqrT), (wout, d_wout), (wg, d_wg)):
                sp.dma_start(dst[:, :], src).then_inc(a_loaded, 16)
            sp.wait_ge(blocks_zeroed, 1)
            for s in range(S):
                at = slice(s * D, (s + 1) * D)
                sp.dma_start(ret_blocks[at, at], d_wkretT).then_inc(blocks_loaded, 16)

            def stack(g, ring):
                sp.wait_ge(tok_done, 2 * g + 2)
                for p in range(NP):
                    for slot, part in enumerate((q_h, q_l, q_h)):
                        sp.dma_start(f32(q_stack[32 * slot:32 * slot + 32, ring, p]), f32(part[32 * p:32 * p + 32, :])
                                     ).then_inc(stacked, 16)
                for s in range(S):
                    for slot, part in enumerate((k_h, k_h, k_l)):
                        row = 32 * slot + D * (s % 2)
                        sp.dma_start(f32(k_stack[row:row + D, ring, s]), f32(part[D * s:D * s + D, :])
                                     ).then_inc(stacked, 16)

            sp.wait_ge(stack_init, 2 + 2 * NP)
            stack(0, 0)
            stack(1, 1)
            with sp.Fori(1, NCH // 2) as pair:
                stack(2 * pair, 0)
                stack(2 * pair + 1, 1)

        @block.gpsimd
        def _(pool):
            pool.memset(ret_blocks[:, :], 0.0).then_inc(blocks_zeroed, 1)
            pool.memset(power[:, :], -0.5).then_inc(c_consts, 1)
            pool.memset(rvx[:, :, :, 2 * D:RVW], 1.0).then_inc(c_consts, 1)
            pool.memset(f32(k_stack[:, :, :, :]), 0.0).then_inc(stack_init, 1)
            pool.memset(f32(m_split[:, :, :, :]), 0.0).then_inc(stack_init, 1)
            pool.wait_ge(blocks_zeroed, 1)
            pool.wait_ge(c_consts, 2)
            pool.wait_ge(stack_init, 2)
            pool.memset(one_rows[96:100], 1.0).then_inc(ones_steps, 1)
            pool.wait_ge(ones_steps, 1)
            pool.affine_select(out=one_rows[96:100], in_=one_rows[96:100], compare_op=ALU.is_ge, fill=0.0, base=0,
                               pattern=[[-2, 2]], channel_multiplier=1).then_inc(ones_steps, 1)
            pool.wait_ge(ones_steps, 2)
            pool.affine_select(out=one_rows[96:100], in_=one_rows[96:100], compare_op=ALU.is_ge, fill=0.0, base=1,
                               pattern=[[2, 2]], channel_multiplier=-1).then_inc(ones_steps, 1)
            pool.wait_ge(ones_steps, 3)
            for n in range(2 * NP):
                ring, p = n // NP, n % NP
                pool.tensor_copy(k_stack[96:100, ring, 2 * p:2 * p + 2, :],
                                 one_rows[96:100].unsqueeze(2).broadcast_to([4, 2, CH])).then_inc(stack_init, 1)
                pool.wait_ge(stack_init, n + 3)

            def rstd(n):
                pool.wait_ge(ln_steps, LS * n + 3)
                pool.tensor_tensor(ln_rstd[:, :], ln_var[:, :], power[:, :], ALU.pow).then_inc(ln_power, 1)

            rstd(0)
            rstd(1)
            with pool.Fori(2, 2 * NCH) as n:
                rstd(n)

        @block.scalar
        def _(act):
            def normalise(n):
                nc.scalar.activation(virt[:, n], virt[:, n], ACT.Relu, scale=norm_a[:, n:n + 1],
                                     bias=norm_b[:, n:n + 1]).then_inc(y_done, 1)

            def high(n):
                act.wait_ge(y_done, n + 1)
                nc.scalar.activation(img_h[:, n, 1:1 + HW, 1:1 + HW], virt[:, n], ACT.Copy).then_inc(y_high, 1)

            for n in range(NI):
                normalise(n)
                if n % 2:
                    high(n - 1)
                    high(n)
            act.wait_ge(a_loaded, 16 * WLOADS)
            nc.scalar.activation(wq_h[:, :], wq[:, :], ACT.Copy, scale=float(D) ** -0.5).then_inc(wa_high, 1)
            nc.scalar.activation(wk_h[:, :], wk[:, :], ACT.Copy).then_inc(wa_high, 1)

            def keep_t(g):
                act.wait_ge(t_ready, g + 1)
                nc.scalar.activation(chunk(resid, g), t_chunk[:, :], ACT.Copy).then_inc(t_kept, 1)

            def split_zt(g):
                act.wait_ge(z_turned, g + 1)
                nc.scalar.activation(zt[:, :], ps_conv[:, :], ACT.Copy).then_inc(zt_steps, 1)
                act.wait_ge(zt_steps, 2 * g + 1)
                nc.scalar.activation(zt_h[:, :], zt[:, :], ACT.Copy).then_inc(zt_steps, 1)

            def split_qk(g):
                if not (isinstance(g, int) and g == 0):
                    act.wait_ge(stacked, STACK * g)
                act.wait_ge(q_done, g + 1)
                nc.scalar.activation(q_h[:, :], ps_x[:, :], ACT.Copy).then_inc(q_high, 1)
                act.wait_ge(k_done, g + 1)
                nc.scalar.activation(k_h[:, :], ps_conv[:, :], ACT.Copy).then_inc(k_high, 1)

            def keep_tok(g, half, ring):
                act.wait_ge(tok_done, 2 * g + half + 1)
                need(act, pv_done, 2 * S * (g - 1))
                src = (ps_x, ps_conv)[half][:, 0:2 * NR].rearrange("p (j f) -> p j f", j=2)
                two = slice(2 * half, 2 * half + 2)
                nc.scalar.activation(r_query[:, g, two, :], src[:, :, 0:P], ACT.Copy).then_inc(tok_copied, 1)
                nc.scalar.activation(rvx[:, ring, two, 0:2 * D], src[:, :, P:NR], ACT.Copy).then_inc(tok_copied, 1)

            def place_max(g, b, ring):
                act.wait_ge(m_turned, 2 * g + b + 1)
                for p in (2, 3):
                    nc.scalar.activation(q_stack[96:100, ring, p, b * PIX:(b + 1) * PIX],
                                         ps_x[32 * p:32 * p + 4, 0:PIX], ACT.Copy).then_inc(m_odd, 1)

            def exponent(g, b, s):
                act.wait_ge(st_done, 2 * S * g + S * b + s + 1)
                need(act, pv_done, 2 * S * g + S * b + s - 1)
                nc.scalar.activation(expd[:, s % 2].rearrange("p a i -> p (a i)"), ps_st[s % 2][:, :], ACT.Exp
                                     ).then_inc(exp_done, 1)

            def keep_ret(g, b, half):
                act.wait_ge(pv_done, 2 * S * g + S * b + 4 * half + 4)
                need(act, ret_steps, RS * (2 * g + b - 1))
                nc.scalar.activation(ret[:, b, 4 * half:4 * half + 4].rearrange("p s i f -> p (s i f)"),
                                     ps_pv[half][:, 0:8 * RV], ACT.Copy).then_inc(ret_copied, 1)

            def gate(g, b):
                act.wait_ge(ret_steps, RS * (2 * g + b) + 4)
                nc.scalar.activation(r_gate[:, :, :], sim[:, :, :], ACT.Exp, scale=-1.0).then_inc(gate_exp, 1)

            def keep_o(g):
                act.wait_ge(o_turned, g + 1)
                nc.scalar.activation(o_t[:, :], ps_x[:, :], ACT.Copy).then_inc(o_t_ready, 1)

            def keep_t2(g):
                act.wait_ge(t2_ready, g + 1)
                nc.scalar.activation(chunk(resid, g), t2_chunk[:, :], ACT.Copy).then_inc(t2_kept, 1)

            def split_z2(g):
                act.wait_ge(z2_turned, g + 1)
                act.wait_ge(t2_kept, g + 1)
                nc.scalar.activation(z2_f[:, :], ps_x[:, :], ACT.Copy).then_inc(z2_steps, 1)
                act.wait_ge(z2_steps, 2 * g + 1)
                nc.scalar.activation(chunk(z2_h, g), z2_f[:, :], ACT.Copy).then_inc(z2_steps, 1)

            def body(g, ring, first=False, last=False):
                if not first:
                    gate(g - 1, 1)
                place_max(g, 0, ring)
                if not last:
                    keep_t(g + 2)
                for s in range(S):
                    exponent(g, 0, s)
                    if not first:
                        if s == 0:
                            keep_o(g - 1)
                        if s == 2:
                            keep_t2(g - 1)
                        if s == 5:
                            split_z2(g - 1)
                keep_ret(g, 0, 0)
                keep_ret(g, 0, 1)
                place_max(g, 1, ring)
                for s in range(S):
                    exponent(g, 1, s)
                    if s == 1:
                        gate(g, 0)
                    if not last and s == 2:
                        split_zt(g + 2)
                    if not last and s == 4:
                        split_qk(g + 2)
                    if s == 5:
                        keep_ret(g, 1, 0)
                keep_ret(g, 1, 1)
                if not last:
                    keep_tok(g + 2, 0, ring)
                    keep_tok(g + 2, 1, ring)

            act.wait_ge(y_ready, NI)
            for g in range(2):
                keep_t(g)
                split_zt(g)
                split_qk(g)
                keep_tok(g, 0, g)
                keep_tok(g, 1, g)
            body(0, 0, first=True)
            body(1, 1)
            with act.Fori(1, NCH // 2 - 1) as pair:
                body(2 * pair, 0)
                body(2 * pair + 1, 1)
            body(NCH - 2, 0, last=True)
            body(NCH - 1, 1, last=True)
            gate(NCH - 1, 1)
            keep_o(NCH - 1)
            keep_t2(NCH - 1)
            split_z2(NCH - 1)

        @block.vector
        def _(dve):
            def low(n):
                dve.wait_ge(y_high, n + 1)
                inside = img_l[:, n, 1:1 + HW, 1:1 + HW]
                nc.vector.tensor_tensor(inside, virt[:, n], f32(img_h[:, n, 1:1 + HW, 1:1 + HW]), ALU.subtract
                                        ).then_inc(y_ready, 1)

            for n in range(NI):
                low(n)
            dve.wait_ge(wa_high, 1)
            nc.vector.scalar_tensor_tensor(wq_l[:, :], wq[:, :], float(D) ** -0.5, f32(wq_h[:, :]), ALU.mult,
                                           ALU.subtract).then_inc(wa_ready, 1)
            dve.wait_ge(wa_high, 2)
            nc.vector.tensor_tensor(wk_l[:, :], wk[:, :], f32(wk_h[:, :]), ALU.subtract).then_inc(wa_ready, 1)
            nc.vector.tensor_tensor(w_tok[:, P:P + D], wvr[:, 0:D], wvr[:, D:2 * D], ALU.subtract
                                    ).then_inc(w_tok_ready, 1)
            nc.vector.tensor_copy(w_tok[:, P + D:NR], wvr[:, D:2 * D]).then_inc(w_tok_ready, 1)
            dve.wait_ge(folded, 1)
            nc.vector.tensor_scalar(w_tok[:, 0:P], ps_x[:, 0:P], float(D) ** -0.5, None, ALU.mult
                                    ).then_inc(w_tok_ready, 1)
            dve.wait_ge(c_consts, 2)

            def add_conv(g):
                dve.wait_ge(conv_done, g + 1)
                need(dve, t_kept, g)
                need(dve, t_turned, g)
                nc.vector.tensor_tensor(t_chunk[:, :], ps_conv[:, :], chunk(resid, g), ALU.add).then_inc(t_ready, 1)

            def layer_norm(n, turned, count, dst):
                dve.wait_ge(turned, count)
                for j in range(G):
                    last = nc.vector.bn_stats(ln_stats[:, j, :], ps_x[:, j * P:(j + 1) * P])
                last.then_inc(ln_steps, 1)
                dve.wait_ge(ln_steps, LS * n + 1)
                nc.vector.memset(ln_var[:, :], 0.0)
                for j in range(G):
                    last = nc.vector.bn_aggr(ln_mv[:, j, :], ln_stats[:, j, :])
                last.then_inc(ln_steps, 1)
                dve.wait_ge(ln_steps, LS * n + 2)
                nc.vector.tensor_scalar(ln_var[:, :], ln_mv[:, :, 1], EPS, None, ALU.add).then_inc(ln_steps, 1)
                dve.wait_ge(ln_power, n + 1)
                for j in range(G):
                    last = nc.vector.tensor_scalar(dst[:, j, :], ps_x[:, j * P:(j + 1) * P], ln_mv[:, j, 0:1],
                                                   ln_rstd[:, j:j + 1], ALU.subtract, ALU.mult)
                last.then_inc(z_ready, 1)

            def low_zt(g):
                dve.wait_ge(zt_steps, 2 * g + 2)
                nc.vector.tensor_tensor(zt_l[:, :], zt[:, :], f32(zt_h[:, :]), ALU.subtract).then_inc(zt_ready, 1)

            def low_qk(g):
                dve.wait_ge(q_high, g + 1)
                nc.vector.tensor_tensor(q_l[:, :], ps_x[:, :], f32(q_h[:, :]), ALU.subtract).then_inc(q_ready, 1)
                dve.wait_ge(k_high, g + 1)
                nc.vector.tensor_tensor(k_l[:, :], ps_conv[:, :], f32(k_h[:, :]), ALU.subtract).then_inc(k_ready, 1)

            def row_max(g, b, s):
                dve.wait_ge(s_done, 2 * S * g + S * b + s + 1)
                nc.vector.tensor_reduce(s_max[:, :, s], ps_s[s % 2][:, :].rearrange("p (a j) -> p a j", a=2), AX.X,
                                        ALU.max).then_inc(max_done, 1)

            def split_max(g, b, ring):
                image = 2 * g + b
                high = m_split[:, :, :, 0:4:2].rearrange("p i q a -> p (i q) a")
                low = m_split[:, :, :, 1:4:2].rearrange("p i q a -> p (i q) a")
                minus = s_neg[:, :, :].rearrange("p i (q a) -> p (i q) a", a=2)
                dve.wait_ge(max_done, S * image + S)
                nc.vector.tensor_scalar(s_neg[:, :, :], s_max[:, :, :], -1.0, None, ALU.mult).then_inc(m_steps, 1)
                dve.wait_ge(m_steps, 3 * image + 1)
                nc.vector.tensor_copy(high, minus).then_inc(m_steps, 1)
                dve.wait_ge(m_steps, 3 * image + 2)
                nc.vector.tensor_tensor(low, minus, f32(high), ALU.subtract).then_inc(m_steps, 1)
                dve.wait_ge(m_turned, image + 1)
                for p in (0, 1):
                    nc.vector.tensor_copy(q_stack[96:100, ring, p, b * PIX:(b + 1) * PIX],
                                          ps_x[32 * p:32 * p + 4, 0:PIX]).then_inc(m_even, 1)

            def retrieve(g, b):
                r = ret[:, b].rearrange("p s i f -> p i s f")
                diff, value1, total = r[:, :, :, 0:D], r[:, :, :, D:2 * D], r[:, :, :, 2 * D]
                query = r_query[:, g, 2 * b:2 * b + 2, :].rearrange("p i (s d) -> p i s d", s=S)
                base = RS * (2 * g + b)
                wide = [P, 2, S, D]
                need(dve, ret_steps, base)
                dve.wait_ge(ret_copied, 2 * (2 * g + b) + 2)
                nc.vector.reciprocal(r_inv[:, :, :], total).then_inc(ret_steps, 1)
                nc.vector.tensor_tensor(prod[:, :, :, :], diff, query, ALU.mult).then_inc(ret_steps, 1)
                dve.wait_ge(ret_steps, base + 2)
                nc.vector.tensor_reduce(sim[:, :, :], prod[:, :, :, :], AX.X, ALU.add).then_inc(ret_steps, 1)
                dve.wait_ge(ret_steps, base + 3)
                nc.vector.tensor_tensor(sim[:, :, :], sim[:, :, :], r_inv[:, :, :], ALU.mult).then_inc(ret_steps, 1)
                dve.wait_ge(gate_exp, 2 * g + b + 1)
                nc.vector.tensor_scalar(r_gate[:, :, :], r_gate[:, :, :], 1.0, None, ALU.add).then_inc(ret_steps, 1)
                dve.wait_ge(ret_steps, base + 5)
                nc.vector.reciprocal(r_gate[:, :, :], r_gate[:, :, :]).then_inc(ret_steps, 1)
                dve.wait_ge(ret_steps, base + 6)
                nc.vector.tensor_tensor(prod[:, :, :, :], diff, r_gate[:, :, :].unsqueeze(3).broadcast_to(wide),
                                        ALU.mult).then_inc(ret_steps, 1)
                dve.wait_ge(ret_steps, base + 7)
                nc.vector.tensor_tensor(prod[:, :, :, :], prod[:, :, :, :], value1, ALU.add).then_inc(ret_steps, 1)
                dve.wait_ge(ret_steps, base + 8)
                need(dve, o_turned, g)
                nc.vector.tensor_tensor(o_tok[:, 2 * b:2 * b + 2, :].rearrange("p i (s d) -> p i s d", s=S),
                                        prod[:, :, :, :], r_inv[:, :, :].unsqueeze(3).broadcast_to(wide),
                                        ALU.mult).then_inc(ret_steps, 2)

            def add_attention(g):
                dve.wait_ge(out_done, g + 1)
                nc.vector.tensor_tensor(t2_chunk[:, :], ps_x[:, :], chunk(resid, g), ALU.add).then_inc(t2_ready, 1)

            def low_z2(g):
                dve.wait_ge(z2_steps, 2 * g + 2)
                nc.vector.tensor_tensor(chunk(z2_l, g), z2_f[:, :], f32(chunk(z2_h, g)), ALU.subtract
                                        ).then_inc(z2_ready, 1)

            def keep_logits(g):
                dve.wait_ge(routed, g + 1)
                nc.vector.tensor_copy(logits[:, bass.ds(g * G, G), :],
                                      ps_x[:, 0:G * S].rearrange("p (j e) -> p j e", j=G)).then_inc(logits_kept, 1)

            def body(g, ring, first=False, last=False):
                for s in range(S):
                    row_max(g, 0, s)
                    if s == 3 and not first:
                        retrieve(g - 1, 1)
                split_max(g, 0, ring)
                for s in range(S):
                    row_max(g, 1, s)
                    if s == 0 and not last:
                        add_conv(g + 2)
                    if not first:
                        if s == 1:
                            add_attention(g - 1)
                        if s == 3:
                            layer_norm(tail_norm(g - 1), t2_turned, g, z2_tok)
                        if s == 6:
                            low_z2(g - 1)
                        if s == 7:
                            keep_logits(g - 1)
                split_max(g, 1, ring)
                if not last:
                    layer_norm(2 * g + 2, t_turned, g + 3, z_tok)
                retrieve(g, 0)
                if not last:
                    low_zt(g + 2)
                    low_qk(g + 2)

            for g in range(2):
                add_conv(g)
                layer_norm(g, t_turned, g + 1, z_tok)
                low_zt(g)
                low_qk(g)
            body(0, 0, first=True)
            body(1, 1)
            with dve.Fori(1, NCH // 2 - 1) as pair:
                body(2 * pair, 0)
                body(2 * pair + 1, 1)
            body(NCH - 2, 0, last=True)
            body(NCH - 1, 1, last=True)
            retrieve(NCH - 1, 1)
            add_attention(NCH - 1)
            layer_norm(tail_norm(NCH - 1), t2_turned, NCH, z2_tok)
            low_z2(NCH - 1)
            keep_logits(NCH - 1)

        @block.tensor
        def _(pe):
            def conv_taps(g, taps):
                if taps[0] == 0:
                    pe.wait_ge(y_ready, 2 * g + 2)
                    need(pe, tok_copied, 4 * g)
                for t in taps:
                    dy, dx = TAPS[t]
                    part = (slice(None), bass.ds(2 * g, 2), slice(dy, dy + HW), slice(dx, dx + HW))
                    last = split_product(pe, ps_conv[:, :], wc_h[:, t, :], wc_l[:, t, :], img_h[part], img_l[part],
                                         t == 0, t == 8)
                if taps[-1] == 8:
                    last.then_inc(conv_done, 1)

            def turn(dst, src, signal):
                for j in range(G):
                    last = pe.transpose(dst[:, j * P:(j + 1) * P], src[:, j * P:(j + 1) * P], ident[:, :])
                last.then_inc(signal, 1)

            def flat(t):
                return t[:, :, :].rearrange("p j f -> p (j f)")

            def head_turn(g):
                pe.wait_ge(t_ready, g + 1)
                turn(ps_x, t_chunk, t_turned)

            def head_turn_back(g, norm):
                pe.wait_ge(z_ready, norm)
                turn(ps_conv, flat(z_tok), z_turned)

            def head_project(g):
                pe.wait_ge(zt_ready, g + 1)
                split_product(pe, ps_x[:, :], wq_h[:, :], wq_l[:, :], zt_h[:, :], zt_l[:, :], True, True
                              ).then_inc(q_done, 1)
                split_product(pe, ps_conv[:, :], wk_h[:, :], wk_l[:, :], zt_h[:, :], zt_l[:, :], True, True
                              ).then_inc(k_done, 1)

            def head_tokens(g):
                for half, (ps, free) in enumerate(((ps_x, q_ready), (ps_conv, k_ready))):
                    pe.wait_ge(free, g + 1)
                    for j in range(2):
                        at = (2 * half + j) * P
                        last = pe.matmul(ps[:, j * NR:(j + 1) * NR], zt[:, at:at + P], w_tok[:, :], start=True,
                                         stop=True)
                    last.then_inc(tok_done, 1)

            def scores(g, b, s, ring):
                if s == 0 and b == 0:
                    pe.wait_ge(stacked, STACK * (g + 1))
                need(pe, max_done, 2 * S * g + S * b + s - 1)
                at = b * PIX
                for i in range(2):
                    last = pe.matmul(ps_s[s % 2][:, i * PIX:(i + 1) * PIX],
                                     q_stack[0:96, ring, s // 2, at + i * P:at + (i + 1) * P],
                                     k_stack[0:96, ring, s, at:at + PIX], start=True, stop=True)
                last.then_inc(s_done, 1)

            def turn_max(g, b, free, count):
                pe.wait_ge(m_steps, 3 * (2 * g + b) + 3)
                need(pe, free, count)
                for i in range(2):
                    src = f32(m_split[:, i].rearrange("p q c -> p (q c)"))
                    last = pe.transpose(ps_x[:, i * P:(i + 1) * P], src, ident[:, :])
                last.then_inc(m_turned, 1)

            def max_placed(image):
                pe.wait_ge(m_even, 2 * image + 2)
                pe.wait_ge(m_odd, 2 * image + 2)

            def shifted_scores(g, b, s, ring):
                if s == 0:
                    max_placed(2 * g + b)
                need(pe, exp_done, 2 * S * g + S * b + s - 1)
                at = b * PIX
                for i in range(2):
                    last = pe.matmul(ps_st[s % 2][:, i * PIX:(i + 1) * PIX],
                                     k_stack[0:100, ring, s, at + i * P:at + (i + 1) * P],
                                     q_stack[0:100, ring, s // 2, at:at + PIX], start=True, stop=True)
                last.then_inc(st_done, 1)

            def retrieve(g, b, s, ring):
                pe.wait_ge(exp_done, 2 * S * g + S * b + s + 1)
                if s % 4 == 0:
                    need(pe, ret_copied, 2 * (2 * g + b - 1) + s // 4 + 1)
                if s == 0 and b == 0:
                    pe.wait_ge(tok_copied, 4 * g + 4)
                for i in range(2):
                    at = ((s % 4) * 2 + i) * RV
                    for a in range(2):
                        last = pe.matmul(ps_pv[s // 4][:, at:at + RVW], expd[:, s % 2, a, i * P:(i + 1) * P],
                                         rvx[:, ring, 2 * b + a, :], start=(a == 0), stop=(a == 1))
                last.then_inc(pv_done, 1)

            def tail_turn(g):
                pe.wait_ge(ret_steps, RS * (2 * g + 2))
                if not (isinstance(g, int) and g == NCH - 1):
                    max_placed(2 * g + 2)
                turn(ps_x, flat(o_tok), o_turned)

            def tail_out(g):
                pe.wait_ge(o_t_ready, g + 1)
                pe.matmul(ps_x[:, :], wout[:, :], o_t[:, :], start=True, stop=True).then_inc(out_done, 1)

            def tail_turn2(g):
                pe.wait_ge(t2_ready, g + 1)
                turn(ps_x, t2_chunk, t2_turned)

            def tail_turn_back(g):
                pe.wait_ge(z_ready, tail_norm(g) + 1)
                turn(ps_x, flat(z2_tok), z2_turned)

            def tail_route(g):
                pe.wait_ge(z2_steps, 2 * g + 1)
                for j in range(G):
                    last = pe.matmul(ps_x[:, j * S:(j + 1) * S], z2_f[:, j * P:(j + 1) * P], wg[:, :], start=True,
                                     stop=True)
                last.then_inc(routed, 1)

            def body(g, ring, first=False, last=False):
                for s in range(S):
                    scores(g, 0, s, ring)
                    if not last:
                        conv_taps(g + 2, range(s, s + 1) if s < 7 else range(7, 9))
                if isinstance(g, int) and g == NCH - 1:
                    max_placed(2 * g - 1)
                    turn_max(g, 0, tok_copied, 4 * NCH)
                else:
                    turn_max(g, 0, tok_copied, 4 * g + 6)
                for s in range(S):
                    shifted_scores(g, 0, s, ring)
                    scores(g, 1, s, ring)
                    if s:
                        retrieve(g, 0, s - 1, ring)
                    if not first:
                        if s == 0:
                            tail_turn(g - 1)
                        if s == 1:
                            tail_out(g - 1)
                        if s == 2:
                            tail_turn2(g - 1)
                        if s == 5:
                            tail_turn_back(g - 1)
                        if s == 6:
                            tail_route(g - 1)
                retrieve(g, 0, S - 1, ring)
                if first:
                    turn_max(g, 1, m_odd, 2)
                else:
                    turn_max(g, 1, logits_kept, g)
                if not last:
                    max_placed(2 * g + 1)
                    head_turn(g + 2)
                for s in range(S):
                    shifted_scores(g, 1, s, ring)
                    if s:
                        retrieve(g, 1, s - 1, ring)
                    if not last and s == 2:
                        head_turn_back(g + 2, 2 * g + 3)
                    if not last and s == 4:
                        head_project(g + 2)
                retrieve(g, 1, S - 1, ring)
                if not last:
                    head_tokens(g + 2)

            pe.wait_ge(a_loaded, 16 * WLOADS)
            pe.wait_ge(blocks_loaded, 16 * S)
            pe.matmul(ps_x[:, 0:P], wqr_t[:, :], ret_blocks[:, :], start=True, stop=True).then_inc(folded, 1)
            conv_taps(0, range(9))
            pe.wait_ge(w_tok_ready, 3)
            pe.wait_ge(wa_ready, 2)
            for g in range(2):
                if g:
                    conv_taps(g, range(9))
                    pe.wait_ge(tok_copied, 4 * g)
                head_turn(g)
                head_turn_back(g, g + 1)
                head_project(g)
                head_tokens(g)
            body(0, 0, first=True)
            body(1, 1)
            with pe.Fori(1, NCH // 2 - 1) as pair:
                body(2 * pair, 0)
                body(2 * pair + 1, 1)
            body(NCH - 2, 0, last=True)
            body(NCH - 1, 1, last=True)
            tail_turn(NCH - 1)
            tail_out(NCH - 1)
            tail_turn2(NCH - 1)
            tail_turn_back(NCH - 1)
            tail_route(NCH - 1)


def experts(nc, sb, sem, bank, resid, z2_h, z2_l, logits, ident, f_w1, f_w2, out):
    E, FB = 8, 4
    NK = E * FB
    NT = NCH * G
    HR, YR = 4, 2
    with ExitStack() as ctx:
        w1 = sb("w1", [P, E, CH], where=ctx)
        w1_h = sb("w1_h", [P, E, CH], F32R, ctx)
        w1_l = sb("w1_l", [P, E, CH], F32R, ctx)
        w2 = sb("w2", [P, E, FB, P], where=ctx)
        rank_i = sb("rank_i", [P, E], I32, ctx)
        rank = sb("rank", [P, E], where=ctx)
        hot = sb("hot", [P, 2, NT, E], where=ctx)
        best = sb("best", [P, 2, NT], where=ctx)
        first = sb("first", [P, NT], where=ctx)
        other = sb("other", [P, NT, E], where=ctx)
        gap = sb("gap", [P, NT], where=ctx)
        share = sb("share", [P, 2, NT], where=ctx)
        weight = sb("weight", [P, NT, E], where=ctx)
        weight_chunk = sb("weight_chunk", [P, G, E], where=ctx)
        weight_t = sb("weight_t", [P, CH], F32R, ctx)
        sel_f = sb("sel_f", [P, E, P], where=ctx)
        sel = sb("sel", [P, E, P], F32R, ctx)
        hid = sb("hid", [P, 2, CH], where=ctx)
        scaled = sb("scaled", [P, 2, CH], where=ctx)
        out_sb = sb("out_sb", [P, 2, CH], where=ctx)

        w1_loaded = [sem(f"w1_loaded{e}") for e in range(E)]
        w2_loaded = [sem(f"w2_loaded{e}") for e in range(E)]
        w1_high = sem("w1_high")
        w1_ready = sem("w1_ready")
        rank_made = sem("rank_made")
        rows_zeroed = sem("rows_zeroed")
        sel_steps = sem("sel_steps")
        choice = sem("choice")
        share_exp = sem("share_exp")
        weights_ready = sem("weights_ready")
        wt_staged = sem("wt_staged")
        wt_turned = sem("wt_turned")
        wt_high = sem("wt_high")
        wt_ready = sem("wt_ready")
        spread = sem("spread_done")
        hidden = sem("hidden_done")
        silu_done = sem("silu_done")
        scaled_done = sem("scaled_done")
        down_done = sem("down_done")
        out_ready = sem("out_ready")
        stored = [sem("stored0"), sem("stored1")]
        ps_h, ps_w, ps_y, ps_t = bank[0:HR], bank[HR:HR + YR], bank[6], bank[7]
        block = ctx.enter_context(nc.Block())

        @block.sync
        def _(sp):
            for e in range(E):
                sp.dma_start(w1[:, e], f_w1[:, e]).then_inc(w1_loaded[e], 16)
                sp.dma_start(w2[:, e], f_w2[:, e]).then_inc(w2_loaded[e], 16)
            for g in range(NCH):
                sp.wait_ge(out_ready, g + 1)
                sp.dma_start(out[:, g * CH:(g + 1) * CH], out_sb[:, g % 2, :]).then_inc(stored[g % 2], 16)
            for half in stored:
                sp.wait_ge(half, 16 * NCH // 2)

        @block.gpsimd
        def _(pool):
            pool.iota(rank_i[:, :], [[-1, E]], base=E, channel_multiplier=0).then_inc(rank_made, 1)
            pool.memset(f32(weight_t[:, :]), 0.0).then_inc(rows_zeroed, 1)
            pool.memset(sel_f[:, :, :], 0.0).then_inc(sel_steps, 1)
            for n, base in enumerate((0, -32)):
                pool.wait_ge(sel_steps, n + 1)
                pool.affine_select(out=sel_f[:, :, :], in_=sel_f[:, :, :], compare_op=ALU.not_equal, fill=1.0,
                                   base=base, pattern=[[-1, E], [0, P]], channel_multiplier=1).then_inc(sel_steps, 1)
            pool.wait_ge(sel_steps, 3)
            pool.tensor_copy(sel[:, :, :], sel_f[:, :, :]).then_inc(sel_steps, 1)

        @block.scalar
        def _(act):
            for e in range(E):
                act.wait_ge(w1_loaded[e], 16)
                nc.scalar.activation(w1_h[:, e], w1[:, e], ACT.Copy).then_inc(w1_high, 1)
            act.wait_ge(choice, 12)
            nc.scalar.activation(share[:, 1, :], gap[:, :], ACT.Exp).then_inc(share_exp, 1)

            def stage_weights(g):
                need(act, wt_turned, g)
                nc.scalar.activation(weight_chunk[:, :, :], weight[:, bass.ds(g * G, G), :], ACT.Copy
                                     ).then_inc(wt_staged, 1)

            def high_weights(g):
                act.wait_ge(wt_turned, g + 1)
                need(act, spread, E * g)
                nc.scalar.activation(weight_t[0:E, :], ps_t[0:E, :], ACT.Copy).then_inc(wt_high, 1)

            def silu(g, k):
                act.wait_ge(hidden, NK * g + k + 1)
                need(act, scaled_done, NK * g + k - 1)
                nc.scalar.activation(hid[:, k % 2], ps_h[k % HR][:, :], ACT.Silu).then_inc(silu_done, 1)

            def body(g, last=False):
                for k in range(NK):
                    silu(g, k)
                    if k == NK // 4 and not last:
                        stage_weights(g + 1)
                    if k == NK - 5 and not last:
                        high_weights(g + 1)

            act.wait_ge(rows_zeroed, 1)
            act.wait_ge(weights_ready, 1)
            stage_weights(0)
            high_weights(0)
            body(0)
            with act.Fori(1, NCH - 1) as g:
                body(g)
            body(NCH - 1, last=True)

        @block.vector
        def _(dve):
            wide = [P, NT, E]

            def step(ins, count):
                ins.then_inc(choice, 1)
                dve.wait_ge(choice, count)

            dve.wait_ge(rank_made, 1)
            step(nc.vector.tensor_copy(rank[:, :], rank_i[:, :]), 1)
            count = 1
            for n, src in ((0, logits), (1, other)):
                top, mark = best[:, n, :], hot[:, n]
                step(nc.vector.tensor_reduce(top, src[:, :, :], AX.X, ALU.max), count + 1)
                step(nc.vector.tensor_tensor(mark, src[:, :, :], top.unsqueeze(2).broadcast_to(wide), ALU.is_equal),
                     count + 2)
                step(nc.vector.tensor_tensor(mark, mark, rank[:, :].unsqueeze(1).broadcast_to(wide), ALU.mult),
                     count + 3)
                step(nc.vector.tensor_reduce(first[:, :], mark, AX.X, ALU.max), count + 4)
                step(nc.vector.tensor_tensor(mark, mark, first[:, :].unsqueeze(2).broadcast_to(wide), ALU.is_equal),
                     count + 5)
                count += 5
                if n == 0:
                    nc.vector.scalar_tensor_tensor(other[:, :, :], mark, NEG, logits[:, :, :], ALU.mult, ALU.add
                                                   ).then_inc(rank_made, 1)
                    dve.wait_ge(rank_made, 2)
            nc.vector.tensor_tensor(gap[:, :], best[:, 1, :], best[:, 0, :], ALU.subtract).then_inc(choice, 1)

            def low_w1(e):
                dve.wait_ge(w1_high, e + 1)
                nc.vector.tensor_tensor(w1_l[:, e], w1[:, e], f32(w1_h[:, e]), ALU.subtract).then_inc(w1_ready, 1)

            for e in range(E):
                low_w1(e)
            dve.wait_ge(share_exp, 1)
            step(nc.vector.tensor_scalar(first[:, :], share[:, 1, :], 1.0, None, ALU.add), 13)
            step(nc.vector.reciprocal(share[:, 0, :], first[:, :]), 14)
            step(nc.vector.tensor_tensor(share[:, 1, :], share[:, 1, :], share[:, 0, :], ALU.mult), 15)
            for n in range(2):
                step(nc.vector.tensor_tensor(hot[:, n], hot[:, n], share[:, n, :].unsqueeze(2).broadcast_to(wide),
                                             ALU.mult), 16 + n)
            nc.vector.tensor_tensor(weight[:, :, :], hot[:, 0], hot[:, 1], ALU.add).then_inc(weights_ready, 1)

            def low_weights(g):
                dve.wait_ge(wt_high, g + 1)
                nc.vector.tensor_tensor(weight_t[32:32 + E, :], ps_t[0:E, :], f32(weight_t[0:E, :]), ALU.subtract
                                        ).then_inc(wt_ready, 1)

            def scale(g, k):
                dve.wait_ge(silu_done, NK * g + k + 1)
                if k % FB == 0:
                    dve.wait_ge(spread, E * g + k // FB + 1)
                need(dve, down_done, NK * g + k - 1)
                nc.vector.tensor_tensor(scaled[:, k % 2], hid[:, k % 2], ps_w[k // FB % YR][:, :], ALU.mult
                                        ).then_inc(scaled_done, 1)

            def finish(g, slot, turn):
                dve.wait_ge(down_done, NK * g + NK)
                need(dve, stored[slot], 16 * turn)
                nc.vector.tensor_tensor(out_sb[:, slot], ps_y[:, :], resid[:, bass.ds(g * CH, CH)], ALU.add
                                        ).then_inc(out_ready, 1)

            def body(g, slot, turn, last=False):
                for k in range(NK):
                    scale(g, k)
                    if k == NK - 4 and not last:
                        low_weights(g + 1)
                finish(g, slot, turn)

            low_weights(0)
            body(0, 0, 0)
            body(1, 1, 0)
            with dve.Fori(1, NCH // 2 - 1) as pair:
                body(2 * pair, 0, pair)
                body(2 * pair + 1, 1, pair)
            body(NCH - 2, 0, NCH // 2 - 1)
            body(NCH - 1, 1, NCH // 2 - 1, last=True)

        @block.tensor
        def _(pe):
            def turn_weights(g):
                pe.wait_ge(wt_staged, g + 1)
                need(pe, wt_ready, g)
                for j in range(G):
                    last = pe.transpose(ps_t[0:E, j * P:(j + 1) * P], weight_chunk[:, j, :], ident[:, :])
                last.then_inc(wt_turned, 1)

            def spread_weight(g, e):
                if e == 0:
                    pe.wait_ge(wt_ready, g + 1)
                need(pe, scaled_done, NK * g + FB * (e - 1))
                pe.matmul(ps_w[e % YR][:, :], sel[:, e, :], weight_t[:, :], start=True, stop=True
                          ).then_inc(spread, 1)

            def up(g, k):
                e, f = k // FB, k % FB
                if isinstance(g, int) and g == 0 and f == 0:
                    pe.wait_ge(w1_ready, e + 1)
                need(pe, silu_done, NK * g + k - HR + 1)
                at = (slice(None), bass.ds(g * CH, CH))
                w = slice(f * P, (f + 1) * P)
                split_product(pe, ps_h[k % HR][:, :], w1_h[:, e, w], w1_l[:, e, w], z2_h[at], z2_l[at], True, True
                              ).then_inc(hidden, 1)

            def down(g, k):
                e, f = k // FB, k % FB
                if isinstance(g, int) and g == 0 and f == 0:
                    pe.wait_ge(w2_loaded[e], 16)
                if k == 0:
                    need(pe, out_ready, g)
                pe.wait_ge(scaled_done, NK * g + k + 1)
                pe.matmul(ps_y[:, :], w2[:, e, f, :], scaled[:, k % 2], start=(k == 0), stop=(k == NK - 1)
                          ).then_inc(down_done, 1)

            LEAD = 3

            def body(g, last=False):
                for k in range(NK):
                    if k + LEAD < NK:
                        if (k + LEAD) % FB == 0:
                            spread_weight(g, (k + LEAD) // FB)
                        up(g, k + LEAD)
                    elif not last:
                        if k + LEAD == NK:
                            spread_weight(g + 1, 0)
                        up(g + 1, k + LEAD - NK)
                    down(g, k)
                    if k == NK // 2 and not last:
                        turn_weights(g + 1)

            for k in range(LEAD):
                up(0, k)
            pe.wait_ge(sel_steps, 4)
            pe.wait_ge(weights_ready, 1)
            turn_weights(0)
            spread_weight(0, 0)
            body(0)
            with pe.Fori(1, NCH - 1) as g:
                body(g)
            body(NCH - 1, last=True)


def mixed_kernel(nc, x_chwn, x_cnhw, w_qkv, w_c, gamma, beta, wqs, wks, wvr, wqrT, wkretT, wout, wg, f_w1, f_w2, out):
    with ExitStack() as ctx:
        def sb(name, shape, dt=F32, where=ctx):
            return where.enter_context(nc.sbuf_tensor(name, shape, dt))

        def sem(name):
            return ctx.enter_context(nc.semaphore(name))

        bank = [ctx.enter_context(nc.psum_tensor(f"bank{i}", [P, CH], F32)) for i in range(8)]
        resid = sb("resid", [P, TOK])
        wc_h = sb("wc_h", [P, 9, P], F32R)
        wc_l = sb("wc_l", [P, 9, P], F32R)
        ident = sb("ident", [P, P])
        ones = sb("ones", [P, P])
        norm_a = sb("norm_a", [P, NI])
        norm_b = sb("norm_b", [P, NI])
        pad_h = sb("pad_h", [P, PAD * PAD * NI], F32R)
        pad_l = sb("pad_l", [P, PAD * PAD * NI], F32R)
        virt = sb("virt", [P, NI, HW, HW])

        conv_attention(nc, sb, sem, bank, pad_h, pad_l, resid, virt, ident, wc_h, wc_l, x_chwn, x_cnhw,
                       w_qkv, w_c)
        image_norm(nc, sb, sem, bank, pad_h, pad_l, virt, gamma, beta, ones, norm_a, norm_b)
        z2_h = sb("z2_h", [P, TOK], F32R)
        z2_l = sb("z2_l", [P, TOK], F32R)
        logits = sb("logits", [P, NCH * G, 8])
        token_attention(nc, sb, sem, bank, pad_h, pad_l, resid, virt, z2_h, z2_l, logits, ident, wc_h, wc_l, norm_a,
                        norm_b, wqs, wks, wvr, wqrT, wkretT, wout, wg)
        experts(nc, sb, sem, bank, resid, z2_h, z2_l, logits, ident, f_w1, f_w2, out)


_INS = ["x_chwn", "x_cnhw", "w_qkv", "w_c", "gamma", "beta", "wqs", "wks", "wvr", "wqrT", "wkretT", "wout", "wg",
        "w1", "w2"]


def kernel(x, L0_conv_Wq, L0_conv_Wk, L0_conv_Wv, L0_conv_Wc, L0_conv_gamma, L0_conv_beta, L1_attn_wq_s,
           L1_attn_wk_s, L1_attn_wv_r, L1_attn_wq_r, L1_attn_wk_ret, L1_attn_w_out, L1_ffn_Wg, L1_ffn_W1, L1_ffn_W2):
    import numpy as np
    import concourse.bacc as bacc
    from concourse.bass_utils import run_bass_kernel_spmd

    def taps(w):
        return np.asarray(w).transpose(1, 2, 3, 0).reshape(P, 9, P)

    x, w1, w2 = np.asarray(x), np.asarray(L1_ffn_W1), np.asarray(L1_ffn_W2)
    laid = [
        x.transpose(1, 2, 3, 0).reshape(P, HW, HW * NI), x.transpose(1, 0, 2, 3).reshape(P, TOK),
        np.stack([taps(w) for w in (L0_conv_Wq, L0_conv_Wk, L0_conv_Wv)], axis=1), taps(L0_conv_Wc),
        np.asarray(L0_conv_gamma).reshape(P, 1), np.asarray(L0_conv_beta).reshape(P, 1),
        np.asarray(L1_attn_wq_s), np.asarray(L1_attn_wk_s), np.asarray(L1_attn_wv_r),
        np.asarray(L1_attn_wq_r).T, np.asarray(L1_attn_wk_ret).T, np.asarray(L1_attn_w_out),
        np.asarray(L1_ffn_Wg), w1.transpose(1, 0, 2), w2.reshape(8, G, P, P).transpose(2, 0, 1, 3),
    ]
    nc = bacc.Bacc("TRN2", target_bir_lowering=False, num_devices=1)
    arrays, args = {}, []
    for name, a in zip(_INS, laid):
        arrays[f"in_{name}"] = np.ascontiguousarray(a)
        args.append(nc.dram_tensor(f"in_{name}", a.shape, mybir.dt.from_np(a.dtype), kind="ExternalInput").ap())
    args.append(nc.dram_tensor("out", (P, TOK), F32, kind="ExternalOutput").ap())
    mixed_kernel(nc, *args)
    r = run_bass_kernel_spmd(nc, [arrays], core_ids=[0])
    return np.ascontiguousarray(r.results[0]["out"].reshape(P, NI, HW, HW).transpose(1, 0, 2, 3))
```

```python
from contextlib import ExitStack

import concourse.bass as bass
from concourse import mybir

F32 = mybir.dt.float32
F32R = mybir.dt.float32r
I32 = mybir.dt.int32
ALU = mybir.AluOpType
ACT = mybir.ActivationFunctionType
AX = mybir.AxisListType

P = 128
NI, HW = 16, 16
PIX = HW * HW
TOK = NI * PIX
PAD = HW + 2
CH = 512
NCH = TOK // CH
G = CH // P
TAPS = [(dy, dx) for dy in range(3) for dx in range(3)]
NEG = -1.0e30
EPS = 1e-5


def f32(ap):
    return ap.bitcast(F32)


def need(eng, semaphore, count):
    if not isinstance(count, int) or count > 0:
        eng.wait_ge(semaphore, count)


def split_product(pe, out, w_h, w_l, x_h, x_l, start, stop):
    pe.matmul(out, w_h, x_h, start=start, stop=False)
    pe.matmul(out, w_h, x_l, start=False, stop=False)
    return pe.matmul(out, w_l, x_h, start=False, stop=stop)


def conv_attention(nc, sb, sem, bank, pad_h, pad_l, resid, virt, ident, wc_h, wc_l, x_chwn, x_cnhw,
                   w_qkv, w_c, stats, ones, power, ret_blocks, late_loads, d_wkretT):
    scale = float(P) ** -0.5
    with ExitStack() as ctx:
        x_raw = sb("x_raw", [P, HW, HW * NI], where=ctx)
        w_raw = sb("w_raw", [P, 4, 9, P], where=ctx)
        w_h = sb("w_h", [P, 3, 9, P], F32R, ctx)
        w_l = sb("w_l", [P, 3, 9, P], F32R, ctx)
        qkv = sb("qkv", [P, 3, CH], where=ctx)
        mask = sb("mask", [P, P], where=ctx)
        scores = sb("scores", [P, G, P], where=ctx)
        expd = sb("expd", [P, G, P], where=ctx)
        probs = sb("probs", [P, G, P], where=ctx)
        probs_t = sb("probs_t", [P, G, P], where=ctx)
        v_tok = sb("v_tok", [P, G, P], where=ctx)
        row_max = sb("row_max", [P, G], where=ctx)
        row_sum = sb("row_sum", [P, G], where=ctx)
        row_inv = sb("row_inv", [P, G], where=ctx)

        x_loaded = [sem(f"x_loaded{i}") for i in range(4)]
        pieces = [(0, slice(0, 3)), (0, slice(3, 9)), (1, slice(0, 9)), (2, slice(0, 9)), (3, slice(0, 9))]
        w_loaded = [sem(f"w_loaded{i}") for i in range(len(pieces))]
        late_loaded = sem("late_loaded")
        border_zeroed = sem("border_zeroed")
        blocks_zeroed = sem("blocks_zeroed")
        ident_zeroed = sem("ident_zeroed")
        ident_ready = sem("ident_ready")
        mask_steps = sem("mask_steps")
        x_high = sem("x_high")
        x_ready = sem("x_ready")
        w_high = sem("w_high")
        w_ready = sem("w_ready")
        conv_done = [sem(f"conv_{n}_done") for n in "qkv"]
        conv_copied = [sem(f"conv_{n}_copied") for n in "qkv"]
        a_scores = sem("a_scores")
        v_turned = sem("v_turned")
        v_tok_ready = sem("v_tok_ready")
        masked = sem("masked")
        maxed = sem("maxed")
        shifted = sem("shifted")
        a_exp = sem("a_exp")
        summed = sem("summed")
        inverted = sem("inverted")
        probs_ready = sem("probs_ready")
        probs_turned = sem("probs_turned")
        probs_t_ready = sem("probs_t_ready")
        a_out = sem("a_out")
        virt_ready = sem("virt_ready")

        ps_conv, ps_s, ps_vt, ps_pt, ps_o = bank[0:3], bank[3], bank[4], bank[5], bank[6]
        grid_h = pad_h[:, :].rearrange("p (h c) -> p h c", h=PAD)
        grid_l = pad_l[:, :].rearrange("p (h c) -> p h c", h=PAD)
        block = ctx.enter_context(nc.Block())

        @block.sync
        def _(sp):
            def load_weights(piece):
                n, taps = pieces[piece]
                src = w_qkv[:, n, taps] if n < 3 else w_c
                sp.dma_start(w_raw[:, n, taps], src).then_inc(w_loaded[piece], 16)

            load_weights(0)
            for i in range(4):
                sp.dma_start(x_raw[:, 4 * i:4 * i + 4], x_chwn[:, 4 * i:4 * i + 4]).then_inc(x_loaded[i], 16)
                if i < 3:
                    load_weights(i + 1)
            load_weights(4)
            sp.dma_start(resid[:, :], x_cnhw).then_inc(late_loaded, 16)
            for dst, src in late_loads:
                sp.dma_start(dst, src).then_inc(late_loaded, 16)
            sp.wait_ge(blocks_zeroed, 1)
            for row in range(0, P, 16):
                sp.dma_start(ret_blocks[row:row + 16, row:row + 16], d_wkretT).then_inc(late_loaded, 16)
            sp.wait_ge(late_loaded, 16 * (1 + len(late_loads) + 8))

        @block.gpsimd
        def _(pool):
            for grid in (grid_h, grid_l):
                pool.memset(f32(grid[:, 0:PAD:PAD - 1, :]), 0.0).then_inc(border_zeroed, 1)
                columns = grid[:, 1:PAD - 1, :].rearrange("p h (c n) -> p h c n", n=NI)
                pool.memset(f32(columns[:, :, 0:PAD:PAD - 1, :]), 0.0).then_inc(border_zeroed, 1)
            pool.memset(ident[:, :], 0.0).then_inc(ident_zeroed, 1)
            pool.memset(ret_blocks[:, :], 0.0).then_inc(blocks_zeroed, 1)
            pool.memset(power[:, :], -0.5)
            pool.memset(ones[:, :], 1.0 / P)
            pool.memset(mask[:, :], 0.0).then_inc(mask_steps, 1)
            pool.wait_ge(ident_zeroed, 1)
            pool.affine_select(out=ident[:, :], in_=ident[:, :], compare_op=ALU.not_equal, fill=1.0, base=0,
                               pattern=[[-1, P]], channel_multiplier=1).then_inc(ident_ready, 1)
            blocks = mask[:, :].rearrange("p (b n) -> p b n", n=NI)
            pool.wait_ge(mask_steps, 1)
            pool.affine_select(out=blocks, in_=blocks, compare_op=ALU.is_ge, fill=NEG, base=0,
                               pattern=[[-NI, P // NI], [0, NI]], channel_multiplier=1).then_inc(mask_steps, 1)
            pool.wait_ge(mask_steps, 2)
            pool.affine_select(out=blocks, in_=blocks, compare_op=ALU.is_ge, fill=NEG, base=NI - 1,
                               pattern=[[NI, P // NI], [0, NI]], channel_multiplier=-1).then_inc(mask_steps, 1)

        def rows(grid, i):
            return grid[:, 2 * i + 1:2 * i + 3, NI:NI + HW * NI]

        @block.scalar
        def _(act):
            def weight_high(piece):
                n, taps = pieces[piece]
                act.wait_ge(w_loaded[piece], 16)
                dst = w_h[:, n, taps] if n < 3 else wc_h[:, :, :]
                nc.scalar.activation(dst, w_raw[:, n, taps], ACT.Copy).then_inc(w_high, 1)

            def x_half(i):
                act.wait_ge(x_loaded[i // 2], 16)
                nc.scalar.activation(rows(grid_h, i), x_raw[:, 2 * i:2 * i + 2], ACT.Copy).then_inc(x_high, 1)

            weight_high(0)
            x_half(0)
            x_half(1)
            weight_high(1)
            weight_high(2)
            x_half(2)
            weight_high(3)
            for i in range(3, NCH):
                x_half(i)
            weight_high(4)

            def copies(c, j):
                act.wait_ge(conv_done[j], c + 1)
                need(act, a_scores, c)
                need(act, v_turned, c)
                nc.scalar.activation(qkv[:, j, :], ps_conv[j][:, :], ACT.Copy).then_inc(conv_copied[j], 1)

            def exponent(c):
                act.wait_ge(shifted, c + 1)
                need(act, probs_ready, c)
                nc.scalar.activation(expd[:, :, :], scores[:, :, :], ACT.Exp, scale=scale).then_inc(a_exp, 1)

            def turn_probs(c):
                act.wait_ge(probs_turned, c + 1)
                need(act, a_out, c)
                nc.scalar.activation(probs_t[:, :, :], ps_pt[:, :].rearrange("p (g n) -> p g n", g=G),
                                     ACT.Copy).then_inc(probs_t_ready, 1)

            for j in range(3):
                copies(0, j)
            def step(c):
                exponent(c)
                copies(c + 1, 0)
                turn_probs(c)
                copies(c + 1, 1)
                copies(c + 1, 2)

            step(0)
            with act.Fori(1, NCH - 1) as c:
                step(c)
            exponent(NCH - 1)
            turn_probs(NCH - 1)

        @block.vector
        def _(dve):
            def weight_low(piece):
                n, taps = pieces[piece]
                dve.wait_ge(w_high, piece + 1)
                high, low = (w_h[:, n, taps], w_l[:, n, taps]) if n < 3 else (wc_h[:, :, :], wc_l[:, :, :])
                nc.vector.tensor_tensor(low, w_raw[:, n, taps], f32(high), ALU.subtract).then_inc(w_ready, 1)

            def x_low(i, count=1):
                dve.wait_ge(x_high, i + 1)
                nc.vector.tensor_tensor(rows(grid_l, i), x_raw[:, 2 * i:2 * i + 2], f32(rows(grid_h, i)),
                                        ALU.subtract).then_inc(x_ready, count)

            weight_low(0)
            x_low(0)
            x_low(1)
            weight_low(1)
            weight_low(2)
            x_low(2)
            weight_low(3)
            for i in range(3, NCH - 1):
                x_low(i)
            x_low(NCH - 1, 2)
            weight_low(4)
            dve.wait_ge(mask_steps, 3)

            def turn_v(c):
                dve.wait_ge(v_turned, c + 1)
                need(dve, a_out, c)
                nc.vector.tensor_copy(v_tok[:, :, :], ps_vt[:, :].rearrange("p (g n) -> p g n", g=G)
                                      ).then_inc(v_tok_ready, 1)

            def softmax(c):
                dve.wait_ge(a_scores, c + 1)
                need(dve, a_exp, c)
                nc.vector.tensor_tensor(scores[:, :, :], ps_s[:, :].rearrange("p (g n) -> p g n", g=G),
                                        mask[:, :].unsqueeze(1).broadcast_to([P, G, P]), ALU.add
                                        ).then_inc(masked, 1)
                dve.wait_ge(masked, c + 1)
                nc.vector.tensor_reduce(row_max[:, :], scores[:, :, :], AX.X, ALU.max).then_inc(maxed, 1)
                dve.wait_ge(maxed, c + 1)
                nc.vector.tensor_tensor(scores[:, :, :], scores[:, :, :],
                                        row_max[:, :].unsqueeze(2).broadcast_to([P, G, P]), ALU.subtract
                                        ).then_inc(shifted, 1)
                turn_v(c)
                dve.wait_ge(a_exp, c + 1)
                nc.vector.tensor_reduce(row_sum[:, :], expd[:, :, :], AX.X, ALU.add).then_inc(summed, 1)
                dve.wait_ge(summed, c + 1)
                nc.vector.reciprocal(row_inv[:, :], row_sum[:, :]).then_inc(inverted, 1)
                dve.wait_ge(inverted, c + 1)
                need(dve, probs_turned, c)
                nc.vector.tensor_tensor(probs[:, :, :], expd[:, :, :],
                                        row_inv[:, :].unsqueeze(2).broadcast_to([P, G, P]), ALU.mult
                                        ).then_inc(probs_ready, 1)

            def store_virt(c):
                dve.wait_ge(a_out, c + 1)
                dst = virt[:, :, bass.ds(2 * c, 2), :]
                nc.vector.tensor_copy(dst, ps_o[:, :].rearrange("p (h w n) -> p n h w", h=2, w=HW)
                                      ).then_inc(virt_ready, 1)
                dve.wait_ge(virt_ready, c + 1)
                for n in range(NI):
                    nc.vector.bn_stats(stats[:, n, bass.ds(c, 1)].rearrange("p c s -> p (c s)"),
                                       virt[:, n, bass.ds(2 * c, 2)].rearrange("p h w -> p (h w)"))

            softmax(0)
            store_virt(0)
            with dve.Fori(1, NCH) as c:
                softmax(c)
                store_virt(c)

        @block.tensor
        def _(pe):
            def convolve(c, j):
                pe.wait_ge(x_ready, c + 2)
                need(pe, conv_copied[j], c)
                for t, (dy, dx) in enumerate(TAPS):
                    if isinstance(c, int) and c == 0 and t == 3 * (j == 0):
                        pe.wait_ge(w_ready, j + 2)
                    span = slice(dx * NI, (dx + HW) * NI)
                    last = split_product(pe, ps_conv[j][:, :], w_h[:, j, t, :], w_l[:, j, t, :],
                                         grid_h[:, bass.ds(2 * c + dy, 2), span],
                                         grid_l[:, bass.ds(2 * c + dy, 2), span], t == 0, t == 8)
                last.then_inc(conv_done[j], 1)

            def score(c):
                pe.wait_ge(conv_copied[0], c + 1)
                pe.wait_ge(conv_copied[1], c + 1)
                need(pe, masked, c)
                for g in range(G):
                    part = slice(g * P, (g + 1) * P)
                    last = pe.matmul(ps_s[:, part], qkv[:, 0, part], qkv[:, 1, part], start=True, stop=True)
                last.then_inc(a_scores, 1)
                pe.wait_ge(conv_copied[2], c + 1)
                need(pe, v_tok_ready, c)
                for g in range(G):
                    part = slice(g * P, (g + 1) * P)
                    last = pe.transpose(ps_vt[:, part], qkv[:, 2, part], ident[:, :])
                last.then_inc(v_turned, 1)

            def turn(c):
                pe.wait_ge(probs_ready, c + 1)
                need(pe, probs_t_ready, c)
                for g in range(G):
                    last = pe.transpose(ps_pt[:, g * P:(g + 1) * P], probs[:, g, :], ident[:, :])
                last.then_inc(probs_turned, 1)

            def attend(c):
                pe.wait_ge(probs_t_ready, c + 1)
                pe.wait_ge(v_tok_ready, c + 1)
                need(pe, virt_ready, c)
                for g in range(G):
                    last = pe.matmul(ps_o[:, g * P:(g + 1) * P], v_tok[:, g, :], probs_t[:, g, :],
                                     start=True, stop=True)
                last.then_inc(a_out, 1)

            pe.wait_ge(border_zeroed, 4)
            pe.wait_ge(ident_ready, 1)
            pe.wait_ge(w_ready, 1)
            for j in range(3):
                convolve(0, j)

            def step(c):
                score(c)
                convolve(c + 1, 0)
                turn(c)
                convolve(c + 1, 1)
                attend(c)
                convolve(c + 1, 2)

            step(0)
            with pe.Fori(1, NCH - 1) as c:
                step(c)
            score(NCH - 1)
            turn(NCH - 1)
            attend(NCH - 1)


def image_norm(nc, sb, sem, bank, pad_h, pad_l, stats, gb, ones, power, norm_a, norm_b):
    with ExitStack() as ctx:
        chan = sb("chan", [P, NI, 2], where=ctx)
        off = sb("off", [P, NI], where=ctx)
        spread = sb("spread", [P, NI], where=ctx)
        mu = sb("mu", [P, NI], where=ctx)
        var = sb("var", [P, NI], where=ctx)

        border2_zeroed = sem("border2_zeroed")
        chan_done = sem("chan_done")
        mean_summed = sem("mean_summed")
        b_steps = sem("b_steps")
        var_summed = sem("var_summed")
        rstd_done = sem("rstd_done")
        block = ctx.enter_context(nc.Block())

        @block.gpsimd
        def _(pool):
            for pad in (pad_h, pad_l):
                grid = pad[:, :].rearrange("p (n h w) -> p n h w", n=NI, h=PAD)
                pool.memset(f32(grid[:, :, 0:PAD:PAD - 1, :]), 0.0).then_inc(border2_zeroed, 1)
                pool.memset(f32(grid[:, :, 1:PAD - 1, 0:PAD:PAD - 1]), 0.0).then_inc(border2_zeroed, 1)
            pool.wait_ge(b_steps, 4)
            pool.tensor_tensor(norm_a[:, :], var[:, :], power[:, :], ALU.pow).then_inc(rstd_done, 1)

        @block.vector
        def _(dve):
            for n in range(NI):
                nc.vector.bn_aggr(chan[:, n, :], stats[:, n].rearrange("p c s -> p (c s)")).then_inc(chan_done, 1)
            dve.wait_ge(mean_summed, 1)
            nc.vector.tensor_copy(mu[:, :], bank[0][:, 0:NI]).then_inc(b_steps, 1)
            dve.wait_ge(b_steps, 1)
            nc.vector.tensor_tensor(off[:, :], chan[:, :, 0], mu[:, :], ALU.subtract).then_inc(b_steps, 1)
            dve.wait_ge(b_steps, 2)
            nc.vector.tensor_tensor(spread[:, :], off[:, :], off[:, :], ALU.mult).then_inc(b_steps, 1)
            dve.wait_ge(b_steps, 3)
            nc.vector.tensor_tensor(off[:, :], spread[:, :], chan[:, :, 1], ALU.add).then_inc(var_summed, 1)
            dve.wait_ge(var_summed, 2)
            nc.vector.tensor_scalar(var[:, :], bank[1][:, 0:NI], EPS, None, ALU.add).then_inc(b_steps, 1)
            dve.wait_ge(rstd_done, 1)
            nc.vector.tensor_scalar(norm_a[:, :], norm_a[:, :], gb[:, 0:1], None, ALU.mult).then_inc(b_steps, 1)
            dve.wait_ge(b_steps, 5)
            nc.vector.tensor_tensor(off[:, :], mu[:, :], norm_a[:, :], ALU.mult).then_inc(b_steps, 1)
            dve.wait_ge(b_steps, 6)
            nc.vector.tensor_scalar(norm_b[:, :], off[:, :], -1.0, gb[:, 1:2], ALU.mult, ALU.add).then_inc(b_steps, 1)

        @block.tensor
        def _(pe):
            pe.wait_ge(chan_done, NI)
            pe.matmul(bank[0][:, 0:NI], ones[:, :], chan[:, :, 0], start=True, stop=True).then_inc(mean_summed, 1)
            pe.wait_ge(var_summed, 1)
            pe.matmul(bank[1][:, 0:NI], ones[:, :], off[:, :], start=True, stop=True).then_inc(var_summed, 1)


def token_attention(nc, sb, sem, bank, pad_h, pad_l, resid, virt, z2_h, z2_l, logits, ident, wc_h, wc_l, norm_a,
                    norm_b, power, wq, wk, wvr, wqr_t, ret_blocks, wout, wg, f_w1, f_w2, qk_rows):
    S, D = 8, 16
    NP = S // 2
    NR = 160
    RV = 34
    RVW = 96
    with ExitStack() as ctx:
        t_chunk = sb("t_chunk", [P, CH], where=ctx)
        z_tok = sb("z_tok", [P, G, P], where=ctx)
        zt = sb("zt", [P, CH], where=ctx)
        zt_h = sb("zt_h", [P, CH], F32R, ctx)
        zt_l = sb("zt_l", [P, CH], F32R, ctx)
        wq_h = sb("wq_h", [P, P], F32R, ctx)
        wq_l = sb("wq_l", [P, P], F32R, ctx)
        wk_h = sb("wk_h", [P, P], F32R, ctx)
        wk_l = sb("wk_l", [P, P], F32R, ctx)
        w_tok = sb("w_tok", [P, NR], where=ctx)
        qk = sb("qk", [P, 4, CH], F32R, ctx)
        k_h, k_l, q_h, q_l = (qk[:, n] for n in range(4))
        q_stack = sb("q_stack", [P, 2, NP, CH], F32R, ctx)
        k_stack = sb("k_stack", [P, 2, S, CH], F32R, ctx)
        rvx = sb("rvx", [P, 2, G, RVW], where=ctx)
        r_query = virt[:, :].rearrange("p n h w -> p (n h w)").rearrange("p (g j f) -> p g j f", j=G, f=P)
        s_max = sb("s_max", [P, 2, S], where=ctx)
        s_neg = sb("s_neg", [P, 2, S], where=ctx)
        m_split = sb("m_split", [P, 2, NP, 32], F32R, ctx)
        expd = sb("s_expd", [P, 2, 2, PIX], where=ctx)
        ret = sb("ret", [P, 2, S, 2, RV], where=ctx)
        prod = sb("prod", [P, 2, S, D], where=ctx)
        sim = sb("sim", [P, 2, S], where=ctx)
        r_inv = sb("r_inv", [P, 2, S], where=ctx)
        r_gate = sb("r_gate", [P, 2, S], where=ctx)
        o_tok = sb("o_tok", [P, G, P], where=ctx)
        z2_tok = sb("z2_tok", [P, G, P], where=ctx)
        o_t = z2_tok[:, :, :].rearrange("p j f -> p (j f)")
        t2_chunk = sb("t2_chunk", [P, CH], where=ctx)
        z2_f = t2_chunk
        ln_stats = sb("ln_stats", [P, G, 6], where=ctx)
        ln_mv = sb("ln_mv", [P, G, 2], where=ctx)
        ln_var = sb("ln_var", [P, G], where=ctx)
        ln_rstd = sb("ln_rstd", [P, G], where=ctx)

        y_done = sem("y_done")
        y_high = sem("y_high")
        y_ready = sem("y_ready")
        c_consts = sem("c_consts")
        ones_made = sem("ones_made")
        stack_init = sem("stack_init")
        wa_high = sem("wa_high")
        wa_ready = sem("wa_ready")
        folded = sem("folded")
        w_tok_ready = sem("w_tok_ready")
        conv_done = sem("convc_done")
        t_ready = sem("t_ready")
        t_kept = sem("t_kept")
        t_turned = sem("t_turned")
        ln_steps = sem("ln_steps")
        ln_power = sem("ln_power_done")
        z_ready = sem("z_ready")
        z_turned = sem("z_turned")
        zt_steps = sem("zt_steps")
        zt_ready = sem("zt_ready")
        q_done = sem("q_done")
        k_done = sem("k_done")
        q_high = sem("q_high")
        k_high = sem("k_high")
        q_ready = sem("q_ready")
        k_ready = sem("k_ready")
        tok_done = sem("tok_done")
        tok_copied = sem("tok_copied")
        k_bounced = sem("k_bounced")
        q_bounced = sem("q_bounced")
        stacked = [sem("stacked0"), sem("stacked1")]
        s_done = sem("s_done")
        max_done = sem("max_done")
        m_steps = sem("m_steps")
        m_turned = sem("m_turned")
        m_even = sem("m_even")
        m_odd = sem("m_odd")
        st_done = sem("st_done")
        exp_done = sem("exp_done")
        pv_done = sem("pv_done")
        ret_copied = sem("ret_copied")
        ret_steps = sem("ret_steps")
        gate_exp = sem("gate_exp")
        o_turned = sem("o_turned")
        o_t_ready = sem("o_t_ready")
        out_done = sem("out_done")
        t2_ready = sem("t2_ready")
        t2_kept = sem("t2_kept")
        t2_turned = sem("t2_turned")
        z2_turned = sem("z2_turned")
        z2_steps = sem("z2_steps")
        z2_ready = sem("z2_ready")
        routed = sem("routed")
        logits_kept = sem("logits_kept")

        EW = 8 + 2
        ew_h, ew_l = pad_h, pad_l
        staging = [zt[:, :], t_chunk[:, :], z_tok[:, :, :].rearrange("p j f -> p (j f)")]
        ew_loaded = [sem(f"ew_loaded{i}") for i in range(3)]
        ew_split = sem("ew_split")

        img_h = pad_h[:, :].rearrange("p (n h w) -> p n h w", n=NI, h=PAD)
        img_l = pad_l[:, :].rearrange("p (n h w) -> p n h w", n=NI, h=PAD)
        ps_conv, ps_s, ps_st, ps_pv, ps_x = bank[0], bank[1:3], bank[3:5], bank[5:7], bank[7]
        LATE_TAPS = {4: range(0, 2), 5: range(2, 3), 6: range(3, 4), 7: range(4, 6)}
        STACK = 16 * 9
        RS, LS = 10, 3
        FIRST, MIDDLE, LAST_BUT_ONE, LAST = range(4)
        block = ctx.enter_context(nc.Block())

        def tail_norm(g):
            return 2 * g + 3 if not isinstance(g, int) or g < NCH - 2 else NCH + g

        def max_bank(stage):
            return ps_x if stage in (FIRST, MIDDLE) else ps_conv

        def chunk(tensor, g):
            return tensor[:, bass.ds(g * CH, CH)]

        @block.sync
        def _(sp):
            def stack(g, ring):
                def bounce(first, signal):
                    sp.dma_start(qk_rows[bass.ds(g, 1), first:first + 2].rearrange("g n c t -> c (g n) t"),
                                 f32(qk[:, first:first + 2, :])).then_inc(signal, 16)

                def fill_k(b):
                    at = slice(b * PIX, (b + 1) * PIX)
                    for slot, n in enumerate((0, 0, 1)):
                        src = qk_rows[bass.ds(g, 1), n, :, at].rearrange("g (p a r) t -> a r (g p) t", p=NP, a=2)
                        for a in range(2):
                            row = 32 * slot + D * a
                            sp.dma_start(f32(k_stack[row:row + D, ring, a:S:2, at]), src[a]).then_inc(stacked[b], 16)

                def fill_q(b):
                    at = slice(b * PIX, (b + 1) * PIX)
                    for slot, n in enumerate((2, 3, 2)):
                        src = qk_rows[bass.ds(g, 1), n, :, at].rearrange("g (p r) t -> r (g p) t", p=NP)
                        sp.dma_start(f32(q_stack[32 * slot:32 * slot + 32, ring, :, at]), src
                                     ).then_inc(stacked[b], 16)

                sp.wait_ge(k_ready, g + 1)
                bounce(0, k_bounced)
                sp.wait_ge(q_ready, g + 1)
                bounce(2, q_bounced)
                sp.wait_ge(k_bounced, 16 * (g + 1))
                fill_k(0)
                sp.wait_ge(q_bounced, 16 * (g + 1))
                fill_q(0)
                fill_k(1)
                fill_q(1)

            sp.wait_ge(stack_init, 2)
            stack(0, 0)
            stack(1, 1)
            with sp.Fori(1, NCH // 2) as pair:
                stack(2 * pair, 0)
                stack(2 * pair + 1, 1)
            sp.wait_ge(tok_done, 2 * NCH)
            sp.wait_ge(t_kept, NCH)
            for n in range(EW):
                if n >= len(staging):
                    sp.wait_ge(ew_split, 2 * (n - len(staging) + 1))
                src = f_w1[:, n] if n < 8 else f_w2[:, n - 8].rearrange("p f o -> p (f o)")
                sp.dma_start(staging[n % 3], src).then_inc(ew_loaded[n % 3], 16)

        @block.gpsimd
        def _(pool):
            pool.memset(rvx[:, :, :, 2 * D:RVW], 1.0).then_inc(c_consts, 1)
            pool.memset(f32(k_stack[:, :, :, :]), 0.0).then_inc(stack_init, 1)
            pool.memset(f32(m_split[:, :, :, :]), 0.0).then_inc(stack_init, 1)
            def rstd(n):
                pool.wait_ge(ln_steps, LS * n + 3)
                pool.tensor_tensor(ln_rstd[:, :], ln_var[:, :], power[:, 0:G], ALU.pow).then_inc(ln_power, 1)

            ones_rows = f32(k_stack[96:100].rearrange("p r s t -> p (r s) t"))
            pool.wait_ge(stack_init, 2)
            pool.memset(ones_rows[0:2, 0:2 * S:2], 1.0).then_inc(ones_made, 1)
            pool.wait_ge(ones_made, 1)
            pool.memset(ones_rows[:, 1:2 * S:2], 1.0).then_inc(ones_made, 1)
            pool.wait_ge(ones_made, 2)
            rstd(0)
            pool.wait_ge(ln_power, 1)
            pool.memset(ones_rows[0:2, 1:2 * S:2], 0.0).then_inc(ones_made, 1)
            pool.wait_ge(ones_made, 3)
            rstd(1)
            def low_z2(g, norms):
                pool.wait_ge(ln_power, norms)
                pool.wait_ge(z2_steps, 2 * g + 2)
                pool.tensor_tensor(chunk(z2_l, g), z2_f[:, :], f32(chunk(z2_h, g)), ALU.subtract
                                   ).then_inc(z2_ready, 1)
                pool.wait_ge(z2_ready, g + 1)

            rstd(2)
            with pool.Fori(1, NCH - 2) as g:
                rstd(2 * g + 1)
                rstd(2 * g + 2)
                low_z2(g - 1, 2 * g + 3)
            rstd(2 * NCH - 3)
            pool.wait_ge(conv_done, NCH)

            def split_block(n):
                high, low = ew_h[:, n * CH:(n + 1) * CH], ew_l[:, n * CH:(n + 1) * CH]
                pool.wait_ge(ew_loaded[n % 3], 16 * (n // 3 + 1))
                pool.tensor_copy(high, staging[n % 3]).then_inc(ew_split, 1)
                pool.wait_ge(ew_split, 2 * n + 1)
                pool.tensor_tensor(low, staging[n % 3], f32(high), ALU.subtract).then_inc(ew_split, 1)
                pool.wait_ge(ew_split, 2 * n + 2)

            for n in range(3):
                split_block(n)
            low_z2(NCH - 3, 2 * NCH - 2)
            for n in range(3, 6):
                split_block(n)
            rstd(2 * NCH - 2)
            low_z2(NCH - 2, 2 * NCH - 1)
            for n in range(6, EW):
                split_block(n)
            rstd(2 * NCH - 1)

        @block.scalar
        def _(act):
            def normalise(n):
                nc.scalar.activation(virt[:, n], virt[:, n], ACT.Relu, scale=norm_a[:, n:n + 1],
                                     bias=norm_b[:, n:n + 1]).then_inc(y_done, 1)

            def high(n):
                act.wait_ge(y_done, n + 1)
                nc.scalar.activation(img_h[:, n, 1:1 + HW, 1:1 + HW], virt[:, n], ACT.Copy).then_inc(y_high, 1)

            def image_pair(pair):
                for n in (2 * pair, 2 * pair + 1):
                    normalise(n)
                for n in (2 * pair, 2 * pair + 1):
                    high(n)

            image_pair(0)
            image_pair(1)
            nc.scalar.activation(wq_h[:, :], wq[:, :], ACT.Copy, scale=float(D) ** -0.5).then_inc(wa_high, 1)
            nc.scalar.activation(wk_h[:, :], wk[:, :], ACT.Copy).then_inc(wa_high, 1)
            for pair in range(2, 6):
                image_pair(pair)

            def keep_t(g):
                act.wait_ge(t_ready, g + 1)
                nc.scalar.activation(chunk(resid, g), t_chunk[:, :], ACT.Copy).then_inc(t_kept, 1)

            def split_zt(g):
                act.wait_ge(z_turned, g + 1)
                nc.scalar.activation(zt[:, :], ps_conv[:, :], ACT.Copy).then_inc(zt_steps, 1)
                act.wait_ge(zt_steps, 2 * g + 1)
                nc.scalar.activation(zt_h[:, :], zt[:, :], ACT.Copy).then_inc(zt_steps, 1)

            def split_k(g):
                need(act, k_bounced, 16 * g)
                act.wait_ge(k_done, g + 1)
                nc.scalar.activation(k_h, ps_conv[:, :], ACT.Copy).then_inc(k_high, 1)

            def split_q(g):
                need(act, q_bounced, 16 * g)
                act.wait_ge(q_done, g + 1)
                nc.scalar.activation(q_h, ps_x[:, :], ACT.Copy).then_inc(q_high, 1)

            def keep_tok(g, half, ring):
                act.wait_ge(tok_done, 2 * g + half + 1)
                need(act, pv_done, 2 * S * (g - 1))
                src = (ps_x, ps_conv)[half][:, 0:2 * NR].rearrange("p (j f) -> p j f", j=2)
                two = slice(2 * half, 2 * half + 2)
                nc.scalar.activation(r_query[:, g, two, :], src[:, :, 0:P], ACT.Copy).then_inc(tok_copied, 1)
                nc.scalar.activation(rvx[:, ring, two, 0:2 * D], src[:, :, P:NR], ACT.Copy).then_inc(tok_copied, 1)

            def place_max(g, b, ring, src=ps_x):
                act.wait_ge(m_turned, 2 * g + b + 1)
                for p in (2, 3):
                    nc.scalar.activation(q_stack[96:100, ring, p, b * PIX:(b + 1) * PIX],
                                         src[32 * p:32 * p + 4, 0:PIX], ACT.Copy).then_inc(m_odd, 1)

            def exponent(g, b, s):
                act.wait_ge(st_done, 2 * S * g + S * b + s + 1)
                need(act, pv_done, 2 * S * g + S * b + s - 1)
                nc.scalar.activation(expd[:, s % 2].rearrange("p a i -> p (a i)"), ps_st[s % 2][:, :], ACT.Exp
                                     ).then_inc(exp_done, 1)

            def keep_ret(g, b, half):
                act.wait_ge(pv_done, 2 * S * g + S * b + 4 * half + 4)
                need(act, ret_steps, RS * (2 * g + b - 1))
                nc.scalar.activation(ret[:, b, 4 * half:4 * half + 4].rearrange("p s i f -> p (s i f)"),
                                     ps_pv[half][:, 0:8 * RV], ACT.Copy).then_inc(ret_copied, 1)

            def gate(g, b):
                act.wait_ge(ret_steps, RS * (2 * g + b) + 4)
                nc.scalar.activation(r_gate[:, :, :], sim[:, :, :], ACT.Exp, scale=-1.0).then_inc(gate_exp, 1)

            def keep_o(g):
                act.wait_ge(o_turned, g + 1)
                nc.scalar.activation(o_t[:, :], ps_x[:, :], ACT.Copy).then_inc(o_t_ready, 1)

            def keep_t2(g):
                act.wait_ge(t2_ready, g + 1)
                nc.scalar.activation(chunk(resid, g), t2_chunk[:, :], ACT.Copy).then_inc(t2_kept, 1)

            def split_z2(g):
                act.wait_ge(z2_turned, g + 1)
                act.wait_ge(t2_kept, g + 1)
                nc.scalar.activation(z2_f[:, :], ps_conv[:, :], ACT.Copy).then_inc(z2_steps, 1)
                act.wait_ge(z2_steps, 2 * g + 1)
                nc.scalar.activation(chunk(z2_h, g), z2_f[:, :], ACT.Copy).then_inc(z2_steps, 1)

            def keep_logits(g):
                act.wait_ge(routed, g + 1)
                nc.scalar.activation(logits[:, bass.ds(g * G, G), :],
                                     ps_conv[:, 0:G * S].rearrange("p (j e) -> p j e", j=G), ACT.Copy
                                     ).then_inc(logits_kept, 1)

            def body(g, ring, stage=MIDDLE):
                for s in range(S):
                    exponent(g, 0, s)
                    if stage != LAST:
                        if s == 0:
                            split_k(g + 1)
                        if s == 1:
                            split_q(g + 1)
                        if s == 3:
                            keep_tok(g + 1, 0, 1 - ring)
                            keep_tok(g + 1, 1, 1 - ring)
                    if stage != FIRST:
                        if s == 2:
                            gate(g - 1, 1)
                        if s == 4:
                            keep_o(g - 1)
                        if s == 6:
                            keep_t2(g - 1)
                    if s == 5:
                        keep_ret(g, 0, 0)
                keep_ret(g, 0, 1)
                place_max(g, 1, ring, max_bank(stage))
                for s in range(S):
                    exponent(g, 1, s)
                    if s == 1 and stage in (FIRST, MIDDLE):
                        keep_t(g + 2)
                    if s == 2:
                        gate(g, 0)
                    if stage != FIRST:
                        if s == 3:
                            split_z2(g - 1)
                        if s == 5:
                            keep_logits(g - 1)
                    if s == 5:
                        keep_ret(g, 1, 0)
                    if s == 7 and stage in (FIRST, MIDDLE):
                        split_zt(g + 2)
                keep_ret(g, 1, 1)
                if stage != LAST:
                    place_max(g + 1, 0, 1 - ring)

            keep_t(0)
            split_zt(0)
            keep_t(1)
            split_k(0)
            split_q(0)
            keep_tok(0, 0, 0)
            keep_tok(0, 1, 0)
            image_pair(6)
            split_zt(1)
            image_pair(7)
            place_max(0, 0, 0)
            body(0, 0, FIRST)
            body(1, 1)
            with act.Fori(1, NCH // 2 - 1) as pair:
                body(2 * pair, 0)
                body(2 * pair + 1, 1)
            body(NCH - 2, 0, LAST_BUT_ONE)
            body(NCH - 1, 1, LAST)
            gate(NCH - 1, 1)
            keep_o(NCH - 1)
            keep_t2(NCH - 1)
            split_z2(NCH - 1)
            keep_logits(NCH - 1)

        @block.vector
        def _(dve):
            def low(n):
                dve.wait_ge(y_high, n + 1)
                inside = img_l[:, n, 1:1 + HW, 1:1 + HW]
                nc.vector.tensor_tensor(inside, virt[:, n], f32(img_h[:, n, 1:1 + HW, 1:1 + HW]), ALU.subtract
                                        ).then_inc(y_ready, 1)

            for n in range(4):
                low(n)
            dve.wait_ge(wa_high, 1)
            nc.vector.scalar_tensor_tensor(wq_l[:, :], wq[:, :], float(D) ** -0.5, f32(wq_h[:, :]), ALU.mult,
                                           ALU.subtract).then_inc(wa_ready, 1)
            dve.wait_ge(wa_high, 2)
            nc.vector.tensor_tensor(wk_l[:, :], wk[:, :], f32(wk_h[:, :]), ALU.subtract).then_inc(wa_ready, 1)
            nc.vector.tensor_tensor(w_tok[:, P:P + D], wvr[:, 0:D], wvr[:, D:2 * D], ALU.subtract
                                    ).then_inc(w_tok_ready, 1)
            nc.vector.tensor_copy(w_tok[:, P + D:NR], wvr[:, D:2 * D]).then_inc(w_tok_ready, 1)
            dve.wait_ge(folded, 1)
            nc.vector.tensor_scalar(w_tok[:, 0:P], ps_x[:, 0:P], float(D) ** -0.5, None, ALU.mult
                                    ).then_inc(w_tok_ready, 1)
            dve.wait_ge(c_consts, 1)

            for n in range(4, 12):
                low(n)

            def add_conv(g, src=ps_conv):
                dve.wait_ge(conv_done, g + 1)
                need(dve, t_kept, g)
                need(dve, t_turned, g)
                nc.vector.tensor_tensor(t_chunk[:, :], src[:, :], chunk(resid, g), ALU.add).then_inc(t_ready, 1)

            def norm_stats(n, turned, count, src=ps_x):
                dve.wait_ge(turned, count)
                for j in range(G):
                    last = nc.vector.bn_stats(ln_stats[:, j, :], src[:, j * P:(j + 1) * P])
                last.then_inc(ln_steps, 1)
                dve.wait_ge(ln_steps, LS * n + 1)
                nc.vector.memset(ln_var[:, :], 0.0)
                for j in range(G):
                    last = nc.vector.bn_aggr(ln_mv[:, j, :], ln_stats[:, j, :])
                last.then_inc(ln_steps, 1)
                dve.wait_ge(ln_steps, LS * n + 2)
                nc.vector.tensor_scalar(ln_var[:, :], ln_mv[:, :, 1], EPS, None, ALU.add).then_inc(ln_steps, 1)

            def normalise(n, dst, src=ps_x):
                dve.wait_ge(ln_power, n + 1)
                for j in range(G):
                    last = nc.vector.tensor_scalar(dst[:, j, :], src[:, j * P:(j + 1) * P], ln_mv[:, j, 0:1],
                                                   ln_rstd[:, j:j + 1], ALU.subtract, ALU.mult)
                last.then_inc(z_ready, 1)

            def low_zt(g):
                dve.wait_ge(zt_steps, 2 * g + 2)
                nc.vector.tensor_tensor(zt_l[:, :], zt[:, :], f32(zt_h[:, :]), ALU.subtract).then_inc(zt_ready, 1)

            def low_k(g):
                dve.wait_ge(k_high, g + 1)
                nc.vector.tensor_tensor(k_l, ps_conv[:, :], f32(k_h), ALU.subtract).then_inc(k_ready, 1)

            def low_q(g):
                dve.wait_ge(q_high, g + 1)
                nc.vector.tensor_tensor(q_l, ps_x[:, :], f32(q_h), ALU.subtract).then_inc(q_ready, 1)

            def row_max(g, b, s):
                dve.wait_ge(s_done, 2 * S * g + S * b + s + 1)
                nc.vector.tensor_reduce(s_max[:, :, s], ps_s[s % 2][:, :].rearrange("p (a j) -> p a j", a=2), AX.X,
                                        ALU.max).then_inc(max_done, 1)

            def split_max(g, b):
                image = 2 * g + b
                high = m_split[:, :, :, 0:4:2].rearrange("p i q a -> p (i q) a")
                low = m_split[:, :, :, 1:4:2].rearrange("p i q a -> p (i q) a")
                minus = s_neg[:, :, :].rearrange("p i (q a) -> p (i q) a", a=2)
                dve.wait_ge(max_done, S * image + S)
                nc.vector.tensor_scalar(s_neg[:, :, :], s_max[:, :, :], -1.0, None, ALU.mult).then_inc(m_steps, 1)
                dve.wait_ge(m_steps, 3 * image + 1)
                nc.vector.tensor_copy(high, minus).then_inc(m_steps, 1)
                dve.wait_ge(m_steps, 3 * image + 2)
                nc.vector.tensor_tensor(low, minus, f32(high), ALU.subtract).then_inc(m_steps, 1)

            def place_max(g, b, ring, src=ps_x):
                dve.wait_ge(m_turned, 2 * g + b + 1)
                for p in (0, 1):
                    nc.vector.tensor_copy(q_stack[96:100, ring, p, b * PIX:(b + 1) * PIX],
                                          src[32 * p:32 * p + 4, 0:PIX]).then_inc(m_even, 1)

            def retrieve(g, b, part):
                r = ret[:, b].rearrange("p s i f -> p i s f")
                diff, value1, total = r[:, :, :, 0:D], r[:, :, :, D:2 * D], r[:, :, :, 2 * D]
                query = r_query[:, g, 2 * b:2 * b + 2, :].rearrange("p i (s d) -> p i s d", s=S)
                base = RS * (2 * g + b)
                wide = [P, 2, S, D]
                if part == 0:
                    need(dve, ret_steps, base)
                    dve.wait_ge(ret_copied, 2 * (2 * g + b) + 2)
                    nc.vector.reciprocal(r_inv[:, :, :], total).then_inc(ret_steps, 1)
                    nc.vector.tensor_tensor(prod[:, :, :, :], diff, query, ALU.mult).then_inc(ret_steps, 1)
                    dve.wait_ge(ret_steps, base + 2)
                    nc.vector.tensor_reduce(sim[:, :, :], prod[:, :, :, :], AX.X, ALU.add).then_inc(ret_steps, 1)
                    dve.wait_ge(ret_steps, base + 3)
                    nc.vector.tensor_tensor(sim[:, :, :], sim[:, :, :], r_inv[:, :, :], ALU.mult
                                            ).then_inc(ret_steps, 1)
                if part == 1:
                    dve.wait_ge(gate_exp, 2 * g + b + 1)
                    nc.vector.tensor_scalar(r_gate[:, :, :], r_gate[:, :, :], 1.0, None, ALU.add
                                            ).then_inc(ret_steps, 1)
                    dve.wait_ge(ret_steps, base + 5)
                    nc.vector.reciprocal(r_gate[:, :, :], r_gate[:, :, :]).then_inc(ret_steps, 1)
                    dve.wait_ge(ret_steps, base + 6)
                    nc.vector.tensor_tensor(prod[:, :, :, :], diff, r_gate[:, :, :].unsqueeze(3).broadcast_to(wide),
                                            ALU.mult).then_inc(ret_steps, 1)
                if part == 2:
                    dve.wait_ge(ret_steps, base + 7)
                    nc.vector.tensor_tensor(prod[:, :, :, :], prod[:, :, :, :], value1, ALU.add
                                            ).then_inc(ret_steps, 1)
                    dve.wait_ge(ret_steps, base + 8)
                    need(dve, o_turned, g)
                    nc.vector.tensor_tensor(o_tok[:, 2 * b:2 * b + 2, :].rearrange("p i (s d) -> p i s d", s=S),
                                            prod[:, :, :, :], r_inv[:, :, :].unsqueeze(3).broadcast_to(wide),
                                            ALU.mult).then_inc(ret_steps, 2)

            def add_attention(g):
                dve.wait_ge(out_done, g + 1)
                need(dve, z2_ready, g)
                nc.vector.tensor_tensor(t2_chunk[:, :], ps_x[:, :], chunk(resid, g), ALU.add).then_inc(t2_ready, 1)

            def low_z2(g):
                dve.wait_ge(z2_steps, 2 * g + 2)
                nc.vector.tensor_tensor(chunk(z2_l, g), z2_f[:, :], f32(chunk(z2_h, g)), ALU.subtract
                                        ).then_inc(z2_ready, 1)

            def body(g, ring, stage=MIDDLE):
                for s in range(S):
                    row_max(g, 1, s)
                    if stage != LAST:
                        if s == 0:
                            low_k(g + 1)
                        if s == 1:
                            low_q(g + 1)
                    if stage != FIRST:
                        if s in (1, 2, 3):
                            retrieve(g - 1, 1, s - 1)
                        if s == 5:
                            add_attention(g - 1)
                        if s == 6:
                            norm_stats(tail_norm(g - 1), t2_turned, g)
                        if s == 7 and stage == MIDDLE:
                            normalise(tail_norm(g - 1), z2_tok)
                split_max(g, 1)
                place_max(g, 1, ring, max_bank(stage))
                if stage in (LAST_BUT_ONE, LAST):
                    normalise(tail_norm(g - 1), z2_tok)
                for s in range(S):
                    if stage != LAST:
                        row_max(g + 1, 0, s)
                    if stage == MIDDLE and s == 0:
                        add_conv(g + 2)
                    if stage in (FIRST, MIDDLE):
                        if s == 2:
                            norm_stats(2 * g + 2, t_turned, g + 3)
                        if s == 3:
                            normalise(2 * g + 2, z_tok)
                    if s == 1:
                        retrieve(g, 0, 0)
                    if s == 4:
                        retrieve(g, 0, 1)
                    if s == 5:
                        retrieve(g, 0, 2)
                if stage != LAST:
                    split_max(g + 1, 0)
                if stage in (FIRST, MIDDLE):
                    low_zt(g + 2)
                if stage != LAST:
                    place_max(g + 1, 0, 1 - ring)

            add_conv(0)
            norm_stats(0, t_turned, 1)
            normalise(0, z_tok)
            add_conv(1, ps_s[0])
            low_zt(0)
            norm_stats(1, t_turned, 2, ps_s[1])
            low_k(0)
            low_q(0)
            dve.wait_ge(z_turned, 1)
            normalise(1, z_tok, ps_s[1])
            low(12)
            low(13)
            low_zt(1)
            low(14)
            low(15)
            for s in range(S):
                row_max(0, 0, s)
                if s == 3:
                    add_conv(2, ps_pv[0])
            split_max(0, 0)
            place_max(0, 0, 0)
            body(0, 0, FIRST)
            body(1, 1)
            with dve.Fori(1, NCH // 2 - 1) as pair:
                body(2 * pair, 0)
                body(2 * pair + 1, 1)
            body(NCH - 2, 0, LAST_BUT_ONE)
            body(NCH - 1, 1, LAST)
            for part in range(3):
                retrieve(NCH - 1, 1, part)
            add_attention(NCH - 1)
            norm_stats(tail_norm(NCH - 1), t2_turned, NCH)
            normalise(tail_norm(NCH - 1), z2_tok)
            low_z2(NCH - 1)

        @block.tensor
        def _(pe):
            def conv_taps(g, taps, dst=ps_conv):
                if taps[0] == 0:
                    pe.wait_ge(y_ready, 2 * g + 2)
                    if dst is ps_conv:
                        need(pe, tok_copied, 4 * g)
                for t in taps:
                    dy, dx = TAPS[t]
                    part = (slice(None), bass.ds(2 * g, 2), slice(dy, dy + HW), slice(dx, dx + HW))
                    last = split_product(pe, dst[:, :], wc_h[:, t, :], wc_l[:, t, :], img_h[part], img_l[part],
                                         t == 0, t == 8)
                if taps[-1] == 8:
                    last.then_inc(conv_done, 1)

            def turn(dst, src, signal):
                for j in range(G):
                    last = pe.transpose(dst[:, j * P:(j + 1) * P], src[:, j * P:(j + 1) * P], ident[:, :])
                last.then_inc(signal, 1)

            def flat(t):
                return t[:, :, :].rearrange("p j f -> p (j f)")

            def head_turn(g, dst=ps_x):
                pe.wait_ge(t_ready, g + 1)
                turn(dst, t_chunk, t_turned)

            def head_turn_back(g, norm):
                pe.wait_ge(z_ready, norm)
                turn(ps_conv, flat(z_tok), z_turned)

            def head_k(g):
                pe.wait_ge(zt_ready, g + 1)
                split_product(pe, ps_conv[:, :], wk_h[:, :], wk_l[:, :], zt_h[:, :], zt_l[:, :], True, True
                              ).then_inc(k_done, 1)

            def head_q(g):
                split_product(pe, ps_x[:, :], wq_h[:, :], wq_l[:, :], zt_h[:, :], zt_l[:, :], True, True
                              ).then_inc(q_done, 1)

            def head_tokens(g):
                for half, (ps, free) in enumerate(((ps_x, q_ready), (ps_conv, k_ready))):
                    pe.wait_ge(free, g + 1)
                    for j in range(2):
                        at = (2 * half + j) * P
                        last = pe.matmul(ps[:, j * NR:(j + 1) * NR], zt[:, at:at + P], w_tok[:, :], start=True,
                                         stop=True)
                    last.then_inc(tok_done, 1)

            def scores(g, b, s, ring):
                if s == 0:
                    pe.wait_ge(stacked[b], STACK * (g + 1))
                need(pe, max_done, 2 * S * g + S * b + s - 1)
                at = b * PIX
                for i in range(2):
                    last = pe.matmul(ps_s[s % 2][:, i * PIX:(i + 1) * PIX],
                                     q_stack[0:96, ring, s // 2, at + i * P:at + (i + 1) * P],
                                     k_stack[0:96, ring, s, at:at + PIX], start=True, stop=True)
                last.then_inc(s_done, 1)

            def turn_max(g, b, dst=ps_x):
                pe.wait_ge(m_steps, 3 * (2 * g + b) + 3)
                for i in range(2):
                    src = f32(m_split[:, i].rearrange("p q c -> p (q c)"))
                    last = pe.transpose(dst[:, i * P:(i + 1) * P], src, ident[:, :])
                last.then_inc(m_turned, 1)

            def max_placed(image):
                pe.wait_ge(m_even, 2 * image + 2)
                pe.wait_ge(m_odd, 2 * image + 2)

            def shifted_scores(g, b, s, ring):
                need(pe, exp_done, 2 * S * g + S * b + s - 1)
                at = b * PIX
                for i in range(2):
                    last = pe.matmul(ps_st[s % 2][:, i * PIX:(i + 1) * PIX],
                                     k_stack[0:100, ring, s, at + i * P:at + (i + 1) * P],
                                     q_stack[0:100, ring, s // 2, at:at + PIX], start=True, stop=True)
                last.then_inc(st_done, 1)

            def retrieve(g, b, s, ring):
                pe.wait_ge(exp_done, 2 * S * g + S * b + s + 1)
                if s % 4 == 0:
                    need(pe, ret_copied, 2 * (2 * g + b - 1) + s // 4 + 1)
                if s == 0 and b == 0:
                    pe.wait_ge(tok_copied, 4 * g + 4)
                for i in range(2):
                    at = ((s % 4) * 2 + i) * RV
                    for a in range(2):
                        last = pe.matmul(ps_pv[s // 4][:, at:at + RVW], expd[:, s % 2, a, i * P:(i + 1) * P],
                                         rvx[:, ring, 2 * b + a, :], start=(a == 0), stop=(a == 1))
                last.then_inc(pv_done, 1)

            def tail_turn(g):
                pe.wait_ge(ret_steps, RS * (2 * g + 2))
                turn(ps_x, flat(o_tok), o_turned)

            def tail_out(g):
                pe.wait_ge(o_t_ready, g + 1)
                pe.matmul(ps_x[:, :], wout[:, :], o_t[:, :], start=True, stop=True).then_inc(out_done, 1)

            def tail_turn2(g):
                pe.wait_ge(t2_ready, g + 1)
                turn(ps_x, t2_chunk, t2_turned)

            def tail_turn_back(g):
                turn(ps_conv, flat(z2_tok), z2_turned)

            def tail_route(g):
                pe.wait_ge(z2_steps, 2 * g + 1)
                for j in range(G):
                    last = pe.matmul(ps_conv[:, j * S:(j + 1) * S], z2_f[:, j * P:(j + 1) * P], wg[:, :], start=True,
                                     stop=True)
                last.then_inc(routed, 1)

            def body(g, ring, stage=MIDDLE):
                ahead = stage in (FIRST, MIDDLE)
                max_placed(2 * g)
                for s in range(S):
                    shifted_scores(g, 0, s, ring)
                    scores(g, 1, s, ring)
                    if s:
                        retrieve(g, 0, s - 1, ring)
                    if stage != LAST:
                        if s == 0:
                            head_q(g + 1)
                        if s == 3:
                            head_tokens(g + 1)
                    if stage != FIRST:
                        if s == 4:
                            if stage != LAST:
                                pe.wait_ge(tok_copied, 4 * (g + 1) + 2)
                            tail_turn(g - 1)
                        if s == 5:
                            tail_out(g - 1)
                        if s == 6:
                            tail_turn2(g - 1)
                    if stage == MIDDLE and s in LATE_TAPS:
                        conv_taps(g + 2, LATE_TAPS[s])
                retrieve(g, 0, S - 1, ring)
                if stage == MIDDLE:
                    conv_taps(g + 2, range(6, 7))
                if stage == FIRST:
                    pe.wait_ge(tok_copied, 4 * (g + 1) + 2)
                elif stage == MIDDLE:
                    pe.wait_ge(z_ready, tail_norm(g - 1) + 1)
                elif stage == LAST_BUT_ONE:
                    pe.wait_ge(tok_copied, 4 * NCH)
                else:
                    pe.wait_ge(logits_kept, g - 1)
                turn_max(g, 1, max_bank(stage))
                if stage == MIDDLE:
                    conv_taps(g + 2, range(7, 9))
                max_placed(2 * g + 1)
                for s in range(S):
                    shifted_scores(g, 1, s, ring)
                    if stage != LAST:
                        scores(g + 1, 0, s, 1 - ring)
                    if s:
                        retrieve(g, 1, s - 1, ring)
                    if ahead and s == 1:
                        head_turn(g + 2)
                    if stage != FIRST:
                        if s == 2:
                            if not ahead:
                                pe.wait_ge(z_ready, tail_norm(g - 1) + 1)
                            tail_turn_back(g - 1)
                        if s == 4:
                            tail_route(g - 1)
                    if ahead and s == 6:
                        need(pe, logits_kept, g)
                        head_turn_back(g + 2, 2 * g + 3)
                retrieve(g, 1, S - 1, ring)
                if stage != LAST:
                    turn_max(g + 1, 0)
                if ahead:
                    head_k(g + 2)

            pe.matmul(ps_x[:, 0:P], wqr_t[:, :], ret_blocks[:, :], start=True, stop=True).then_inc(folded, 1)
            conv_taps(0, range(9))
            conv_taps(1, range(0, 3), ps_s[0])
            pe.wait_ge(w_tok_ready, 3)
            head_turn(0)
            conv_taps(1, range(3, 9), ps_s[0])
            head_turn_back(0, 1)
            head_turn(1, ps_s[1])
            conv_taps(2, range(0, 2), ps_pv[0])
            pe.wait_ge(wa_ready, 2)
            head_k(0)
            head_q(0)
            conv_taps(2, range(2, 3), ps_pv[0])
            head_tokens(0)
            conv_taps(2, range(3, 4), ps_pv[0])
            pe.wait_ge(tok_copied, 4)
            head_turn_back(1, 2)
            conv_taps(2, range(4, 8), ps_pv[0])
            head_k(1)
            for s in range(S):
                scores(0, 0, s, 0)
                if s == 0:
                    conv_taps(2, range(8, 9), ps_pv[0])
            turn_max(0, 0)
            pe.wait_ge(ones_made, 3)
            pe.wait_ge(t_ready, 3)
            body(0, 0, FIRST)
            body(1, 1)
            with pe.Fori(1, NCH // 2 - 1) as pair:
                body(2 * pair, 0)
                body(2 * pair + 1, 1)
            body(NCH - 2, 0, LAST_BUT_ONE)
            body(NCH - 1, 1, LAST)
            tail_turn(NCH - 1)
            tail_out(NCH - 1)
            tail_turn2(NCH - 1)
            pe.wait_ge(z_ready, tail_norm(NCH - 1) + 1)
            tail_turn_back(NCH - 1)
            tail_route(NCH - 1)


def experts(nc, sb, sem, bank, pad_h, pad_l, resid, virt, z2_h, z2_l, logits, ident, f_w2, out, w_rows):
    E, FB = 8, 4
    NK = E * FB
    NT = NCH * G
    HR = 4
    LEAD = 4
    with ExitStack() as ctx:
        ew_h = pad_h[:, 0:10 * CH].rearrange("p (n f) -> p n f", f=CH)
        ew_l = pad_l[:, 0:10 * CH].rearrange("p (n f) -> p n f", f=CH)
        E2 = 2
        w2 = sb("w2", [P, E - E2, CH], where=ctx)
        w2_h = sb("w2_h", [P, E - E2, CH], F32R, ctx)
        w2_l = sb("w2_l", [P, E - E2, CH], F32R, ctx)
        rank_i = sb("rank_i", [P, E], I32, ctx)
        rank = sb("rank", [P, E], where=ctx)
        hot = sb("hot", [P, 2, NT, E], where=ctx)
        best = sb("best", [P, 2, NT], where=ctx)
        first = sb("first", [P, NT], where=ctx)
        other = sb("other", [P, NT, E], where=ctx)
        gap = sb("gap", [P, NT], where=ctx)
        share = sb("share", [P, 2, NT], where=ctx)
        weight = sb("weight", [P, NT, E], where=ctx)
        weight_chunk = sb("weight_chunk", [P, G, E], where=ctx)
        weight_t = sb("weight_t", [E, CH], where=ctx)
        hid_h = sb("hid_h", [P, FB, CH], F32R, ctx)
        hid_l = sb("hid_l", [P, FB, CH], F32R, ctx)
        w_all = sb("w_all", [P, 2, CH], where=ctx)
        spare = virt[:, :].rearrange("p n h w -> p (n h w)").rearrange("p (n f) -> p n f", f=CH)
        hid = spare[:, 0:FB]
        part = spare[:, FB:FB + 2]
        out_sb = spare[:, 6:8]

        w2_loaded = [sem(f"w2_loaded{e}") for e in range(E - E2)]
        w2_steps = sem("w2_steps")
        rank_made = sem("rank_made")
        choice = sem("choice")
        share_exp = sem("share_exp")
        weights_ready = sem("weights_ready")
        wt_staged = sem("wt_staged")
        wt_turned = sem("wt_turned")
        wt_ready = sem("wt_ready")
        rows_out = sem("rows_out")
        spread = [sem("spread0"), sem("spread1")]
        hidden = sem("hidden_done")
        silu_done = sem("silu_done")
        hid_high = sem("hid_high")
        hid_last_high = sem("hid_last_high")
        hid_ready = sem("hid_ready")
        down_done = sem("down_done")
        weighed = sem("weighed")
        added = sem("added")
        stored = [sem("stored0"), sem("stored1")]
        ps_h, ps_y, ps_t = bank[0:HR], bank[5:7], bank[7]
        block = ctx.enter_context(nc.Block())

        @block.sync
        def _(sp):
            for e in range(E - E2):
                sp.dma_start(w2[:, e], f_w2[:, e + E2].rearrange("p f o -> p (f o)")).then_inc(w2_loaded[e], 16)

            def rows_to_dram(g):
                sp.wait_ge(wt_ready, g + 1)
                sp.dma_start(w_rows[bass.ds(g, 1)].rearrange("g e t -> (g e) t"), weight_t[:, :]
                             ).then_inc(rows_out, 16)

            def spread_weights(g, e):
                need(sp, weighed, E * g + e - 1)
                sp.dma_start(w_all[:, e % 2], w_rows[bass.ds(g, 1), e].broadcast_to([P, CH])
                             ).then_inc(spread[e % 2], 16)

            def store(g, slot):
                sp.dma_start(out[:, bass.ds(g * CH, CH)], out_sb[:, slot]).then_inc(stored[slot], 16)

            def body(g, slot, last=False):
                for e in range(E):
                    if e == E - 1 and not last:
                        rows_to_dram(g + 1)
                    spread_weights(g, e)
                if not last:
                    sp.wait_ge(rows_out, 16 * (g + 2))
                if not (isinstance(g, int) and g == 0):
                    store(g - 1, 1 - slot)

            rows_to_dram(0)
            sp.wait_ge(rows_out, 16)
            body(0, 0)
            body(1, 1)
            with sp.Fori(1, NCH // 2 - 1) as pair:
                body(2 * pair, 0)
                body(2 * pair + 1, 1)
            body(NCH - 2, 0)
            body(NCH - 1, 1, last=True)
            sp.wait_ge(added, E * NCH)
            store(NCH - 1, 1)
            for half in stored:
                sp.wait_ge(half, 16 * NCH // 2)

        @block.gpsimd
        def _(pool):
            def split_w2(e):
                pool.wait_ge(w2_loaded[e], 16)
                pool.tensor_copy(w2_h[:, e], w2[:, e]).then_inc(w2_steps, 1)
                pool.wait_ge(w2_steps, 2 * e + 1)
                pool.tensor_tensor(w2_l[:, e], w2[:, e], f32(w2_h[:, e]), ALU.subtract).then_inc(w2_steps, 1)

            pool.iota(rank_i[:, :], [[-1, E]], base=E, channel_multiplier=0).then_inc(rank_made, 1)
            split_w2(0)
            split_w2(1)

            def add(g, e, slot, turn):
                pool.wait_ge(weighed, E * g + e + 1)
                need(pool, added, E * g + e)
                if e == 0:
                    need(pool, stored[slot], 16 * turn)
                before = resid[:, bass.ds(g * CH, CH)] if e == 0 else out_sb[:, slot]
                pool.tensor_tensor(out_sb[:, slot], part[:, e % 2], before, ALU.add).then_inc(added, 1)

            for e in range(E):
                add(0, e, 0, 0)
                if e + 2 < E - E2:
                    split_w2(e + 2)
            for e in range(E):
                add(1, e, 1, 0)
            with pool.Fori(1, NCH // 2) as pair:
                for slot in range(2):
                    for e in range(E):
                        add(2 * pair + slot, e, slot, pair)

        @block.scalar
        def _(act):
            def stage_weights(g):
                need(act, wt_turned, g)
                nc.scalar.activation(weight_chunk[:, :, :], weight[:, bass.ds(g * G, G), :], ACT.Copy
                                     ).then_inc(wt_staged, 1)

            def keep_rows(g):
                act.wait_ge(wt_turned, g + 1)
                need(act, rows_out, 16 * g)
                nc.scalar.activation(weight_t[:, :], ps_t[0:E, :], ACT.Copy).then_inc(wt_ready, 1)

            def silu(g, k):
                act.wait_ge(hidden, NK * g + k + 1)
                need(act, hid_ready, NK * g + k - FB + 1)
                nc.scalar.activation(hid[:, k % FB], ps_h[k % HR][:, :], ACT.Silu
                                     ).then_inc(silu_done, 1)

            def high(g, k):
                act.wait_ge(silu_done, NK * g + k + 1)
                need(act, down_done, NK * g + k - FB + 1)
                nc.scalar.activation(hid_h[:, k % FB], hid[:, k % FB], ACT.Copy).then_inc(hid_high, 1)

            def body(g, start=False, last=False):
                for k in range(NK):
                    silu(g, k)
                    if k % FB:
                        high(g, k - 1)
                    if start and k == 0:
                        act.wait_ge(weights_ready, 1)
                        stage_weights(0)
                    if start and k == 3:
                        keep_rows(0)
                    if k == 8 and not last:
                        stage_weights(g + 1)
                    if k == 20 and not last:
                        keep_rows(g + 1)

            act.wait_ge(choice, 12)
            nc.scalar.activation(share[:, 1, :], gap[:, :], ACT.Exp).then_inc(share_exp, 1)
            body(0, start=True)
            with act.Fori(1, NCH - 1) as g:
                body(g)
            body(NCH - 1, last=True)

        @block.vector
        def _(dve):
            wide = [P, NT, E]

            def step(ins, count):
                ins.then_inc(choice, 1)
                dve.wait_ge(choice, count)

            dve.wait_ge(rank_made, 1)
            step(nc.vector.tensor_copy(rank[:, :], rank_i[:, :]), 1)
            count = 1
            for n, src in ((0, logits), (1, other)):
                top, mark = best[:, n, :], hot[:, n]
                step(nc.vector.tensor_reduce(top, src[:, :, :], AX.X, ALU.max), count + 1)
                step(nc.vector.tensor_tensor(mark, src[:, :, :], top.unsqueeze(2).broadcast_to(wide), ALU.is_equal),
                     count + 2)
                step(nc.vector.tensor_tensor(mark, mark, rank[:, :].unsqueeze(1).broadcast_to(wide), ALU.mult),
                     count + 3)
                step(nc.vector.tensor_reduce(first[:, :], mark, AX.X, ALU.max), count + 4)
                step(nc.vector.tensor_tensor(mark, mark, first[:, :].unsqueeze(2).broadcast_to(wide), ALU.is_equal),
                     count + 5)
                count += 5
                if n == 0:
                    nc.vector.scalar_tensor_tensor(other[:, :, :], mark, NEG, logits[:, :, :], ALU.mult, ALU.add
                                                   ).then_inc(rank_made, 1)
                    dve.wait_ge(rank_made, 2)
            nc.vector.tensor_tensor(gap[:, :], best[:, 1, :], best[:, 0, :], ALU.subtract).then_inc(choice, 1)

            dve.wait_ge(share_exp, 1)
            step(nc.vector.tensor_scalar(first[:, :], share[:, 1, :], 1.0, None, ALU.add), 13)
            step(nc.vector.reciprocal(share[:, 0, :], first[:, :]), 14)
            step(nc.vector.tensor_tensor(share[:, 1, :], share[:, 1, :], share[:, 0, :], ALU.mult), 15)
            for n in range(2):
                step(nc.vector.tensor_tensor(hot[:, n], hot[:, n], share[:, n, :].unsqueeze(2).broadcast_to(wide),
                                             ALU.mult), 16 + n)
            nc.vector.tensor_tensor(weight[:, :, :], hot[:, 0], hot[:, 1], ALU.add).then_inc(weights_ready, 1)

            def low(g, k):
                e, f = k // FB, k % FB
                need(dve, down_done, NK * g + k - FB + 1)
                if f < FB - 1:
                    dve.wait_ge(hid_high, (FB - 1) * (E * g + e) + f + 1)
                else:
                    dve.wait_ge(silu_done, NK * g + k + 1)
                    nc.vector.tensor_copy(hid_h[:, f], hid[:, f]).then_inc(hid_last_high, 1)
                    dve.wait_ge(hid_last_high, E * g + e + 1)
                nc.vector.tensor_tensor(hid_l[:, f], hid[:, f], f32(hid_h[:, f]), ALU.subtract
                                        ).then_inc(hid_ready, 1)

            def weigh(g, e):
                dve.wait_ge(down_done, NK * g + FB * e + FB)
                dve.wait_ge(spread[e % 2], 16 * (E // 2 * g + e // 2 + 1))
                need(dve, added, E * g + e - 1)
                nc.vector.tensor_tensor(part[:, e % 2], ps_y[e % 2][:, :], w_all[:, e % 2], ALU.mult
                                        ).then_inc(weighed, 1)

            def body(g, start=False, last=False):
                for k in range(NK):
                    e, f = k // FB, k % FB
                    low(g, k)
                    if (f == 2 and e and not (last and e == E - 1)) or (last and k == NK - 1):
                        weigh(g, e - 1)
                    elif f == 2 and not e and not start:
                        weigh(g - 1, E - 1)

            body(0, start=True)
            with dve.Fori(1, NCH - 1) as g:
                body(g)
            body(NCH - 1, last=True)
            weigh(NCH - 1, E - 1)

        @block.tensor
        def _(pe):
            def turn_weights(g):
                pe.wait_ge(wt_staged, g + 1)
                need(pe, wt_ready, g)
                for j in range(G):
                    last = pe.transpose(ps_t[0:E, j * P:(j + 1) * P], weight_chunk[:, j, :], ident[:, :])
                last.then_inc(wt_turned, 1)

            def up(g, k):
                e, f = k // FB, k % FB
                need(pe, silu_done, NK * g + k - HR + 1)
                at = (slice(None), bass.ds(g * CH, CH))
                w = slice(f * P, (f + 1) * P)
                split_product(pe, ps_h[k % HR][:, :], ew_h[:, e, w], ew_l[:, e, w], z2_h[at], z2_l[at], True, True
                              ).then_inc(hidden, 1)

            def down(g, k):
                e, f = k // FB, k % FB
                if isinstance(g, int) and g == 0 and f == 0 and e >= E2:
                    pe.wait_ge(w2_steps, 2 * (e - E2) + 2)
                high, low = (ew_h[:, E + e], ew_l[:, E + e]) if e < E2 else (w2_h[:, e - E2], w2_l[:, e - E2])
                w = slice(f * P, (f + 1) * P)
                if f == 0:
                    need(pe, weighed, E * g + e - 1)
                pe.wait_ge(hid_ready, NK * g + k + 1)
                split_product(pe, ps_y[e % 2][:, :], high[:, w], low[:, w], hid_h[:, f], hid_l[:, f],
                              f == 0, f == FB - 1).then_inc(down_done, 1)

            def body(g, last=False):
                for k in range(NK):
                    if k + LEAD < NK:
                        up(g, k + LEAD)
                    elif not last:
                        up(g + 1, k + LEAD - NK)
                    if isinstance(g, int) and g == 0 and k == 0:
                        turn_weights(0)
                    down(g, k)
                    if k == 12 and not last:
                        turn_weights(g + 1)

            for k in range(LEAD):
                up(0, k)
            body(0)
            with pe.Fori(1, NCH - 1) as g:
                body(g)
            body(NCH - 1, last=True)


def mixed_kernel(nc, x_chwn, x_cnhw, w_qkv, w_c, gamma, beta, wqs, wks, wvr_d, wqrT, wkretT, wout_d,
                 wg_d, f_w1, f_w2, out, qk_rows, w_rows):
    with ExitStack() as ctx:
        def sb(name, shape, dt=F32, where=ctx):
            return where.enter_context(nc.sbuf_tensor(name, shape, dt))

        def sem(name):
            return ctx.enter_context(nc.semaphore(name))

        bank = [ctx.enter_context(nc.psum_tensor(f"bank{i}", [P, CH], F32)) for i in range(8)]
        resid = sb("resid", [P, TOK])
        wc_h = sb("wc_h", [P, 9, P], F32R)
        wc_l = sb("wc_l", [P, 9, P], F32R)
        ident = sb("ident", [P, P])
        ones = sb("ones", [P, P])
        norm_a = sb("norm_a", [P, NI])
        norm_b = sb("norm_b", [P, NI])
        pad_h = sb("pad_h", [P, PAD * PAD * NI], F32R)
        pad_l = sb("pad_l", [P, PAD * PAD * NI], F32R)
        virt = sb("virt", [P, NI, HW, HW])

        gb = sb("gb", [P, 2])
        power = sb("power", [P, NI])
        wq = sb("wq", [P, P])
        wk = sb("wk", [P, P])
        wvr = sb("wvr", [P, 32])
        wqr_t = sb("wqr_t", [P, P])
        ret_blocks = sb("ret_blocks", [P, P])
        wout = sb("wout", [P, P])
        wg = sb("wg", [P, 8])
        late_loads = [(gb[:, 0:1], gamma), (gb[:, 1:2], beta), (wq[:, :], wqs), (wk[:, :], wks), (wvr[:, :], wvr_d),
                      (wqr_t[:, :], wqrT), (wout[:, :], wout_d), (wg[:, :], wg_d)]

        with ExitStack() as early:
            stats = sb("stats", [P, NI, NCH, 6], where=early)
            conv_attention(nc, sb, sem, bank, pad_h, pad_l, resid, virt, ident, wc_h, wc_l, x_chwn, x_cnhw,
                           w_qkv, w_c, stats, ones, power, ret_blocks, late_loads, wkretT)
            image_norm(nc, sb, sem, bank, pad_h, pad_l, stats, gb, ones, power, norm_a, norm_b)
        z2_h = sb("z2_h", [P, TOK], F32R)
        z2_l = sb("z2_l", [P, TOK], F32R)
        logits = sb("logits", [P, NCH * G, 8])
        token_attention(nc, sb, sem, bank, pad_h, pad_l, resid, virt, z2_h, z2_l, logits, ident, wc_h, wc_l, norm_a,
                        norm_b, power, wq, wk, wvr, wqr_t, ret_blocks, wout, wg, f_w1, f_w2, qk_rows)
        experts(nc, sb, sem, bank, pad_h, pad_l, resid, virt, z2_h, z2_l, logits, ident, f_w2, out, w_rows)


_INS = ["x_chwn", "x_cnhw", "w_qkv", "w_c", "gamma", "beta", "wqs", "wks", "wvr", "wqrT", "wkretT", "wout", "wg",
        "w1", "w2"]


def kernel(x, L0_conv_Wq, L0_conv_Wk, L0_conv_Wv, L0_conv_Wc, L0_conv_gamma, L0_conv_beta, L1_attn_wq_s,
           L1_attn_wk_s, L1_attn_wv_r, L1_attn_wq_r, L1_attn_wk_ret, L1_attn_w_out, L1_ffn_Wg, L1_ffn_W1, L1_ffn_W2):
    import numpy as np
    import concourse.bacc as bacc
    from concourse.bass_utils import run_bass_kernel_spmd

    def taps(w):
        return np.asarray(w).transpose(1, 2, 3, 0).reshape(P, 9, P)

    x, w1, w2 = np.asarray(x), np.asarray(L1_ffn_W1), np.asarray(L1_ffn_W2)
    laid = [
        x.transpose(1, 2, 3, 0).reshape(P, HW, HW * NI), x.transpose(1, 0, 2, 3).reshape(P, TOK),
        np.stack([taps(w) for w in (L0_conv_Wq, L0_conv_Wk, L0_conv_Wv)], axis=1), taps(L0_conv_Wc),
        np.asarray(L0_conv_gamma).reshape(P, 1), np.asarray(L0_conv_beta).reshape(P, 1),
        np.asarray(L1_attn_wq_s), np.asarray(L1_attn_wk_s), np.asarray(L1_attn_wv_r),
        np.asarray(L1_attn_wq_r).T, np.asarray(L1_attn_wk_ret).T, np.asarray(L1_attn_w_out),
        np.asarray(L1_ffn_Wg), w1.transpose(1, 0, 2), w2.reshape(8, G, P, P).transpose(2, 0, 1, 3),
    ]
    nc = bacc.Bacc("TRN2", target_bir_lowering=False, num_devices=1)
    arrays, args = {}, []
    for name, a in zip(_INS, laid):
        arrays[f"in_{name}"] = np.ascontiguousarray(a)
        args.append(nc.dram_tensor(f"in_{name}", a.shape, mybir.dt.from_np(a.dtype), kind="ExternalInput").ap())
    args.append(nc.dram_tensor("out", (P, TOK), F32, kind="ExternalOutput").ap())
    args.append(nc.dram_tensor("qk_rows", (NCH, 4, P, CH), F32, kind="Internal").ap())
    args.append(nc.dram_tensor("w_rows", (NCH, 8, CH), F32, kind="Internal").ap())
    mixed_kernel(nc, *args)
    r = run_bass_kernel_spmd(nc, [arrays], core_ids=[0])
    return np.ascontiguousarray(r.results[0]["out"].reshape(P, NI, HW, HW).transpose(1, 0, 2, 3))
```
